# Optimizing a Trainium2 kernel written in Bass

```python
import numpy as np
import jax
import jax.numpy as jnp

def _softmax(x, axis=-1):
    return jax.nn.softmax(x, axis=axis)

def _gelu(x):
    return jax.nn.gelu(x, approximate=True)

def _silu(x):
    return jax.nn.silu(x)

def _sigmoid(x):
    return jax.nn.sigmoid(x)

def _layernorm(x, axis=-1, eps=1e-05):
    m = jnp.mean(x, axis=axis, keepdims=True)
    v = jnp.var(x, axis=axis, keepdims=True)
    return (x - m) / jnp.sqrt(v + eps)

def _scatter_add(tgt, idx, src, axis=0):
    return tgt.at[idx].add(src)

def _segment_sum(src, seg, n):
    return jax.ops.segment_sum(src, seg, n)
kernel_name = 'mk_gnn_resnorm_d4_gnn_r8_9f2984'

def setup_inputs(seed: int=0):
    np.random.seed(seed)
    _w = jnp.asarray

    def _rec_inputs():
        import jax
        import jax.numpy as jnp
        _gk = jax.random.key(seed)
        x = -0.0005121 + 1.001 * jax.random.normal(jax.random.fold_in(_gk, 1), (6250, 64), jnp.float32)
        src = jax.random.randint(jax.random.fold_in(_gk, 2), (200000,), 0, 6250, jnp.int32)
        dst = jnp.minimum((6250 * jax.random.uniform(jax.random.fold_in(_gk, 3), (200000,)) ** 2.0).astype(jnp.int32), 49999)
        _o = jnp.argsort(dst, stable=True)
        src = src[_o]
        dst = dst[_o]
        edge_attr_16 = 0.000254156 + 0.999948 * jax.random.normal(jax.random.fold_in(_gk, 12), (200000, 16), jnp.float32)
        edge_attr_64 = 7.68618e-05 + 1.00005 * jax.random.normal(jax.random.fold_in(_gk, 13), (200000, 64), jnp.float32)
        edge_weight1 = jax.random.uniform(jax.random.fold_in(_gk, 15), (200000, 1), jnp.float32, 0.0, 0.999999)
        return (x, src, dst, edge_attr_16, edge_attr_64, edge_weight1)
    x, src, dst, edge_attr_16, edge_attr_64, edge_weight1 = _rec_inputs()

    def _L0_gnn_setup():
        import jax, jax.numpy as jnp
        import numpy as np
        from jax.ops import segment_sum
        N = 6250
        E = 100000
        D_IN = 64
        D_HID = 256
        D_OUT = 64
        key = jax.random.key(seed)
        ks = jax.random.split(key, 8)
        x = jax.random.normal(ks[0], (N, D_IN), dtype=jnp.float32)
        row = jax.random.randint(ks[1], (E,), 0, N, dtype=jnp.int64)
        col_rand = jax.random.randint(ks[2], (E - N,), 0, N, dtype=jnp.int64)
        col = jnp.concatenate([jnp.arange(N, dtype=jnp.int64), col_rand])
        edge_index = jnp.stack([row, col])
        edge_attr = jax.random.uniform(ks[3], (E, 1), dtype=jnp.float32)
        u = jnp.zeros((1, D_IN), dtype=jnp.float32)
        batch = jnp.zeros((N,), dtype=jnp.int64)
        W1 = jax.random.normal(ks[4], (D_IN, D_HID), dtype=jnp.float32) * (1.0 / np.sqrt(D_IN))
        b1 = jnp.zeros((D_HID,), dtype=jnp.float32)
        W2 = jax.random.normal(ks[5], (D_HID, D_OUT), dtype=jnp.float32) * (1.0 / np.sqrt(D_HID))
        b2 = jnp.zeros((D_OUT,), dtype=jnp.float32)
        return {'x': x, 'edge_index': edge_index, 'edge_attr': edge_attr, 'u': u, 'batch': batch, 'W1': W1, 'b1': b1, 'W2': W2, 'b2': b2}
    _L0_gnn_all = _L0_gnn_setup()
    _L0_gnn_in = {k: v for k, v in _L0_gnn_all.items() if k in ('u', 'W1', 'b1', 'W2', 'b2')}
    del _L0_gnn_all

    def _L1_gnn_setup():
        import jax, jax.numpy as jnp
        import numpy as np
        N_NODES = 6250
        N_EDGES = 125000
        D = 64
        HID = 128
        N_GRAPHS = 16
        LN_EPS = 1e-05
        key = jax.random.key(seed)
        ks = jax.random.split(key, 10)
        x = jax.random.normal(ks[0], (N_NODES, D), dtype=jnp.float32)
        edge_index = jax.random.randint(ks[1], (2, N_EDGES), 0, N_NODES, dtype=jnp.int64)
        edge_attr = jax.random.normal(ks[2], (N_EDGES, D), dtype=jnp.float32)
        u = jax.random.normal(ks[3], (N_GRAPHS, 1), dtype=jnp.float32)
        batch = jnp.sort(jax.random.randint(ks[4], (N_NODES,), 0, N_GRAPHS, dtype=jnp.int64))
        in_dim = D + 3 * D + 1
        lim1 = 1.0 / np.sqrt(in_dim)
        lim2 = 1.0 / np.sqrt(HID)
        W1 = jax.random.uniform(ks[5], (in_dim, HID), dtype=jnp.float32, minval=-lim1, maxval=lim1)
        b1 = jax.random.uniform(ks[6], (HID,), dtype=jnp.float32, minval=-lim1, maxval=lim1)
        W2 = jax.random.uniform(ks[7], (HID, D), dtype=jnp.float32, minval=-lim2, maxval=lim2)
        b2 = jax.random.uniform(ks[8], (D,), dtype=jnp.float32, minval=-lim2, maxval=lim2)
        gamma = jnp.ones((D,), dtype=jnp.float32)
        beta = jnp.zeros((D,), dtype=jnp.float32)
        return {'x': x, 'edge_index': edge_index, 'edge_attr': edge_attr, 'u': u, 'batch': batch, 'W1': W1, 'b1': b1, 'W2': W2, 'b2': b2, 'gamma': gamma, 'beta': beta}
    _L1_gnn_all = _L1_gnn_setup()
    _L1_gnn_in = {k: v for k, v in _L1_gnn_all.items() if k in ('u', 'W1', 'b1', 'W2', 'b2', 'gamma', 'beta')}
    del _L1_gnn_all

    def _L2_gnn_setup():
        import jax, jax.numpy as jnp
        import numpy as np
        N, E, D = (6250, 100000, 64)
        key = jax.random.key(seed)
        ks = jax.random.split(key, 8)
        s = 1.0 / np.sqrt(2 * D)
        inp = {'node_emb': jax.random.normal(ks[0], (N, D), dtype=jnp.float32), 'edge_index': jax.random.randint(ks[1], (2, E), 0, N, dtype=jnp.int64), 'W1': jax.random.normal(ks[2], (2 * D, D), dtype=jnp.float32) * s, 'b1': jnp.zeros((D,), dtype=jnp.float32), 'W2': jax.random.normal(ks[3], (D, D), dtype=jnp.float32) * (1.0 / np.sqrt(D)), 'b2': jnp.zeros((D,), dtype=jnp.float32), 'Wg': jax.random.normal(ks[4], (D, D), dtype=jnp.float32) * (1.0 / np.sqrt(D)), 'bg': jnp.zeros((D,), dtype=jnp.float32)}
        return inp
    _L2_gnn_all = _L2_gnn_setup()
    _L2_gnn_in = {k: v for k, v in _L2_gnn_all.items() if k in ('W1', 'b1', 'W2', 'b2', 'Wg', 'bg')}
    del _L2_gnn_all

    def _L3_gnn_setup():
        import jax, jax.numpy as jnp
        import numpy as np
        N, E = (6250, 100000)
        NODE_DIM, EDGE_DIM, HEADS = (64, 16, 4)
        C = NODE_DIM // HEADS
        NEG_SLOPE = 0.2
        BN_EPS = 1e-05
        key = jax.random.key(seed)
        ks = jax.random.split(key, 12)
        glorot = lambda k, shape: jax.random.normal(k, shape, jnp.float32) * np.sqrt(2.0 / (shape[0] + shape[-1]))
        return {'x': jax.random.normal(ks[0], (N, NODE_DIM), jnp.float32), 'edge_index': jax.random.randint(ks[1], (2, E), 0, N, jnp.int32), 'edge_attr': jax.random.normal(ks[2], (E, EDGE_DIM), jnp.float32), 'W_l': glorot(ks[3], (NODE_DIM, HEADS * C)), 'b_l': jnp.zeros((HEADS * C,), jnp.float32), 'W_r': glorot(ks[4], (NODE_DIM, HEADS * C)), 'b_r': jnp.zeros((HEADS * C,), jnp.float32), 'W_e': glorot(ks[5], (EDGE_DIM, HEADS * C)), 'att': glorot(ks[6], (HEADS, C)), 'bias': jnp.zeros((HEADS * C,), jnp.float32), 'gamma': jnp.ones((NODE_DIM,), jnp.float32), 'beta': jnp.zeros((NODE_DIM,), jnp.float32)}
    _L3_gnn_all = _L3_gnn_setup()
    _L3_gnn_in = {k: v for k, v in _L3_gnn_all.items() if k in ('W_l', 'b_l', 'W_r', 'b_r', 'W_e', 'att', 'bias', 'gamma', 'beta')}
    del _L3_gnn_all
    return {'x': x, 'src': src, 'dst': dst, 'edge_attr_16': edge_attr_16, 'edge_attr_64': edge_attr_64, 'edge_weight1': edge_weight1, 'L0_gnn_u': _L0_gnn_in['u'], 'L0_gnn_W1': _L0_gnn_in['W1'], 'L0_gnn_b1': _L0_gnn_in['b1'], 'L0_gnn_W2': _L0_gnn_in['W2'], 'L0_gnn_b2': _L0_gnn_in['b2'], 'L1_gnn_u': _L1_gnn_in['u'], 'L1_gnn_W1': _L1_gnn_in['W1'], 'L1_gnn_b1': _L1_gnn_in['b1'], 'L1_gnn_W2': _L1_gnn_in['W2'], 'L1_gnn_b2': _L1_gnn_in['b2'], 'L1_gnn_gamma': _L1_gnn_in['gamma'], 'L1_gnn_beta': _L1_gnn_in['beta'], 'L2_gnn_W1': _L2_gnn_in['W1'], 'L2_gnn_b1': _L2_gnn_in['b1'], 'L2_gnn_W2': _L2_gnn_in['W2'], 'L2_gnn_b2': _L2_gnn_in['b2'], 'L2_gnn_Wg': _L2_gnn_in['Wg'], 'L2_gnn_bg': _L2_gnn_in['bg'], 'L3_gnn_W_l': _L3_gnn_in['W_l'], 'L3_gnn_b_l': _L3_gnn_in['b_l'], 'L3_gnn_W_r': _L3_gnn_in['W_r'], 'L3_gnn_b_r': _L3_gnn_in['b_r'], 'L3_gnn_W_e': _L3_gnn_in['W_e'], 'L3_gnn_att': _L3_gnn_in['att'], 'L3_gnn_bias': _L3_gnn_in['bias'], 'L3_gnn_gamma': _L3_gnn_in['gamma'], 'L3_gnn_beta': _L3_gnn_in['beta']}

def reference(x, src, dst, edge_attr_16, edge_attr_64, edge_weight1, L0_gnn_u, L0_gnn_W1, L0_gnn_b1, L0_gnn_W2, L0_gnn_b2, L1_gnn_u, L1_gnn_W1, L1_gnn_b1, L1_gnn_W2, L1_gnn_b2, L1_gnn_gamma, L1_gnn_beta, L2_gnn_W1, L2_gnn_b1, L2_gnn_W2, L2_gnn_b2, L2_gnn_Wg, L2_gnn_bg, L3_gnn_W_l, L3_gnn_b_l, L3_gnn_W_r, L3_gnn_b_r, L3_gnn_W_e, L3_gnn_att, L3_gnn_bias, L3_gnn_gamma, L3_gnn_beta):
    import jax
    import jax.numpy as jnp

    def _L0_gnn_ref(x, edge_index, edge_attr, u, batch, W1, b1, W2, b2):
        import jax, jax.numpy as jnp
        import numpy as np
        from jax.ops import segment_sum
        N = 6250
        E = 100000
        D_IN = 64
        D_HID = 256
        D_OUT = 64
        col = edge_index[1]
        geo_sum = segment_sum(edge_attr * x[col], col, num_segments=x.shape[0])
        geo_denom = segment_sum(edge_attr, col, num_segments=x.shape[0])
        geo_agg = x + geo_sum / geo_denom
        geo_agg = jnp.where(jnp.isnan(geo_agg), jnp.float32(0.0), geo_agg)
        h = jax.nn.relu(geo_agg @ W1 + b1)
        return jax.nn.relu(h @ W2 + b2)

    def _L1_gnn_ref(x, edge_index, edge_attr, u, batch, W1, b1, W2, b2, gamma, beta):
        import jax, jax.numpy as jnp
        import numpy as np
        N_NODES = 6250
        N_EDGES = 125000
        D = 64
        HID = 128
        N_GRAPHS = 16
        LN_EPS = 1e-05
        n = x.shape[0]
        col = edge_index[1]
        agg_sum = jax.ops.segment_sum(edge_attr, col, num_segments=n)
        agg_max = jax.ops.segment_max(edge_attr, col, num_segments=n)
        cnt = jax.ops.segment_sum(jnp.ones((edge_attr.shape[0], 1), edge_attr.dtype), col, num_segments=n)
        agg_max = jnp.where(cnt > 0, agg_max, 0.0)
        agg_mean = agg_sum / jnp.maximum(cnt, 1.0)
        h = jnp.concatenate([x, agg_sum, agg_max, agg_mean, u[batch]], axis=1)
        h = jax.nn.gelu(h @ W1 + b1, approximate=False)
        h = h @ W2 + b2
        mu = jnp.mean(h, axis=-1, keepdims=True)
        var = jnp.mean((h - mu) ** 2, axis=-1, keepdims=True)
        h = (h - mu) * jax.lax.rsqrt(var + LN_EPS) * gamma + beta
        return h + x

    def _L2_gnn_ref(node_emb, edge_index, W1, b1, W2, b2, Wg, bg):
        import jax, jax.numpy as jnp
        import numpy as np
        src, dst = (edge_index[0], edge_index[1])
        pair_emb = jnp.concatenate([node_emb[src], node_emb[dst]], axis=-1)
        h = jax.nn.relu(pair_emb @ W1 + b1)
        interaction = h @ W2 + b2
        gate = jax.nn.sigmoid(interaction @ Wg + bg)
        gated = interaction * gate
        N = node_emb.shape[0]
        summed = jax.ops.segment_sum(gated, src, num_segments=N)
        counts = jax.ops.segment_sum(jnp.ones((src.shape[0],), dtype=gated.dtype), src, num_segments=N)
        pooled = summed / jnp.maximum(counts, 1.0)[:, None]
        return pooled

    def _L3_gnn_ref(x, edge_index, edge_attr, W_l, b_l, W_r, b_r, W_e, att, bias, gamma, beta):
        import jax, jax.numpy as jnp
        import numpy as np
        N, E = (6250, 100000)
        NODE_DIM, EDGE_DIM, HEADS = (64, 16, 4)
        C = NODE_DIM // HEADS
        NEG_SLOPE = 0.2
        BN_EPS = 1e-05
        src, dst = (edge_index[0], edge_index[1])
        n = x.shape[0]
        xl = (x @ W_l + b_l).reshape(n, HEADS, C)
        xr = (x @ W_r + b_r).reshape(n, HEADS, C)
        e = (edge_attr @ W_e).reshape(-1, HEADS, C)
        g = jax.nn.leaky_relu(xl[src] + xr[dst] + e, NEG_SLOPE)
        logits = jnp.einsum('ehc,hc->eh', g, att)
        amax = jax.ops.segment_max(logits, dst, num_segments=n)
        ex = jnp.exp(logits - amax[dst])
        denom = jax.ops.segment_sum(ex, dst, num_segments=n)
        alpha = ex / (denom[dst] + 1e-16)
        msg = xl[src] * alpha[..., None]
        out = jax.ops.segment_sum(msg, dst, num_segments=n).reshape(n, HEADS * C) + bias
        mean = out.mean(axis=0)
        var = out.var(axis=0)
        out = (out - mean) * jax.lax.rsqrt(var + BN_EPS) * gamma + beta
        return jax.nn.gelu(out + x, approximate=False)
    edge_index = jnp.stack([src, dst])
    batch0 = jnp.zeros((6250,), jnp.int32)
    x = _layernorm(x + _L0_gnn_ref(x, edge_index, edge_weight1, L0_gnn_u, batch0, L0_gnn_W1, L0_gnn_b1, L0_gnn_W2, L0_gnn_b2), axis=-1)
    x = _layernorm(x + _L1_gnn_ref(x, edge_index, edge_attr_64, L1_gnn_u, batch0, L1_gnn_W1, L1_gnn_b1, L1_gnn_W2, L1_gnn_b2, L1_gnn_gamma, L1_gnn_beta), axis=-1)
    x = _layernorm(x + _L2_gnn_ref(x, edge_index, L2_gnn_W1, L2_gnn_b1, L2_gnn_W2, L2_gnn_b2, L2_gnn_Wg, L2_gnn_bg), axis=-1)
    x = _layernorm(x + _L3_gnn_ref(x, edge_index, edge_attr_16, L3_gnn_W_l, L3_gnn_b_l, L3_gnn_W_r, L3_gnn_b_r, L3_gnn_W_e, L3_gnn_att, L3_gnn_bias, L3_gnn_gamma, L3_gnn_beta), axis=-1)
    return x

_drawn_inputs = setup_inputs


def setup_inputs(seed=0):
    import zlib

    import numpy as np

    out = dict(_drawn_inputs(seed))
    spreads = {'L0_gnn_u': (0.0, 0.1),
     'L0_gnn_b1': (0.0, 0.1),
     'L0_gnn_b2': (0.0, 0.1),
     'L1_gnn_gamma': (1.0, 0.2),
     'L1_gnn_beta': (0.0, 0.1),
     'L2_gnn_b1': (0.0, 0.299),
     'L2_gnn_b2': (0.0, 0.1),
     'L2_gnn_bg': (0.0, 0.605),
     'L3_gnn_b_l': (0.0, 0.662),
     'L3_gnn_b_r': (0.0, 0.572),
     'L3_gnn_bias': (0.0, 0.8),
     'L3_gnn_gamma': (1.0, 0.2),
     'L3_gnn_beta': (0.0, 0.1)}
    factors = {'edge_weight1': 8.0, 'L1_gnn_u': 5.889, 'L1_gnn_b1': 4.847}
    for name, (base, spread) in spreads.items():
        noise = np.random.default_rng([zlib.crc32(name.encode()), seed]).standard_normal(out[name].shape)
        drawn = base * np.exp(spread * noise) if base else spread * noise
        out[name] = jnp.asarray(drawn.astype(out[name].dtype))
    for name, factor in factors.items():
        out[name] = (out[name] * factor).astype(out[name].dtype)
    return out
```

```python
import itertools
import numpy as np
import concourse.bass as bass
from concourse import mybir
from contextlib import ExitStack

F32 = mybir.dt.float32
I32 = mybir.dt.int32
BF16 = mybir.dt.bfloat16
ALU = mybir.AluOpType
ACT = mybir.ActivationFunctionType
AX = mybir.AxisListType
ds = bass.ds

P = 128
N = 6250
E = 200000
D = 64
H = E // 2
NJ = -(-N // P)
NP = P * NJ
FULLP, LASTJ = N // NJ, N % NJ
W = 512
C = 4
NG = H // W
TAIL = H - NG * W
FIRST = NG - 2 * ((NG - 3) // 2)
NPAIR = (NG - FIRST) // 2
SR, SC = 64, E // 64
KR, KC, KT = 1600, 125, 40
NONE = 1 << 20
NEG = -2.0 ** 126
EPS = 1e-5
HEADS, HC, ED = 4, 16, 16
LOGN = 18
SF = (1 << LOGN) // P
SB = 13
KEYBASE = 1 << 29
T3 = 72


class Stage(ExitStack):

    def __init__(self, nc):
        super().__init__()
        self.nc, self.sems = nc, []

    def __exit__(self, *what):
        if self.sems and what[0] is None:
            self.nc.clear_and_free_semaphores(self.sems)
            self.nc.all_engine_barrier()
        return super().__exit__(*what)


def each_group(eng, front, back=None):
    def group(g, pair):
        return g % 2, pair * 2 + g, pair + g // 2, (pair * 2 + g) * W, W

    for g in range(FIRST):
        front(*group(g, 0))
        if back and g:
            back(*group(g - 1, 0))
    with eng.Fori(0, NPAIR) as it:
        pair = eng.snap(it)
        for g in (FIRST, FIRST + 1):
            front(*group(g, pair))
            if back:
                back(*group(g - 1, pair))
    tail = (NG % 2, NG, NG // 2, NG * W, TAIL)
    front(*tail)
    if back:
        back(*group(NG - 1, 0))
        back(*tail)


def wait_from(eng, sem, value):
    if not isinstance(value, int) or value > 0:
        eng.wait_ge(sem, value)


def last(n):
    return isinstance(n, int) and n == NG


def next_width(n):
    return TAIL if isinstance(n, int) and n == NG - 1 else W


def by_edge(table, h, row, width):
    half = table[h * H:(h + 1) * H, :][ds(row, width), :]
    return half.rearrange("(p c) f -> p c f", c=C)


def build(nc, x, src, dst, ea16, ea64, ew, w0a, b0a, w0b, b0b, u1, w1a, b1a, w1b, b1b, g1, be1,
          w2a, b2a, w2b, b2b, w2g, b2g, wl, bl, wr, br, we, att, bias3, g3, be3, out):
    ctx = ExitStack()
    with ctx:
        def dram(name, shape, dt):
            return nc.dram_tensor(name, shape, dt, kind="Internal").ap()

        t1 = dram("t1", [E, 2 * D], F32)
        t2 = dram("t2", [E, D], F32)
        t3 = dram("t3", [E, T3], F32)
        start2 = dram("start2", [E, D], F32)
        start3 = dram("start3", [E, D], F32)
        wsum = dram("wsum", [E, 1], F32)
        srcs = dram("srcs", [E, 1], I32)
        dsts = dram("dsts", [E, 1], I32)
        rowlast = [dram(f"rowlast{o}", [KT, KT], I32) for o in range(2)]
        marks = dram("marks", [2, 2, 2, H], BF16)
        tabg = [dram(f"tabg{i}", [NP, D], F32) for i in range(2)]
        tabs = [dram(f"tabs{i}", [NP, D], F32) for i in range(2)]

        serial = itertools.count()

        def sb(c, name, shape, dt=F32):
            return c.enter_context(nc.sbuf_tensor(f"{name}_{next(serial)}", shape, dt))

        def ps(c, name, shape, dt=F32):
            return c.enter_context(nc.psum_tensor(f"{name}_{next(serial)}", shape, dt))

        def sem(c, name):
            c.sems.append(nc.alloc_semaphore(f"{name}_{next(serial)}"))
            return c.sems[-1]

        X = sb(ctx, "X", [P, NJ, D])
        ident = sb(ctx, "ident", [P, P])
        nid = sb(ctx, "nid", [P, NJ])
        valid = sb(ctx, "valid", [P, NJ])
        sel2 = sb(ctx, "sel2", [2, P], BF16)
        order = [{k: sb(ctx, f"{k}{o}", [P, NJ], dt) for k, dt in
                  (("first", I32), ("last", I32), ("span", F32), ("cnt", F32))} for o in range(2)]

        ident_of[0] = ident
        keys = [dst, srcs]
        setup_and_sort(nc, sb, ps, sem, x, src, dst, X, ident, nid, valid, sel2, start2, start3, srcs, dsts)
        for o in range(2):
            runs_of(nc, sb, ps, sem, o, keys[o], order[o], nid, rowlast, marks, ident, ew, wsum)
        edge_sums(nc, sb, ps, sem, ea64, marks, t1, ident, sel2)
        node_layers_1_2(nc, sb, ps, sem, X, order[0], t1, wsum, ident, w0a, b0a, w0b, b0b, u1, w1a, b1a,
                        w1b, b1b, g1, be1)
        node_tables(nc, sb, ps, sem, 0, X, order[1], srcs, (w2a[D:2 * D, :], b2a), (w2a[0:D, :], None),
                    tabg[0], tabs[0], start2, ident)
        edges_3(nc, sb, ps, sem, dsts, marks, tabg[0], start2, t2, ident, sel2, w2b, b2b, w2g, b2g)
        pool_3(nc, sb, ps, sem, X, order[1], t2)
        node_tables(nc, sb, ps, sem, 1, X, order[0], dst, (wl, bl), (wr, br), tabg[1], tabs[1], start3, ident)
        edges_4(nc, sb, ps, sem, src, ea16, marks, tabg[1], start3, t3, ident, sel2, we, att)
        finish_4(nc, sb, ps, sem, X, order[0], t3, valid, bias3, g3, be3, out)


def node_rows(flat):
    cut = FULLP // 16 * 16
    for a, b in ((0, cut), (cut, FULLP)):
        yield slice(a, b), NJ, flat[a * NJ:b * NJ, :].rearrange("(p j) f -> p j f", j=NJ)
    yield slice(FULLP, FULLP + 1), LASTJ, flat[FULLP * NJ:N, :].rearrange("(p j) f -> p j f", j=LASTJ)



ROW = LOGN - 7


def network():
    for k in range(1, LOGN + 1):
        if k >= ROW:
            yield "sign", k
        if k > ROW:
            yield "turn", k
            for j in range(k - 1, ROW - 1, -1):
                yield "step", k, j - ROW
            yield "turn", k
        for j in range(min(k, ROW) - 1, -1, -1):
            yield "step", k, j


def ops_before_turns():
    n, out = 2, []
    for what in network():
        if what[0] == "turn":
            out.append(n)
        else:
            n += 1 if what[0] == "sign" else (4 if what[1] < ROW else 2)
    return out


def setup_and_sort(nc, sb, ps, sem, x, src, dst, X, ident, nid, valid, sel2, start2, start3, srcs, dsts):
    FULL, REST = E // SF, E % SF
    CUT = FULL // 16 * 16
    ZC = 4000
    TURNS = ops_before_turns()
    with Stage(nc) as c:
        zeros = sb(c, "zeros", [P, ZC])
        nodei = sb(c, "nodei", [P, NJ], I32)
        parti = sb(c, "parti", [P, 1], I32)
        bits = sb(c, "bits", [P, LOGN - ROW + 2], I32)
        sign = sb(c, "sign", [P, LOGN - ROW + 2])
        flip = sb(c, "flip", [P, LOGN - ROW + 1])
        ones2, sel2f, sel2g = (sb(c, n, [2, P]) for n in ("ones2", "sel2f", "sel2g"))
        zerop = sb(c, "zerop", [P, P])
        si, di = (sb(c, n, [P, SF], I32) for n in ("si", "di"))
        ka, kb = (sb(c, n, [P, SF]) for n in ("ka", "kb"))
        pt = ps(c, "pt", [P, SF])

        made, consts = sem(c, "made"), sem(c, "consts")
        cleared, nodes_in, zeroed, pairs_in = (sem(c, n) for n in ("cleared", "nodes_in", "zeroed", "pairs_in"))
        step, turned, back, split, sorted_out = (sem(c, n) for n in ("step", "turned", "back", "split", "sorted_out"))
        with nc.Block() as block:
            @block.sync
            def _(sp):
                sp.wait_ge(cleared, 2)
                for t, k in ((si, src), (di, dst)):
                    for a, b in ((0, CUT), (CUT, FULL)):
                        sp.dma_start(t[a:b, :], k[a * SF:b * SF, :].rearrange("(p f) o -> p (f o)", f=SF)).then_inc(pairs_in, 16)
                    sp.dma_start(t[FULL:FULL + 1, 0:REST], k[FULL * SF:E, :].rearrange("(p f) o -> p (f o)", p=1)).then_inc(pairs_in, 16)
                sp.wait_ge(cleared, 4)
                for s, j, rows in node_rows(x):
                    sp.dma_start(X[s, 0:j, :], rows).then_inc(nodes_in, 16)
                for t in (start2, start3):
                    flat = t.rearrange("r f -> (r f)").rearrange("(p n) -> p n", p=P)
                    for k in range(E * D // P // ZC):
                        sp.dma_start(flat[:, k * ZC:(k + 1) * ZC], zeros[:, :]).then_inc(zeroed, 16)
                sp.wait_ge(split, 2)
                for t, k in ((si, srcs), (di, dsts)):
                    for a, b in ((0, CUT), (CUT, FULL)):
                        sp.dma_start(k[a * SF:b * SF, :].rearrange("(p f) o -> p (f o)", f=SF), t[a:b, :]).then_inc(sorted_out, 16)
                    sp.dma_start(k[FULL * SF:E, :].rearrange("(p f) o -> p (f o)", p=1), t[FULL:FULL + 1, 0:REST]).then_inc(sorted_out, 16)
                sp.wait_ge(sorted_out, 96)
                sp.wait_ge(nodes_in, 48)
                sp.wait_ge(zeroed, 16 * 2 * (E * D // P // ZC))

            @block.gpsimd
            def _(pool):
                nc.gpsimd.memset(zerop[:, :], 0.0).then_inc(made, 1)
                nc.gpsimd.memset(ones2[:, :], 1.0).then_inc(made, 1)
                nc.gpsimd.iota(nodei[:, :], pattern=[[1, NJ]], base=0, channel_multiplier=NJ).then_inc(made, 1)
                nc.gpsimd.iota(parti[:, :], pattern=[[0, 1]], base=0, channel_multiplier=1).then_inc(made, 1)
                pool.wait_ge(made, 4)
                nc.gpsimd.affine_select(out=ident[:, :], in_=zerop[:, :], compare_op=ALU.not_equal, fill=1.0, base=0,
                                        pattern=[[-1, P]], channel_multiplier=1).then_inc(made, 1)
                nc.gpsimd.affine_select(out=sel2g[:, :], in_=ones2[:, :], compare_op=ALU.is_ge, fill=0.0, base=0,
                                        pattern=[[1, P]], channel_multiplier=-D).then_inc(made, 1)
                pool.wait_ge(made, 6)
                nc.gpsimd.affine_select(out=sel2f[:, :], in_=sel2g[:, :], compare_op=ALU.is_ge, fill=0.0, base=D - 1,
                                        pattern=[[-1, P]], channel_multiplier=D).then_inc(made, 1)

            @block.vector
            def _(dve):
                nc.vector.memset(si[:, :], (1 << SB) - 1).then_inc(cleared, 1)
                nc.vector.memset(di[:, :], (1 << SB) - 1).then_inc(cleared, 1)
                nc.vector.memset(zeros[:, :], 0.0).then_inc(cleared, 1)
                nc.vector.memset(X[:, :, :], 0.0).then_inc(cleared, 1)
                nc.vector.memset(bits[:, :], 0).then_inc(consts, 1)
                dve.wait_ge(made, 7)
                nc.vector.tensor_copy(sel2[:, :], sel2f[:, :]).then_inc(consts, 1)
                nc.vector.tensor_copy(nid[:, :], nodei[:, :]).then_inc(consts, 1)
                dve.wait_ge(consts, 3)
                nc.vector.tensor_scalar(valid[:, :], nid[:, :], float(N), None, ALU.is_lt).then_inc(consts, 1)
                for k in range(ROW, LOGN):
                    at = k - ROW + 1
                    nc.vector.tensor_scalar(bits[:, at:at + 1], parti[:, :], k - ROW, 1, ALU.logical_shift_right,
                                            ALU.bitwise_and).then_inc(consts, 1)
                dve.wait_ge(consts, 4 + LOGN - ROW)
                nc.vector.tensor_scalar(sign[:, :], bits[:, :], -2.0, 1.0, ALU.mult, ALU.add).then_inc(consts, 1)
                dve.wait_ge(consts, 5 + LOGN - ROW)
                nc.vector.tensor_tensor(flip[:, :], sign[:, 0:LOGN - ROW + 1], sign[:, 1:LOGN - ROW + 2], ALU.mult).then_inc(consts, 1)
                dve.wait_ge(consts, 6 + LOGN - ROW)
                dve.wait_ge(pairs_in, 96)
                done = 0
                nc.vector.tensor_scalar(ka[:, :].bitcast(I32), si[:, :], SB, KEYBASE, ALU.logical_shift_left,
                                        ALU.bitwise_or).then_inc(step, 1)
                dve.wait_ge(step, 1)
                nc.vector.tensor_tensor(kb[:, :].bitcast(I32), ka[:, :].bitcast(I32), di[:, :], ALU.bitwise_or).then_inc(step, 1)
                done = 2
                now, then, turns = kb, ka, 0
                for what in network():
                    if what[0] == "turn":
                        turns += 1
                        now, then = then, now
                        dve.wait_ge(back, 4 * turns)
                        continue
                    dve.wait_ge(step, done)
                    if what[0] == "sign":
                        at = what[1] - ROW
                        nc.vector.tensor_scalar(then[:, :], now[:, :], flip[:, at:at + 1], None, ALU.mult).then_inc(step, 1)
                        done += 1
                    elif what[1] < ROW:
                        k, i = what[1:]
                        a, b = (z[:, :].rearrange("p (n d s l i) -> p n d s l i", d=2, s=1 << (k - i - 1), l=2, i=1 << i) for z in (now, then))
                        for d, (low, high) in enumerate(((ALU.min, ALU.max), (ALU.max, ALU.min))):
                            for side, op in ((0, low), (1, high)):
                                nc.vector.tensor_tensor(b[:, :, d, :, side, :], a[:, :, d, :, 0, :], a[:, :, d, :, 1, :], op).then_inc(step, 1)
                        done += 4
                    else:
                        a, b = (z[:, :].rearrange("p (n l i) -> p n l i", l=2, i=1 << what[2]) for z in (now, then))
                        for side, op in ((0, ALU.min), (1, ALU.max)):
                            nc.vector.tensor_tensor(b[:, :, side, :], a[:, :, 0, :], a[:, :, 1, :], op).then_inc(step, 1)
                        done += 2
                    now, then = then, now
                dve.wait_ge(step, done)
                ki = now[:, :].bitcast(I32)
                nc.vector.tensor_scalar(si[:, :], ki, SB, (1 << SB) - 1, ALU.logical_shift_right, ALU.bitwise_and).then_inc(split, 1)
                nc.vector.tensor_scalar(di[:, :], ki, (1 << SB) - 1, None, ALU.bitwise_and).then_inc(split, 1)

            def keys_at(turn):
                ops = 0
                for what in network():
                    if what[0] == "turn":
                        if turn == 0:
                            break
                        turn -= 1
                    ops += 1
                return (kb, ka) if ops % 2 == 0 else (ka, kb)

            @block.tensor
            def _(pe):
                pe.wait_ge(made, 7)
                for t, ops in enumerate(TURNS):
                    pe.wait_ge(step, ops)
                    if t:
                        pe.wait_ge(back, 4 * t)
                    now, _ = keys_at(t)
                    for q in range(SF // P):
                        last = nc.tensor.transpose(pt[:, q * P:(q + 1) * P], now[:, q * P:(q + 1) * P], ident[:, :])
                        if q % 4 == 3:
                            last.then_inc(turned, 1)

            @block.scalar
            def _(act):
                for t in range(len(TURNS)):
                    _, then = keys_at(t)
                    for q in range(4):
                        act.wait_ge(turned, 4 * t + q + 1)
                        nc.scalar.activation(then[:, q * 512:(q + 1) * 512], pt[:, q * 512:(q + 1) * 512], ACT.Copy).then_inc(back, 1)


def runs_of(nc, sb, ps, sem, o, key, info, nid, rowlast, marks, ident, ew, wsum):
    with Stage(nc) as c:
        top = sb(c, "top", [P, KT], I32)
        low = sb(c, "low", [KT, KT], I32)
        rows1 = sb(c, "rows1", [P, NJ, KT], I32)
        rows2 = sb(c, "rows2", [P, NJ, KC], I32)
        hits = sb(c, "hits", [P, NJ, KC])
        below1, below2, below3, row, upto, before = (sb(c, n, [P, NJ]) for n in ("below1", "below2", "below3", "row", "upto", "before"))
        index1, index2 = (sb(c, n, [P, NJ], I32) for n in ("index1", "index2"))
        has, f1, f2, f3, l1, l2, l3, s1, s2 = (sb(c, n, [P, NJ]) for n in ("has", "f1", "f2", "f3", "l1", "l2", "l3", "s1", "s2"))
        edge = sb(c, "edge", [SR, SC + 1], I32)
        mark = sb(c, "mark", [SR, SC])
        mark16 = sb(c, "mark16", [SR, SC], BF16)
        reset16 = sb(c, "reset16", [SR, SC], BF16)
        wt, wrun, wprod, wall = (sb(c, n, [SR, SC]) for n in ("wt", "wrun", "wprod", "wall"))
        crow = sb(c, "crow", [1, 2 * SR])
        cscan = sb(c, "cscan", [1, SR + 1])
        ccol = sb(c, "ccol", [SR, 1])
        pe1 = ps(c, "pe1", [1, 2 * SR])
        pe2 = ps(c, "pe2", [SR, 1])
        got, lows, prefill, gat1, gat2, chain, v = (sem(c, n) for n in ("got", "lows", "prefill", "gat1", "gat2", "chain", "v"))
        edges_in, marked, marks_out, shifted, w_in, carries, cback, cturn, w_out = (
            sem(c, n) for n in ("edges_in", "marked", "marks_out", "shifted", "w_in", "carries", "cback", "cturn", "w_out"))
        flat = key.rearrange("e o -> (e o)")
        with nc.Block() as block:
            @block.sync
            def _(sp):
                block_last = flat.rearrange("(q s) -> q s", s=KT * KC)[:, KT * KC - 1:KT * KC].rearrange("q o -> o q")
                with nc.allow_non_contiguous_dma(reason="the last key of each block"):
                    sp.dma_start(top[:, :], block_last.to_broadcast((P, KT))).then_inc(got, 16)
                    sp.dma_start(low[:, :], flat.rearrange("(q r s) -> q r s", r=KT, s=KC)[:, :, KC - 1]).then_inc(lows, 16)
                sp.dma_start(edge[:, 1:SC + 1], flat.rearrange("(p f) -> p f", f=SC)).then_inc(edges_in, 16)
                with nc.allow_non_contiguous_dma(reason="one key of each row"):
                    sp.dma_start(edge[1:SR, 0:1], flat.rearrange("(p f) -> p f", f=SC)[0:SR - 1, SC - 1:SC]).then_inc(edges_in, 16)
                if not o:
                    sp.dma_start(wt[:, :], ew.rearrange("(p f) o -> p (f o)", f=SC)).then_inc(w_in, 16)
                sp.wait_ge(lows, 16)
                sp.dma_start(rowlast[o], low[:, :]).then_inc(lows, 16)
                sp.wait_ge(marked, 2)
                for h in range(2):
                    for kind, t in enumerate((mark16, reset16)):
                        sp.dma_start(marks[o, h, kind].rearrange("(p f) -> p f", f=SC), t[h * SR // 2:(h + 1) * SR // 2, :]).then_inc(marks_out, 16)
                if not o:
                    sp.wait_ge(chain, 5)
                    sp.dma_start(wsum.rearrange("(p f) o -> p (f o)", f=SC), wall[:, :]).then_inc(w_out, 16)
                    sp.wait_ge(w_out, 16)
                sp.wait_ge(v, 8)
                with nc.allow_non_contiguous_dma(reason="one count of each partition"):
                    sp.dma_start(before[1:P, 0:1], upto[0:P - 1, NJ - 1:NJ]).then_inc(shifted, 16)
                sp.wait_ge(shifted, 16)
                sp.wait_ge(marks_out, 64)

            @block.gpsimd
            def _(pool):
                nc.gpsimd.memset(rows1[:, :, :], NONE).then_inc(prefill, 1)
                nc.gpsimd.memset(rows2[:, :, :], NONE).then_inc(prefill, 1)
                pool.wait_ge(prefill, 2)
                pool.wait_ge(lows, 32)
                pool.wait_ge(v, 3)
                for j in range(NJ):
                    nc.gpsimd.indirect_dma_start(rows1[:, j, :], None, rowlast[o], bass.IndirectOffsetOnAxis(ap=index1[:, j:j + 1], axis=0),
                                                 bounds_check=KT - 1, oob_is_err=False).then_inc(gat1, 16)
                pool.wait_ge(v, 6)
                for j in range(NJ):
                    nc.gpsimd.indirect_dma_start(rows2[:, j, :], None, key.rearrange("(r s) o -> r (s o)", s=KC),
                                                 bass.IndirectOffsetOnAxis(ap=index2[:, j:j + 1], axis=0),
                                                 bounds_check=KR - 1, oob_is_err=False).then_inc(gat2, 16)

            @block.vector
            def _(dve):
                def node(width):
                    return nid[:, :].unsqueeze(2).to_broadcast((P, NJ, width))

                dve.wait_ge(got, 16)
                nc.vector.tensor_tensor(hits[:, :, 0:KT], top[:, :].unsqueeze(1).to_broadcast((P, NJ, KT)), node(KT), ALU.is_le).then_inc(v, 1)
                dve.wait_ge(v, 1)
                nc.vector.tensor_reduce(below1[:, :], hits[:, :, 0:KT], AX.X, ALU.add).then_inc(v, 1)
                dve.wait_ge(v, 2)
                nc.vector.tensor_copy(index1[:, :], below1[:, :]).then_inc(v, 1)
                nc.vector.memset(edge[0:1, 0:1], -1).then_inc(chain, 1)
                dve.wait_ge(chain, 1)
                dve.wait_ge(edges_in, 32)
                nc.vector.tensor_tensor(mark[:, :], edge[:, 1:SC + 1], edge[:, 0:SC], ALU.is_equal).then_inc(chain, 1)
                dve.wait_ge(chain, 2)
                nc.vector.tensor_copy(mark16[:, :], mark[:, :]).then_inc(marked, 1)
                nc.vector.tensor_scalar(reset16[:, :], mark[:, :], -1.0, -NEG, ALU.add, ALU.mult).then_inc(marked, 1)
                if not o:
                    dve.wait_ge(w_in, 16)
                    nc.vector.tensor_tensor_scan(wrun[:, :], mark[:, :], wt[:, :], 0.0, ALU.mult, ALU.add).then_inc(carries, 1)
                    nc.vector.tensor_tensor_scan(wprod[:, :], mark[:, :], mark[:, :], 1.0, ALU.mult, ALU.min).then_inc(carries, 1)
                    nc.vector.memset(cscan[:, 0:1], 0.0).then_inc(chain, 1)
                    dve.wait_ge(cturn, 1)
                    nc.vector.tensor_copy(crow[:, :], pe1[:, :]).then_inc(cback, 1)
                    dve.wait_ge(cback, 1)
                    dve.wait_ge(chain, 3)
                    nc.vector.tensor_tensor_scan(cscan[:, 1:SR + 1], crow[:, SR:2 * SR], crow[:, 0:SR], 0.0, ALU.mult, ALU.add).then_inc(cback, 1)
                    dve.wait_ge(cturn, 2)
                    nc.vector.tensor_copy(ccol[:, :], pe2[:, :]).then_inc(chain, 1)
                    dve.wait_ge(chain, 4)
                    nc.vector.scalar_tensor_tensor(out=wall[:, :], in0=wprod[:, :], scalar=ccol[:, 0:1], in1=wrun[:, :],
                                                   op0=ALU.mult, op1=ALU.add).then_inc(chain, 1)
                dve.wait_ge(gat1, 16 * NJ)
                nc.vector.tensor_tensor(hits[:, :, 0:KT], rows1[:, :, :], node(KT), ALU.is_le).then_inc(v, 1)
                dve.wait_ge(v, 4)
                nc.vector.tensor_reduce(below2[:, :], hits[:, :, 0:KT], AX.X, ALU.add).then_inc(v, 1)
                dve.wait_ge(v, 5)
                nc.vector.scalar_tensor_tensor(out=row[:, :], in0=below1[:, :], scalar=float(KT), in1=below2[:, :],
                                               op0=ALU.mult, op1=ALU.add).then_inc(cback, 1)
                dve.wait_ge(cback, 1 if o else 3)
                nc.vector.tensor_copy(index2[:, :], row[:, :]).then_inc(v, 1)
                dve.wait_ge(gat2, 16 * NJ)
                nc.vector.tensor_tensor(hits[:, :, :], rows2[:, :, :], node(KC), ALU.is_le).then_inc(cback, 1)
                dve.wait_ge(cback, 2 if o else 4)
                nc.vector.tensor_reduce(below3[:, :], hits[:, :, :], AX.X, ALU.add).then_inc(cback, 1)
                dve.wait_ge(cback, 3 if o else 5)
                nc.vector.scalar_tensor_tensor(out=upto[:, :], in0=row[:, :], scalar=float(KC), in1=below3[:, :],
                                               op0=ALU.mult, op1=ALU.add).then_inc(v, 1)
                dve.wait_ge(v, 7)
                nc.vector.tensor_copy(before[:, 1:NJ], upto[:, 0:NJ - 1]).then_inc(cback, 1)
                nc.vector.memset(before[0:1, 0:1], 0.0).then_inc(v, 1)
                dve.wait_ge(cback, 4 if o else 6)
                dve.wait_ge(v, 8)
                dve.wait_ge(shifted, 16)
                n = 8

                def link(ins):
                    ins.then_inc(v, 1)

                link(nc.vector.tensor_tensor(info["cnt"][:, :], upto[:, :], before[:, :], ALU.subtract))
                link(nc.vector.tensor_scalar(f1[:, :], before[:, :], -float(NONE), None, ALU.add))
                link(nc.vector.tensor_scalar(l1[:, :], upto[:, :], -float(NONE + 1), None, ALU.add))
                link(nc.vector.tensor_scalar(s1[:, :], before[:, :], float(H), None, ALU.is_lt))
                link(nc.vector.tensor_scalar(s2[:, :], upto[:, :], float(H), None, ALU.is_gt))
                dve.wait_ge(v, n + 5)
                link(nc.vector.tensor_scalar(has[:, :], info["cnt"][:, :], 0.0, None, ALU.is_gt))
                link(nc.vector.tensor_tensor(info["span"][:, :], s1[:, :], s2[:, :], ALU.mult))
                dve.wait_ge(v, n + 7)
                link(nc.vector.tensor_tensor(f2[:, :], f1[:, :], has[:, :], ALU.mult))
                link(nc.vector.tensor_tensor(l2[:, :], l1[:, :], has[:, :], ALU.mult))
                dve.wait_ge(v, n + 9)
                link(nc.vector.tensor_scalar(info["first"][:, :], f2[:, :], float(NONE), None, ALU.add))
                link(nc.vector.tensor_scalar(info["last"][:, :], l2[:, :], float(NONE), None, ALU.add))

            @block.tensor
            def _(pe):
                if not o:
                    pe.wait_ge(carries, 2)
                    nc.tensor.matmul(pe1[:, 0:SR], wrun[:, SC - 1:SC], ident[0:SR, 0:SR], start=True, stop=True)
                    nc.tensor.matmul(pe1[:, SR:2 * SR], wprod[:, SC - 1:SC], ident[0:SR, 0:SR], start=True, stop=True).then_inc(cturn, 1)
                    pe.wait_ge(cback, 2)
                    nc.tensor.matmul(pe2[:, :], cscan[:, 0:SR], ident[0:1, 0:1], start=True, stop=True).then_inc(cturn, 1)


def edge_sums(nc, sb, ps, sem, ea64, marks, t1, ident, sel2):
    with Stage(nc) as c:
        ea = [sb(c, f"ea{i}", [P, C, 2, D]) for i in range(2)]
        mk = [sb(c, f"mk{i}", [2, 2, W], BF16) for i in range(2)]
        feat = [sb(c, f"feat{i}", [P, W]) for i in range(2)]
        run = [[sb(c, f"run{k}{i}", [P, W]) for i in range(2)] for k in range(2)]
        rows = [sb(c, f"rows{i}", [P, 2, C, 2, D]) for i in range(2)]
        p_in = [ps(c, f"p_in{i}", [P, C, P]) for i in range(2)]
        p_mk = [[ps(c, f"p_mk{k}{i}", [P, W]) for i in range(2)] for k in range(2)]
        p_out = [ps(c, f"p_out{k}", [P, C, P]) for k in range(2)]
        ea_in = [sem(c, f"ea_in{i}") for i in range(2)]
        stored = [sem(c, f"stored{i}") for i in range(2)]
        turned, spread, feats, summed, maxed, rowed, drained = (
            sem(c, n) for n in ("turned", "spread", "feats", "summed", "maxed", "rowed", "drained"))
        scanned = (summed, maxed)
        with nc.Block() as block:
            @block.sync
            def _(sp):
                def load(s, n, k, row, w):
                    row = sp.snap(row) if not isinstance(row, int) else row
                    wait_from(sp, spread, n - 1)
                    for h in range(2):
                        sp.dma_start(ea[s][0:w // C, :, h, :], by_edge(ea64, h, row, w)).then_inc(ea_in[s], 16)
                    sp.dma_start(mk[s][:, :, 0:w], marks[0][:, :, ds(row, w)]).then_inc(ea_in[s], 16)

                each_group(sp, load)

            @block.gpsimd
            def _(pool):
                def store(s, n, k, row, w):
                    pool.wait_ge(drained, 2 * n + 2)
                    for h in range(2):
                        pool.dma_start(by_edge(t1, h, row, w), rows[s][0:w // C, h, :, :, :].rearrange("p c k f -> p c (k f)")).then_inc(stored[s], 16)

                each_group(pool, store)
                for s in range(2):
                    pool.wait_ge(stored[s], 32 * ((NG + 2 - s) // 2))

            @block.tensor
            def _(pe):
                def spread_and_turn(s, n, k, row, w):
                    p = w // C
                    pe.wait_ge(ea_in[s], 48 * k + 48)
                    wait_from(pe, feats, n - 1)
                    for cc in range(C):
                        last = nc.tensor.transpose(p_in[s][:, cc, 0:p], ea[s][0:p, cc, :, :].rearrange("p h f -> p (h f)"), ident[0:p, 0:p])
                    last.then_inc(turned, 1)
                    wait_from(pe, maxed, n - 1)
                    for kind in range(2):
                        last = nc.tensor.matmul(p_mk[kind][s][:, 0:w], sel2[:, :], mk[s][:, kind, 0:w], start=True, stop=True)
                    last.then_inc(spread, 1)

                def turn_back(s, n, k, row, w):
                    p = w // C
                    for kind in range(2):
                        pe.wait_ge(scanned[kind], n + 1)
                        wait_from(pe, drained, 2 * n + kind - 1)
                        r = run[kind][s][:, 0:w].rearrange("q (p c) -> q p c", c=C)
                        for cc in range(C):
                            last = nc.tensor.transpose(p_out[kind][0:p, cc, :], r[:, :, cc], ident[:, :])
                        last.then_inc(rowed, 1)

                each_group(pe, spread_and_turn, turn_back)

            @block.scalar
            def _(act):
                def to_order(s, n, k, row, w):
                    p = w // C
                    act.wait_ge(turned, n + 1)
                    wait_from(act, maxed, n - 1)
                    nc.scalar.activation(feat[s][:, 0:w].rearrange("q (p c) -> q p c", c=C),
                                         p_in[s][:, :, 0:p].rearrange("q c p -> q p c"), ACT.Copy).then_inc(feats, 1)

                def to_rows(s, n, k, row, w):
                    p = w // C
                    wait_from(act, stored[s], 32 * k)
                    for kind in range(2):
                        act.wait_ge(rowed, 2 * n + kind + 1)
                        nc.scalar.activation(rows[s][0:p, :, :, kind, :].rearrange("p h c f -> p c h f"),
                                             p_out[kind][0:p, :, :].rearrange("p c (h f) -> p c h f", h=2),
                                             ACT.Copy).then_inc(drained, 1)

                each_group(act, to_order, to_rows)

            @block.vector
            def _(dve):
                def scan(s, n, k, row, w):
                    dve.wait_ge(spread, n + 1)
                    dve.wait_ge(feats, n + 1)
                    wait_from(dve, rowed, 2 * n - 2)
                    first = isinstance(n, int) and n == 0
                    for kind, (op0, op1, initial) in enumerate(((ALU.mult, ALU.add, 0.0), (ALU.add, ALU.max, NEG))):
                        if not first:
                            dve.wait_ge(scanned[kind], n)
                            initial = run[kind][1 - s][:, W - 1:W]
                        nc.vector.tensor_tensor_scan(run[kind][s][:, 0:w], p_mk[kind][s][:, 0:w], feat[s][:, 0:w],
                                                     initial, op0, op1).then_inc(scanned[kind], 1)

                each_group(dve, scan)


NB = 7
PARTS = ((0, 4), (4, 3))
ITERS = NJ // NB


def per_node(t, width=D):
    return t[:, :].unsqueeze(2).to_broadcast((P, NJ, width))


def per_feature(t, width=D):
    return t[:, :].unsqueeze(1).to_broadcast((P, NJ, width))


def row_of(vector, width=D):
    return vector.rearrange("(o f) -> o f", o=1).to_broadcast((P, width))


def column_of(vector):
    return vector.rearrange("(p o) -> p o", o=1)


def dense(nc, sb, ps, sem, groups, loads, hidden, last, put):
    NQ = len(groups)
    width = [sum(w for _, w in g) for g in groups]
    with Stage(nc) as c:
        w1, w2, bias1, bias2, bring, nload = loads(c)
        cat = [[sb(c, f"cat{q}{i}", [P, 4, width[q]]) for i in range(2)] for q in range(NQ)]
        feats = [[sb(c, f"feats{q}{i}", [P, 4 * P]) for i in range(2)] for q in range(NQ)]
        bank_in = [[ps(c, f"bank_in{q}{i}", [P, 4 * P]) for i in range(2)] for q in range(2)]
        bank_hid = [ps(c, f"bank_hid{i}", [P, 4 * P]) for i in range(2)]
        bank_out = [ps(c, f"bank_out{i}", [P, 4 * P]) for i in range(2)]
        chunks = hidden[1] if hidden else 0
        hid = [[sb(c, f"hid{m}{i}", [P, 4 * P]) for i in range(2)] for m in range(chunks)]
        outf = [sb(c, f"outf{i}", [last[1], 4 * P]) for i in range(2)]
        bank_of = (bank_hid, bank_in[1])
        weights_in, passed = sem(c, "weights_in"), sem(c, "passed")
        taken, turned, copied, summed, acted, mixed, biased, rowed, placed = (
            [sem(c, f"{n}{i}") for i in range(2)] for n in
            ("taken", "turned", "copied", "summed", "acted", "mixed", "biased", "rowed", "placed"))
        NCAT = sum(len(g) for g in groups)
        with nc.Block() as block:
            @block.sync
            def _(sp):
                bring(sp, weights_in)

            @block.vector
            def _(dve):
                with dve.Fori(0, ITERS) as it:
                    t = dve.snap(it)
                    for i, (a, k) in enumerate(PARTS):
                        dve.wait_ge(turned[i], t)
                        for q, g in enumerate(groups):
                            at = 0
                            for tensor, f in g:
                                nc.vector.tensor_copy(cat[q][i][:, 0:k, at:at + f], tensor[:, ds(t * NB + a, k), :]).then_inc(taken[i], 1)
                                at += f
                    for i, (a, k) in enumerate(PARTS):
                        dve.wait_ge(rowed[i], t + 1)
                        put(nc.vector, ds(t * NB + a, k), bank_in[0][i][:, 0:k * last[1]].rearrange("p (j f) -> p j f", f=last[1])).then_inc(placed[i], 1)

            @block.tensor
            def _(pe):
                pe.wait_ge(weights_in, nload)
                with pe.Fori(0, ITERS) as it:
                    t = pe.snap(it)
                    for i, (a, k) in enumerate(PARTS):
                        pe.wait_ge(taken[i], t * NCAT + NCAT)
                        pe.wait_ge(placed[i], t)
                        if chunks > 1:
                            pe.wait_ge(acted[i], t * chunks)
                        pe.sem_inc(passed, 1)
                        for q in range(NQ):
                            for j in range(k):
                                last_mm = nc.tensor.transpose(bank_in[q][i][0:width[q], j * P:(j + 1) * P], cat[q][i][:, j, :], ident_of[0][:, :])
                        last_mm.then_inc(turned[i], 1)
                    for m in range(chunks):
                        for i, (a, k) in enumerate(PARTS):
                            pe.wait_ge(copied[i], t * NQ + NQ)
                            pe.wait_ge(acted[i], t * chunks)
                            for q in range(NQ):
                                mm = nc.tensor.matmul(bank_of[m][i][:, 0:k * P], w1[q][0:width[q], m * P:(m + 1) * P], feats[q][i][0:width[q], 0:k * P],
                                                      start=q == 0, stop=q == NQ - 1)
                            mm.then_inc(summed[i], 1)
                    for i, (a, k) in enumerate(PARTS):
                        if chunks:
                            pe.wait_ge(acted[i], t * chunks + chunks)
                        else:
                            pe.wait_ge(copied[i], t * NQ + NQ)
                        pe.wait_ge(biased[i], t)
                        ins = [(w2[m], hid[m][i]) for m in range(chunks)] or [(w1[0][0:width[0], :], feats[0][i][0:width[0], :])]
                        for m, (wm, xm) in enumerate(ins):
                            mm = nc.tensor.matmul(bank_out[i][0:last[1], 0:k * P], wm, xm[:, 0:k * P], start=m == 0, stop=m == len(ins) - 1)
                        mm.then_inc(mixed[i], 1)
                    for i, (a, k) in enumerate(PARTS):
                        pe.wait_ge(biased[i], t + 1)
                        pe.sem_inc(passed, 1)
                        for j in range(k):
                            mm = nc.tensor.transpose(bank_in[0][i][:, j * last[1]:(j + 1) * last[1]], outf[i][:, j * P:(j + 1) * P], ident_of[0][0:last[1], 0:last[1]])
                        mm.then_inc(rowed[i], 1)

            @block.scalar
            def _(act):
                act.wait_ge(weights_in, nload)
                with act.Fori(0, ITERS) as it:
                    t = act.snap(it)
                    for i, (a, k) in enumerate(PARTS):
                        act.wait_ge(turned[i], t + 1)
                        act.wait_ge(mixed[i], t)
                        for q in range(NQ):
                            nc.scalar.activation(feats[q][i][0:width[q], 0:k * P], bank_in[q][i][0:width[q], 0:k * P], ACT.Copy).then_inc(copied[i], 1)
                    for m in range(chunks):
                        for i, (a, k) in enumerate(PARTS):
                            act.wait_ge(summed[i], t * chunks + m + 1)
                            nc.scalar.activation(hid[m][i][:, 0:k * P], bank_of[m][i][:, 0:k * P], hidden[0], bias=bias1[:, m:m + 1]).then_inc(acted[i], 1)
                    for i, (a, k) in enumerate(PARTS):
                        act.wait_ge(mixed[i], t + 1)
                        act.wait_ge(rowed[i], t)
                        nc.scalar.activation(outf[i][:, 0:k * P], bank_out[i][0:last[1], 0:k * P], last[0], bias=bias2[:, 0:1]).then_inc(biased[i], 1)


ident_of = [None]


def norm(nc, sb, sem, ahead, t, o, behind):
    with Stage(nc) as c:
        s_sum, s_mean, s_sq, s_var, s_sd, s_rs = (sb(c, n, [P, NJ]) for n in ("s_sum", "s_mean", "s_sq", "s_var", "s_sd", "s_rs"))
        chain, root = sem(c, "chain"), sem(c, "root")
        with nc.Block() as block:
            @block.vector
            def _(dve):
                count = [0]

                def link(ins):
                    count[0] += 1
                    ins.then_inc(chain, 1)
                    dve.wait_ge(chain, count[0])

                for f in ahead:
                    link(f(nc.vector))
                link(nc.vector.tensor_reduce(s_sum[:, :], t[:, :, :], AX.X, ALU.add))
                link(nc.vector.tensor_scalar(s_mean[:, :], s_sum[:, :], 1.0 / D, None, ALU.mult))
                link(nc.vector.tensor_tensor(o[:, :, :], t[:, :, :], per_node(s_mean), ALU.subtract))
                link(nc.vector.tensor_tensor(t[:, :, :], o[:, :, :], o[:, :, :], ALU.mult))
                link(nc.vector.tensor_reduce(s_sq[:, :], t[:, :, :], AX.X, ALU.add))
                link(nc.vector.tensor_scalar(s_var[:, :], s_sq[:, :], 1.0 / D, EPS, ALU.mult, ALU.add))
                dve.wait_ge(root, 1)
                link(nc.vector.reciprocal(s_rs[:, :], s_sd[:, :]))
                link(nc.vector.tensor_tensor(o[:, :, :], o[:, :, :], per_node(s_rs), ALU.mult))
                for f in behind:
                    link(f(nc.vector))

            @block.scalar
            def _(act):
                act.wait_ge(chain, len(ahead) + 6)
                nc.scalar.activation(s_sd[:, :], s_var[:, :], ACT.Sqrt).then_inc(root, 1)


def gather_rows(pool, nc, dest, width, table, index, counted):
    for j in range(NJ):
        nc.gpsimd.indirect_dma_start(dest[:, j, :], None, table, bass.IndirectOffsetOnAxis(ap=index[:, j:j + 1], axis=0),
                                     bounds_check=E - 1, oob_is_err=False).then_inc(counted, 16)


def node_layers_1_2(nc, sb, ps, sem, X, info, t1, wsum, ident, w0a, b0a, w0b, b0b, u1, w1a, b1a, w1b, b1b, g1, be1):
    with Stage(nc) as c:
        agg = sb(c, "agg", [P, NJ, 2 * D])
        mean = sb(c, "mean", [P, NJ, D])
        Y, Z = sb(c, "Y", [P, NJ, D]), sb(c, "Z", [P, NJ, D])
        GA, BE = sb(c, "GA", [P, D]), sb(c, "BE", [P, D])
        with Stage(nc) as cc:
            wn = sb(cc, "wn", [P, NJ, 1])
            carry = sb(cc, "carry", [P, 2 * D])
            nz, iszero, safe, inv, reset, atleast, per = (sb(cc, n, [P, NJ]) for n in ("nz", "iszero", "safe", "inv", "reset", "atleast", "per"))
            cleared, agg_in, wn_in, carry_in, chain = (sem(cc, n) for n in ("cleared", "agg_in", "wn_in", "carry_in", "chain"))
            with nc.Block() as block:
                @block.sync
                def _(sp):
                    sp.dma_start(carry[:, :], t1[H - 1:H, :].to_broadcast((P, 2 * D))).then_inc(carry_in, 16)
                    sp.dma_start(GA[:, :], row_of(g1)).then_inc(carry_in, 16)
                    sp.dma_start(BE[:, :], row_of(be1)).then_inc(carry_in, 16)

                @block.gpsimd
                def _(pool):
                    pool.wait_ge(cleared, 2)
                    gather_rows(pool, nc, wn, 1, wsum, info["last"], wn_in)
                    gather_rows(pool, nc, agg, 2 * D, t1, info["last"], agg_in)

                @block.vector
                def _(dve):
                    count = [0]

                    def link(ins):
                        count[0] += 1
                        ins.then_inc(chain, 1)
                        dve.wait_ge(chain, count[0])

                    nc.vector.memset(wn[:, :, :], 0.0).then_inc(cleared, 1)
                    nc.vector.memset(agg[:, :, :], 0.0).then_inc(cleared, 1)
                    dve.wait_ge(wn_in, 16 * NJ)
                    w = wn[:, :, 0]
                    link(nc.vector.tensor_scalar(nz[:, :], w, 0.0, None, ALU.not_equal))
                    link(nc.vector.tensor_scalar(iszero[:, :], w, 0.0, None, ALU.is_equal))
                    link(nc.vector.tensor_tensor(safe[:, :], iszero[:, :], w, ALU.add))
                    link(nc.vector.reciprocal(inv[:, :], safe[:, :]))
                    link(nc.vector.tensor_tensor(Y[:, :, :], X[:, :, :], wn[:, :, :].to_broadcast((P, NJ, D)), ALU.mult))
                    link(nc.vector.tensor_tensor(Z[:, :, :], Y[:, :, :], per_node(inv), ALU.mult))
                    link(nc.vector.tensor_tensor(Y[:, :, :], Z[:, :, :], X[:, :, :], ALU.add))
                    link(nc.vector.tensor_tensor(Z[:, :, :], Y[:, :, :], per_node(nz), ALU.mult))
                    link(nc.vector.tensor_scalar(reset[:, :], info["span"][:, :], -1.0, -NEG, ALU.add, ALU.mult))
                    link(nc.vector.tensor_scalar(atleast[:, :], info["cnt"][:, :], 1.0, None, ALU.max))
                    link(nc.vector.reciprocal(per[:, :], atleast[:, :]))
                    dve.wait_ge(agg_in, 16 * NJ)
                    dve.wait_ge(carry_in, 48)
                    link(nc.vector.tensor_tensor(mean[:, :, :], per_node(info["span"]), per_feature(carry[:, 0:D]), ALU.mult))
                    link(nc.vector.tensor_tensor(agg[:, :, 0:D], agg[:, :, 0:D], mean[:, :, :], ALU.add))
                    link(nc.vector.tensor_tensor(mean[:, :, :], per_node(info["span"]), per_feature(carry[:, D:2 * D]), ALU.mult))
                    link(nc.vector.tensor_tensor(mean[:, :, :], mean[:, :, :], per_node(reset), ALU.add))
                    has = count[0]
                    link(nc.vector.tensor_tensor(agg[:, :, D:2 * D], agg[:, :, D:2 * D], mean[:, :, :], ALU.max))
                    link(nc.vector.tensor_tensor(mean[:, :, :], agg[:, :, 0:D], per_node(per), ALU.mult))

        def loads_1(c):
            W1, W2 = sb(c, "W1", [D, 2 * P]), sb(c, "W2", [P, 2, D])
            B1, B2 = sb(c, "B1", [P, 2]), sb(c, "B2", [D, 1])

            def bring(sp, done):
                sp.dma_start(W1[:, :], w0a).then_inc(done, 16)
                sp.dma_start(W2[:, :, :], w0b.rearrange("(q p) f -> p q f", q=2)).then_inc(done, 16)
                with nc.allow_non_contiguous_dma(reason="biases by partition"):
                    sp.dma_start(B1[:, :], b0a.rearrange("(q p) -> p q", q=2)).then_inc(done, 16)
                    sp.dma_start(B2[:, :], column_of(b0b)).then_inc(done, 16)
            return [W1], [W2[:, 0, :], W2[:, 1, :]], B1, B2, bring, 64

        dense(nc, sb, ps, sem, [[(Z, D)]], loads_1, (ACT.Relu, 2), (ACT.Relu, D),
              lambda eng, cols, bank: eng.tensor_tensor(Y[:, cols, :], X[:, cols, :], bank, ALU.add))
        norm(nc, sb, sem, [], Y, X, [])

        V1a, V1b, V2 = sb(c, "V1a", [P, P]), sb(c, "V1b", [P, P]), sb(c, "V2", [P, D])
        VU, UB, C1, C1B, C2 = (sb(c, n, [P, 1]) for n in ("VU", "UB", "C1", "C1B", "C2"))
        weights2, folded = sem(c, "weights2"), sem(c, "folded")
        with nc.Block() as block:
            @block.sync
            def _(sp):
                sp.dma_start(V1a[:, :], w1a[D:3 * D, :]).then_inc(weights2, 16)
                sp.dma_start(V1b[0:D, :], w1a[0:D, :]).then_inc(weights2, 16)
                sp.dma_start(V1b[D:P, :], w1a[3 * D:4 * D, :]).then_inc(weights2, 16)
                sp.dma_start(V2[:, :], w1b).then_inc(weights2, 16)
                with nc.allow_non_contiguous_dma(reason="biases by partition"):
                    sp.dma_start(C1[:, :], column_of(b1a)).then_inc(weights2, 16)
                    sp.dma_start(C2[0:D, :], column_of(b1b)).then_inc(weights2, 16)
                    sp.dma_start(VU[:, :], w1a[4 * D:4 * D + 1, :].rearrange("o f -> f o")).then_inc(weights2, 16)
                    sp.dma_start(UB[:, :], u1[0:1, 0:1].to_broadcast((P, 1))).then_inc(weights2, 16)

            @block.vector
            def _(dve):
                dve.wait_ge(weights2, 16 * 8)
                nc.vector.scalar_tensor_tensor(out=C1B[:, :], in0=VU[:, :], scalar=UB[:, 0:1], in1=C1[:, :],
                                               op0=ALU.mult, op1=ALU.add).then_inc(folded, 1)

        dense(nc, sb, ps, sem, [[(agg, 2 * D)], [(X, D), (mean, D)]], lambda c: ([V1a, V1b], [V2[:, :]], C1B, C2[0:D, :], lambda sp, done: None, 0),
              (ACT.Gelu, 1), (ACT.Identity, D), lambda eng, cols, bank: eng.tensor_copy(Y[:, cols, :], bank))
        norm(nc, sb, sem, [], Y, Z, [
            lambda eng: eng.tensor_tensor(Y[:, :, :], Z[:, :, :], per_feature(GA), ALU.mult),
            lambda eng: eng.tensor_tensor(Z[:, :, :], Y[:, :, :], per_feature(BE), ALU.add),
            lambda eng: eng.tensor_tensor(Y[:, :, :], Z[:, :, :], X[:, :, :], ALU.add),
            lambda eng: eng.tensor_tensor(Z[:, :, :], Y[:, :, :], X[:, :, :], ALU.add)])
        norm(nc, sb, sem, [], Z, X, [])


def node_tables(nc, sb, ps, sem, which, X, info, key, gathered, spread, tabg, tabs, start, ident):
    with Stage(nc) as c:
        rows = sb(c, "rows", [P, NJ, 2 * D])
        prime_key = sb(c, "prime_key", [2, 1], I32)
        prime = sb(c, "prime", [2, D])

        def loads(cc):
            WW, BB = sb(cc, "WW", [D, 2 * D]), sb(cc, "BB", [2 * D, 1])
            biases = [b for b in (gathered[1], spread[1]) if b is not None]
            zero = sem(cc, "zero")

            def bring(sp, done):
                sp.dma_start(WW[:, 0:D], gathered[0]).then_inc(done, 16)
                sp.dma_start(WW[:, D:2 * D], spread[0]).then_inc(done, 16)
                if len(biases) < 2:
                    sp.wait_ge(zero, 1)
                for q, b in enumerate(biases):
                    with nc.allow_non_contiguous_dma(reason="biases by partition"):
                        sp.dma_start(BB[q * D:(q + 1) * D, :], column_of(b)).then_inc(done, 16)

            if len(biases) < 2:
                with nc.Block() as block:
                    @block.vector
                    def _(dve):
                        nc.vector.memset(BB[:, :], 0.0).then_inc(zero, 1)
            return [WW], None, None, BB, bring, 32 + 16 * len(biases)

        dense(nc, sb, ps, sem, [[(X, D)]], loads, None, (ACT.Identity, 2 * D),
              lambda eng, cols, bank: eng.tensor_copy(rows[:, cols, :], bank))
        stored, keyed, primed, firsts, put = (sem(c, n) for n in ("stored", "keyed", "primed", "firsts", "put"))
        with nc.Block() as block:
            @block.sync
            def _(sp):
                sp.dma_start(prime_key[:, :], key[H:H + 1, :].to_broadcast((2, 1))).then_inc(keyed, 16)
                sp.dma_start(tabs.rearrange("(p j) f -> p j f", j=NJ), rows[:, :, D:2 * D]).then_inc(stored, 16)
                sp.dma_start(tabg.rearrange("(p j) f -> p j f", j=NJ), rows[:, :, 0:D]).then_inc(stored, 16)
                sp.wait_ge(primed, 16)
                sp.wait_ge(firsts, 16 * NJ)
                sp.dma_start(start[H:H + 1, :], prime[0:1, :]).then_inc(put, 16)
                sp.wait_ge(put, 16)

            @block.gpsimd
            def _(pool):
                for j in range(NJ):
                    nc.gpsimd.indirect_dma_start(start, bass.IndirectOffsetOnAxis(ap=info["first"][:, j:j + 1], axis=0), rows[:, j, D:2 * D], None,
                                                 bounds_check=E - 1, oob_is_err=False).then_inc(firsts, 16)
                pool.wait_ge(keyed, 16)
                pool.wait_ge(stored, 32)
                nc.gpsimd.indirect_dma_start(prime[:, :], None, tabs, bass.IndirectOffsetOnAxis(ap=prime_key[:, :], axis=0)).then_inc(primed, 16)


def edges_3(nc, sb, ps, sem, other, marks, tabg, start, t2, ident, sel2, w2b, b2b, w2g, b2g):
    with Stage(nc) as c:
        W2, WG = sb(c, "W2", [P, P]), sb(c, "WG", [P, P])
        B2, BG = sb(c, "B2", [P, 1]), sb(c, "BG", [P, 1])
        first = [sb(c, f"first{i}", [P, C, 2, D]) for i in range(2)]
        mk = [sb(c, f"mk{i}", [2, W], BF16) for i in range(2)]
        ix = [sb(c, f"ix{i}", [P, 2, C], I32) for i in range(2)]
        got = [sb(c, f"got{i}", [P, C, 2, D]) for i in range(2)]
        starts, own, pre, hid, inter, gate, gated, run = (
            [sb(c, f"{n}{i}", [P, W]) for i in range(2)] for n in ("starts", "own", "pre", "hid", "inter", "gate", "gated", "run"))
        rows = [sb(c, f"rows{i}", [P, 2, C, D]) for i in range(2)]
        p_first, p_got, p_inter, p_gate = (ps(c, n, [P, C * P]) for n in ("p_first", "p_got", "p_inter", "p_gate"))
        p_mk = [ps(c, f"p_mk{i}", [P, W]) for i in range(2)]
        p_out = [ps(c, f"p_out{i}", [P, C, P]) for i in range(2)]
        zeroed, weights_in, passed = (sem(c, n) for n in ("zeroed", "weights_in", "passed"))
        first_in, ix_in, got_in, stored = ([sem(c, f"{n}{i}") for i in range(2)] for n in ("first_in", "ix_in", "got_in", "stored"))
        marked, turned_first, turned_got, started, owned, added, relued, mixed, biased, scored, gates, products, summed, rowed, drained = (
            sem(c, n) for n in ("marked", "turned_first", "turned_got", "started", "owned", "added", "relued", "mixed", "biased",
                                "scored", "gates", "products", "summed", "rowed", "drained"))
        with nc.Block() as block:
            @block.sync
            def _(sp):
                sp.wait_ge(zeroed, 2)
                for h in range(2):
                    at = slice(h * D, (h + 1) * D)
                    for t, w in ((W2, w2b), (WG, w2g)):
                        sp.dma_start(t[at, at], w).then_inc(weights_in, 16)
                    with nc.allow_non_contiguous_dma(reason="biases by partition"):
                        for t, b in ((B2, b2b), (BG, b2g)):
                            sp.dma_start(t[at, :], column_of(b)).then_inc(weights_in, 16)

                def load(s, n, k, row, w):
                    row = row if isinstance(row, int) else sp.snap(row)
                    wait_from(sp, turned_got, n - 1)
                    for h in range(2):
                        sp.dma_start(ix[s][0:w // C, h, :], by_edge(other, h, row, w).rearrange("p c o -> p (c o)")).then_inc(ix_in[s], 16)
                    wait_from(sp, marked, n - 1)
                    for h in range(2):
                        sp.dma_start(first[s][0:w // C, :, h, :], by_edge(start, h, row, w)).then_inc(first_in[s], 16)
                    sp.dma_start(mk[s][:, 0:w], marks[1][:, 0, ds(row, w)]).then_inc(first_in[s], 16)

                each_group(sp, load)

            @block.gpsimd
            def _(pool):
                def gather(s, n, k, row, w):
                    pool.wait_ge(ix_in[s], 32 * k + 32)
                    wait_from(pool, turned_got, n - 1)
                    pool.sem_inc(passed, 1)
                    for cc in range(C):
                        for h in range(2):
                            nc.gpsimd.indirect_dma_start(got[s][0:w // C, cc, h, :], None, tabg,
                                                         bass.IndirectOffsetOnAxis(ap=ix[s][0:w // C, h, cc:cc + 1], axis=0)).then_inc(got_in[s], 16)
                each_group(pool, gather)

            @block.tensor
            def _(pe):
                pe.wait_ge(weights_in, 128)

                def interact(s, n, k, row, w):
                    p = w // C
                    pe.wait_ge(first_in[s], 48 * k + 48)
                    wait_from(pe, started, n)
                    for cc in range(C):
                        mm = nc.tensor.transpose(p_first[:, cc * P:cc * P + p], first[s][0:p, cc, :, :].rearrange("p h f -> p (h f)"), ident[0:p, 0:p])
                    mm.then_inc(turned_first, 1)
                    wait_from(pe, summed, n - 1)
                    nc.tensor.matmul(p_mk[s][:, 0:w], sel2[:, :], mk[s][:, 0:w], start=True, stop=True).then_inc(marked, 1)
                    pe.wait_ge(got_in[s], 128 * k + 128)
                    wait_from(pe, added, n)
                    for cc in range(C):
                        mm = nc.tensor.transpose(p_got[:, cc * P:cc * P + p], got[s][0:p, cc, :, :].rearrange("p h f -> p (h f)"), ident[0:p, 0:p])
                    mm.then_inc(turned_got, 1)
                    pe.wait_ge(relued, n + 1)
                    nc.tensor.matmul(p_inter[:, 0:w], W2[:, :], hid[s][:, 0:w], start=True, stop=True).then_inc(mixed, 1)
                    pe.wait_ge(biased, n + 1)
                    nc.tensor.matmul(p_gate[:, 0:w], WG[:, :], inter[s][:, 0:w], start=True, stop=True).then_inc(scored, 1)

                def turn_back(s, n, k, row, w):
                    p = w // C
                    pe.wait_ge(summed, n + 1)
                    wait_from(pe, drained, n - 1)
                    r = run[s][:, 0:w].rearrange("q (p c) -> q p c", c=C)
                    for cc in range(C):
                        mm = nc.tensor.transpose(p_out[s][0:p, cc, :], r[:, :, cc], ident[:, :])
                    mm.then_inc(rowed, 1)

                each_group(pe, interact, turn_back)

            @block.scalar
            def _(act):
                act.wait_ge(weights_in, 128)

                def activate(s, n, k, row, w):
                    p = w // C
                    act.wait_ge(turned_first, n + 1)
                    wait_from(act, owned, n - 1)
                    nc.scalar.activation(starts[s][:, 0:w].rearrange("q (p c) -> q p c", c=C),
                                         p_first[:, :].rearrange("q (c p) -> q p c", c=C)[:, 0:p, :], ACT.Copy).then_inc(started, 1)
                    act.wait_ge(added, n + 1)
                    wait_from(act, mixed, n - 1)
                    nc.scalar.activation(hid[s][:, 0:w], pre[s][:, 0:w], ACT.Relu).then_inc(relued, 1)
                    act.wait_ge(mixed, n + 1)
                    wait_from(act, products, n - 1)
                    nc.scalar.activation(inter[s][:, 0:w], p_inter[:, 0:w], ACT.Identity, bias=B2[:, 0:1]).then_inc(biased, 1)
                    act.wait_ge(scored, n + 1)
                    nc.scalar.activation(gate[s][:, 0:w], p_gate[:, 0:w], ACT.Sigmoid, bias=BG[:, 0:1]).then_inc(gates, 1)

                def to_rows(s, n, k, row, w):
                    p = w // C
                    act.wait_ge(rowed, n + 1)
                    wait_from(act, stored[s], 32 * k)
                    nc.scalar.activation(rows[s][0:p, :, :, :].rearrange("p h c f -> p c h f"),
                                         p_out[s][0:p, :, :].rearrange("p c (h f) -> p c h f", h=2), ACT.Copy).then_inc(drained, 1)
                    act.wait_ge(drained, n + 1)
                    for h in range(2):
                        act.dma_start(by_edge(t2, h, row, w), rows[s][0:p, h, :, :]).then_inc(stored[s], 16)

                each_group(act, activate, to_rows)
                for s in range(2):
                    act.wait_ge(stored[s], 32 * ((NG + 2 - s) // 2))

            @block.vector
            def _(dve):
                nc.vector.memset(W2[:, :], 0.0).then_inc(zeroed, 1)
                nc.vector.memset(WG[:, :], 0.0).then_inc(zeroed, 1)

                def work(s, n, k, row, w):
                    p = w // C
                    zero = isinstance(n, int) and n == 0
                    dve.wait_ge(marked, n + 1)
                    dve.wait_ge(started, n + 1)
                    wait_from(dve, added, n)
                    nc.vector.tensor_tensor_scan(own[s][:, 0:w], p_mk[s][:, 0:w], starts[s][:, 0:w],
                                                 0.0 if zero else own[1 - s][:, W - 1:W], ALU.mult, ALU.add).then_inc(owned, 1)
                    dve.wait_ge(owned, n + 1)
                    dve.wait_ge(turned_got, n + 1)
                    wait_from(dve, relued, n - 1)
                    nc.vector.tensor_tensor(pre[s][:, 0:w].rearrange("q (p c) -> q p c", c=C), own[s][:, 0:w].rearrange("q (p c) -> q p c", c=C),
                                            p_got[:, :].rearrange("q (c p) -> q p c", c=C)[:, 0:p, :], ALU.add).then_inc(added, 1)
                    dve.wait_ge(gates, n + 1)
                    wait_from(dve, summed, n)
                    nc.vector.tensor_tensor(gated[s][:, 0:w], inter[s][:, 0:w], gate[s][:, 0:w], ALU.mult).then_inc(products, 1)
                    dve.wait_ge(products, n + 1)
                    wait_from(dve, rowed, n - 1)
                    nc.vector.tensor_tensor_scan(run[s][:, 0:w], p_mk[s][:, 0:w], gated[s][:, 0:w],
                                                 0.0 if zero else run[1 - s][:, W - 1:W], ALU.mult, ALU.add).then_inc(summed, 1)

                each_group(dve, work)


def pool_3(nc, sb, ps, sem, X, info, t2):
    with Stage(nc) as c:
        pooled, Z = sb(c, "pooled", [P, NJ, D]), sb(c, "Z", [P, NJ, D])
        carry = sb(c, "carry", [P, D])
        atleast, per = sb(c, "atleast", [P, NJ]), sb(c, "per", [P, NJ])
        cleared, rows_in, carry_in, chain = (sem(c, n) for n in ("cleared", "rows_in", "carry_in", "chain"))
        with nc.Block() as block:
            @block.sync
            def _(sp):
                sp.dma_start(carry[:, :], t2[H - 1:H, :].to_broadcast((P, D))).then_inc(carry_in, 16)

            @block.gpsimd
            def _(pool):
                pool.wait_ge(cleared, 1)
                gather_rows(pool, nc, pooled, D, t2, info["last"], rows_in)

            @block.vector
            def _(dve):
                nc.vector.memset(pooled[:, :, :], 0.0).then_inc(cleared, 1)
                nc.vector.tensor_scalar(atleast[:, :], info["cnt"][:, :], 1.0, None, ALU.max).then_inc(chain, 1)
                dve.wait_ge(chain, 1)
                nc.vector.reciprocal(per[:, :], atleast[:, :]).then_inc(chain, 1)
                dve.wait_ge(carry_in, 16)
                nc.vector.tensor_tensor(Z[:, :, :], per_node(info["span"]), per_feature(carry), ALU.mult).then_inc(chain, 1)
                dve.wait_ge(chain, 3)
                dve.wait_ge(rows_in, 16 * NJ)
                nc.vector.tensor_tensor(pooled[:, :, :], pooled[:, :, :], Z[:, :, :], ALU.add).then_inc(chain, 1)
                dve.wait_ge(chain, 4)
                nc.vector.tensor_tensor(pooled[:, :, :], pooled[:, :, :], per_node(per), ALU.mult).then_inc(chain, 1)
                dve.wait_ge(chain, 5)
                nc.vector.tensor_tensor(Z[:, :, :], pooled[:, :, :], X[:, :, :], ALU.add).then_inc(chain, 1)
        norm(nc, sb, sem, [], Z, X, [])


def edges_4(nc, sb, ps, sem, other, ea16, marks, tabg, start, t3, ident, sel2, we, att):
    R = 2 * HEADS
    with Stage(nc) as c:
        WE, AT = sb(c, "WE", [2 * ED, P]), sb(c, "AT", [P, R])
        sel8, sel8a, sel8b = (sb(c, n, [R, P]) for n in ("sel8", "sel8a", "sel8b"))
        first, got = ([sb(c, f"{n}{i}", [P, C, 2, D]) for i in range(2)] for n in ("first", "got"))
        ea = [sb(c, f"ea{i}", [P, C, 2, ED]) for i in range(2)]
        mk = [sb(c, f"mk{i}", [2, W], BF16) for i in range(2)]
        reset = [sb(c, f"reset{i}", [R, W], BF16) for i in range(2)]
        ix = [sb(c, f"ix{i}", [P, 2, C], I32) for i in range(2)]
        starts, own, theirs, both, pre, act_in, weighted, run = (
            [sb(c, f"{n}{i}", [P, W]) for i in range(2)] for n in ("starts", "own", "theirs", "both", "pre", "act_in", "weighted", "run"))
        eat = [sb(c, f"eat{i}", [2 * ED, W]) for i in range(2)]
        top = [sb(c, f"top{i}", [R, 1 + W]) for i in range(2)]
        left = [sb(c, f"left{i}", [R, W]) for i in range(2)]
        expo, grow = ([sb(c, f"{n}{i}", [R, 2, W]) for i in range(2)] for n in ("expo", "grow"))
        den = [sb(c, f"den{i}", [R, W]) for i in range(2)]
        rows = [sb(c, f"rows{i}", [P, 2, C, T3]) for i in range(2)]
        p_turn, p_keep, p_mk, p_small, p_pre, p_logit, p_take, p_out = (
            ps(c, n, [P, C * P]) for n in ("p_turn", "p_keep", "p_mk", "p_small", "p_pre", "p_logit", "p_take", "p_out"))
        zeroed, made, weights_in, passed = (sem(c, n) for n in ("zeroed", "made", "weights_in", "passed"))
        first_in, ix_in, got_in, stored = ([sem(c, f"{n}{i}") for i in range(2)] for n in ("first_in", "ix_in", "got_in", "stored"))
        (marked, turned_first, turned_ea, turned_got, started, featured, gotten, summed_ea, owned, twice, added, leaked, scored,
         carried, maxed, lefts, expos, grown, kept, taken, weighted_s, summed, dens, rowed, drained) = (
            sem(c, n) for n in ("marked", "turned_first", "turned_ea", "turned_got", "started", "featured", "gotten", "summed_ea",
                                "owned", "twice", "added", "leaked", "scored", "carried", "maxed", "lefts", "expos", "grown", "kept",
                                "taken", "weighted_s", "summed", "dens", "rowed", "drained"))
        with nc.Block() as block:
            @block.sync
            def _(sp):
                sp.wait_ge(zeroed, 2)
                for h in range(2):
                    sp.dma_start(WE[h * ED:(h + 1) * ED, h * D:(h + 1) * D], we).then_inc(weights_in, 16)
                    for a in range(HEADS):
                        at = h * D + a * HC
                        with nc.allow_non_contiguous_dma(reason="a head's vector by partition"):
                            sp.dma_start(AT[at:at + HC, h * HEADS + a:h * HEADS + a + 1], att[a:a + 1, :].rearrange("o f -> f o")).then_inc(weights_in, 16)

                def load(s, n, k, row, w):
                    row = row if isinstance(row, int) else sp.snap(row)
                    wait_from(sp, turned_got, n - 1)
                    for h in range(2):
                        sp.dma_start(ix[s][0:w // C, h, :], by_edge(other, h, row, w).rearrange("p c o -> p (c o)")).then_inc(ix_in[s], 16)
                    wait_from(sp, lefts, n - 1)
                    for h in range(2):
                        sp.dma_start(first[s][0:w // C, :, h, :], by_edge(start, h, row, w)).then_inc(first_in[s], 16)
                        sp.dma_start(ea[s][0:w // C, :, h, :], by_edge(ea16, h, row, w)).then_inc(first_in[s], 16)
                        sp.dma_start(reset[s][h * HEADS:(h + 1) * HEADS, 0:w], marks[0][h, 1:2, ds(row, w)].to_broadcast((HEADS, w))).then_inc(first_in[s], 16)
                    sp.dma_start(mk[s][:, 0:w], marks[0][:, 0, ds(row, w)]).then_inc(first_in[s], 16)

                each_group(sp, load)

            @block.gpsimd
            def _(pool):
                nc.gpsimd.memset(sel8[:, :], 1.0).then_inc(made, 1)
                pool.wait_ge(made, 1)
                nc.gpsimd.affine_select(out=sel8a[:, :], in_=sel8[:, :], compare_op=ALU.is_ge, fill=0.0, base=0,
                                        pattern=[[1, P]], channel_multiplier=-HC).then_inc(made, 1)
                pool.wait_ge(made, 2)
                nc.gpsimd.affine_select(out=sel8b[:, :], in_=sel8a[:, :], compare_op=ALU.is_ge, fill=0.0, base=HC - 1,
                                        pattern=[[-1, P]], channel_multiplier=HC).then_inc(made, 1)

                def gather(s, n, k, row, w):
                    pool.wait_ge(ix_in[s], 32 * k + 32)
                    wait_from(pool, turned_got, n - 1)
                    pool.sem_inc(passed, 1)
                    for cc in range(C):
                        for h in range(2):
                            nc.gpsimd.indirect_dma_start(got[s][0:w // C, cc, h, :], None, tabg,
                                                         bass.IndirectOffsetOnAxis(ap=ix[s][0:w // C, h, cc:cc + 1], axis=0)).then_inc(got_in[s], 16)
                each_group(pool, gather)

            @block.tensor
            def _(pe):
                pe.wait_ge(weights_in, 160)
                pe.wait_ge(made, 3)

                def keep_and_take(s, n, k, row, w):
                    pe.wait_ge(grown, n + 1)
                    wait_from(pe, weighted_s, n)
                    nc.tensor.matmul(p_take[:, 0:w], sel8b[:, :], grow[s][:, 1, 0:w], start=True, stop=True).then_inc(taken, 1)
                    wait_from(pe, summed, n)
                    nc.tensor.matmul(p_keep[:, 0:w], sel8b[:, :], grow[s][:, 0, 0:w], start=True, stop=True).then_inc(kept, 1)

                def front(s, n, k, row, w):
                    p = w // C
                    if not isinstance(n, int) or n:
                        keep_and_take(1 - s, n - 1, None, None, W)
                    pe.wait_ge(first_in[s], 112 * k + 112)
                    wait_from(pe, gotten, n)
                    for cc in range(C):
                        mm = nc.tensor.transpose(p_turn[:, cc * P:cc * P + p], first[s][0:p, cc, :, :].rearrange("p h f -> p (h f)"), ident[0:p, 0:p])
                    mm.then_inc(turned_first, 1)
                    wait_from(pe, owned, n)
                    nc.tensor.matmul(p_mk[:, 0:w], sel2[:, :], mk[s][:, 0:w], start=True, stop=True).then_inc(marked, 1)
                    wait_from(pe, drained, 3 * n - 3)
                    for cc in range(C):
                        mm = nc.tensor.transpose(p_small[0:2 * ED, cc * P:cc * P + p], ea[s][0:p, cc, :, :].rearrange("p h f -> p (h f)"), ident[0:p, 0:p])
                    mm.then_inc(turned_ea, 1)
                    pe.wait_ge(featured, n + 1)
                    wait_from(pe, added, n)
                    nc.tensor.matmul(p_pre[:, 0:w], WE[:, :], eat[s][:, 0:w], start=True, stop=True).then_inc(summed_ea, 1)
                    pe.wait_ge(got_in[s], 128 * k + 128)
                    pe.wait_ge(started, n + 1)
                    for cc in range(C):
                        mm = nc.tensor.transpose(p_turn[:, cc * P:cc * P + p], got[s][0:p, cc, :, :].rearrange("p h f -> p (h f)"), ident[0:p, 0:p])
                    mm.then_inc(turned_got, 1)
                    pe.wait_ge(leaked, n + 1)
                    wait_from(pe, expos, 2 * n)
                    nc.tensor.matmul(p_logit[0:R, 0:w], AT[:, :], act_in[s][:, 0:w], start=True, stop=True).then_inc(scored, 1)

                def back(s, n, k, row, w):
                    p = w // C
                    if last(n):
                        keep_and_take(s, n, None, None, w)
                    pe.wait_ge(summed, n + 1)
                    wait_from(pe, drained, 3 * n)
                    r = run[s][:, 0:w].rearrange("q (p c) -> q p c", c=C)
                    for cc in range(C):
                        mm = nc.tensor.transpose(p_out[0:p, cc * P:(cc + 1) * P], r[:, :, cc], ident[:, :])
                    mm.then_inc(rowed, 1)
                    pe.wait_ge(dens, n + 1)
                    if not last(n):
                        pe.wait_ge(featured, n + 2)
                    pe.sem_inc(passed, 1)
                    for q, t in enumerate((den[s][:, 0:w], top[s][:, 1:1 + w])):
                        r = t.rearrange("q (p c) -> q p c", c=C)
                        for cc in range(C):
                            at = (q * C + cc) * R
                            mm = nc.tensor.transpose(p_small[0:p, at:at + R], r[:, :, cc], ident[0:R, 0:R])
                    mm.then_inc(rowed, 1)

                each_group(pe, front, back)

            @block.scalar
            def _(act):
                def front(s, n, k, row, w):
                    p = w // C
                    def by_slot(bank, q=P):
                        return bank[0:q, :].rearrange("q (c p) -> q p c", c=C)[:, 0:p, :]
                    act.wait_ge(turned_first, n + 1)
                    wait_from(act, owned, n - 1)
                    nc.scalar.activation(starts[s][:, 0:w].rearrange("q (p c) -> q p c", c=C), by_slot(p_turn), ACT.Copy).then_inc(started, 1)
                    act.wait_ge(turned_ea, n + 1)
                    wait_from(act, summed_ea, n - 1)
                    nc.scalar.activation(eat[s][:, 0:w].rearrange("q (p c) -> q p c", c=C), by_slot(p_small, 2 * ED), ACT.Copy).then_inc(featured, 1)
                    act.wait_ge(turned_got, n + 1)
                    wait_from(act, weighted_s, n - 1)
                    nc.scalar.activation(theirs[s][:, 0:w].rearrange("q (p c) -> q p c", c=C), by_slot(p_turn), ACT.Copy).then_inc(gotten, 1)

                def exps(s, n, w):
                    act.wait_ge(expos, 2 * n + 2)
                    wait_from(act, dens, n - 1)
                    nc.scalar.activation(grow[s][:, :, 0:w], expo[s][:, :, 0:w], ACT.Exp).then_inc(grown, 1)

                def back(s, n, k, row, w):
                    p = w // C
                    wait_from(act, stored[s], 32 * k)
                    act.wait_ge(rowed, 2 * n + 1)
                    nc.scalar.activation(rows[s][0:p, :, :, 0:D].rearrange("p h c f -> p c h f"),
                                         p_out[0:p, :].rearrange("p (c h f) -> p c h f", h=2, f=D), ACT.Copy).then_inc(drained, 1)
                    act.wait_ge(rowed, 2 * n + 2)
                    for q in range(2):
                        nc.scalar.activation(rows[s][0:p, :, :, D + q * HEADS:D + (q + 1) * HEADS].rearrange("p h c f -> p c h f"),
                                             p_small[0:p, q * C * R:(q + 1) * C * R].rearrange("p (c h f) -> p c h f", h=2, f=HEADS),
                                             ACT.Copy).then_inc(drained, 1)
                    act.wait_ge(drained, 3 * n + 3)
                    for h in range(2):
                        act.dma_start(by_edge(t3, h, row, w), rows[s][0:p, h, :, :]).then_inc(stored[s], 16)
                    if not last(n):
                        exps(1 - s, n + 1, next_width(n))

                def front_first(s, n, k, row, w):
                    front(s, n, k, row, w)
                    if isinstance(n, int) and n == 0:
                        exps(s, n, w)

                each_group(act, front_first, back)
                for s in range(2):
                    act.wait_ge(stored[s], 32 * ((NG + 2 - s) // 2))

            @block.vector
            def _(dve):
                nc.vector.memset(WE[:, :], 0.0).then_inc(zeroed, 1)
                nc.vector.memset(AT[:, :], 0.0).then_inc(zeroed, 1)

                def attend(s, n, k, row, w):
                    zero = isinstance(n, int) and n == 0
                    dve.wait_ge(marked, n + 1)
                    dve.wait_ge(started, n + 1)
                    wait_from(dve, owned, n)
                    wait_from(dve, twice, n - 1)
                    nc.vector.tensor_tensor_scan(own[s][:, 0:w], p_mk[:, 0:w], starts[s][:, 0:w],
                                                 0.0 if zero else own[1 - s][:, W - 1:W], ALU.mult, ALU.add).then_inc(owned, 1)
                    dve.wait_ge(owned, n + 1)
                    dve.wait_ge(gotten, n + 1)
                    wait_from(dve, added, n - 1)
                    nc.vector.tensor_tensor(both[s][:, 0:w], own[s][:, 0:w], theirs[s][:, 0:w], ALU.add).then_inc(twice, 1)
                    dve.wait_ge(twice, n + 1)
                    dve.wait_ge(summed_ea, n + 1)
                    wait_from(dve, leaked, n - 1)
                    nc.vector.tensor_tensor(pre[s][:, 0:w], both[s][:, 0:w], p_pre[:, 0:w], ALU.add).then_inc(added, 1)
                    dve.wait_ge(added, n + 1)
                    wait_from(dve, scored, n - 1)
                    nc.vector.scalar_tensor_tensor(out=act_in[s][:, 0:w], in0=pre[s][:, 0:w], scalar=0.2, in1=pre[s][:, 0:w],
                                                   op0=ALU.mult, op1=ALU.max).then_inc(leaked, 1)

                def exponents(s, n, k, w):
                    wait_from(dve, rowed, 2 * n - 2)
                    if isinstance(n, int) and n == 0:
                        nc.vector.memset(top[s][:, 0:1], NEG).then_inc(carried, 1)
                    else:
                        dve.wait_ge(maxed, n)
                        nc.vector.tensor_copy(top[s][:, 0:1], top[1 - s][:, W:W + 1]).then_inc(carried, 1)
                    dve.wait_ge(carried, n + 1)
                    dve.wait_ge(scored, n + 1)
                    dve.wait_ge(first_in[s], 112 * k + 112)
                    nc.vector.tensor_tensor_scan(top[s][:, 1:1 + w], reset[s][:, 0:w], p_logit[0:R, 0:w], top[s][:, 0:1], ALU.add, ALU.max).then_inc(maxed, 1)
                    dve.wait_ge(maxed, n + 1)
                    wait_from(dve, expos, 2 * n - 2)
                    nc.vector.tensor_tensor(left[s][:, 0:w], top[s][:, 0:w], reset[s][:, 0:w], ALU.add).then_inc(lefts, 1)
                    dve.wait_ge(lefts, n + 1)
                    wait_from(dve, grown, n - 1)
                    nc.vector.tensor_tensor(expo[s][:, 0, 0:w], left[s][:, 0:w], top[s][:, 1:1 + w], ALU.subtract).then_inc(expos, 1)
                    nc.vector.scalar_tensor_tensor(out=expo[s][:, 1, 0:w], in0=top[s][:, 1:1 + w], scalar=-1.0, in1=p_logit[0:R, 0:w],
                                                   op0=ALU.mult, op1=ALU.add).then_inc(expos, 1)

                def front(s, n, k, row, w):
                    attend(s, n, k, row, w)
                    if isinstance(n, int) and n == 0:
                        exponents(s, n, k, w)

                def back(s, n, k, row, w):
                    zero = isinstance(n, int) and n == 0
                    dve.wait_ge(taken, n + 1)
                    wait_from(dve, summed, n - 1)
                    nc.vector.tensor_tensor(weighted[s][:, 0:w], theirs[s][:, 0:w], p_take[:, 0:w], ALU.mult).then_inc(weighted_s, 1)
                    dve.wait_ge(weighted_s, n + 1)
                    dve.wait_ge(kept, n + 1)
                    wait_from(dve, rowed, 2 * n - 2)
                    wait_from(dve, summed, n)
                    nc.vector.tensor_tensor_scan(run[s][:, 0:w], p_keep[:, 0:w], weighted[s][:, 0:w],
                                                 0.0 if zero else run[1 - s][:, W - 1:W], ALU.mult, ALU.add).then_inc(summed, 1)
                    dve.wait_ge(grown, n + 1)
                    wait_from(dve, dens, n)
                    nc.vector.tensor_tensor_scan(den[s][:, 0:w], grow[s][:, 0, 0:w], grow[s][:, 1, 0:w],
                                                 0.0 if zero else den[1 - s][:, W - 1:W], ALU.mult, ALU.add).then_inc(dens, 1)
                    if not last(n):
                        exponents(1 - s, n + 1, k + s, next_width(n))

                each_group(dve, front, back)


def finish_4(nc, sb, ps, sem, X, info, t3, valid, bias3, g3, be3, out):
    with Stage(nc) as c:
        rows = sb(c, "rows", [P, NJ, T3])
        carry = sb(c, "carry", [P, T3])
        Y, Z = sb(c, "Y", [P, NJ, D]), sb(c, "Z", [P, NJ, D])
        BI, GA, BE = (sb(c, n, [P, D]) for n in ("BI", "GA", "BE"))
        inv = sb(c, "inv", [P, NJ])
        theirs, mx, dif, fac, scaled, denom, rden = (sb(c, n, [P, NJ, HEADS]) for n in ("theirs", "mx", "dif", "fac", "scaled", "denom", "rden"))
        dif2, fac2 = sb(c, "dif2", [P, NJ, HEADS]), sb(c, "fac2", [P, NJ, HEADS])
        part, mean, var, sd, rs = (sb(c, n, [P, D]) for n in ("part", "mean", "var", "sd", "rs"))
        ones = sb(c, "ones", [P, P])
        tot = ps(c, "tot", [P, 2 * D])
        cleared, rows_in, small_in, chain, fed, exped, totals, rooted = (
            sem(c, n) for n in ("cleared", "rows_in", "small_in", "chain", "fed", "exped", "totals", "rooted"))
        with nc.Block() as block:
            @block.sync
            def _(sp):
                sp.dma_start(carry[:, :], t3[H - 1:H, :].to_broadcast((P, T3))).then_inc(small_in, 16)
                for t, w in ((BI, bias3), (GA, g3), (BE, be3)):
                    sp.dma_start(t[:, :], row_of(w)).then_inc(small_in, 16)

            @block.gpsimd
            def _(pool):
                pool.wait_ge(cleared, 1)
                gather_rows(pool, nc, rows, T3, t3, info["last"], rows_in)

            @block.vector
            def _(dve):
                count = [0]

                def link(ins):
                    count[0] += 1
                    ins.then_inc(chain, 1)
                    dve.wait_ge(chain, count[0])

                def heads(t):
                    return t.unsqueeze(1).to_broadcast((P, NJ, HEADS))

                def spread_out(t):
                    return t[:, :, :].unsqueeze(3).to_broadcast((P, NJ, HEADS, HC))

                def split(t):
                    return t.rearrange("p j (a f) -> p j a f", a=HEADS)

                nc.vector.memset(rows[:, :, :], 0.0).then_inc(cleared, 1)
                link(nc.vector.memset(ones[:, :], 1.0))
                dve.wait_ge(rows_in, 16 * NJ)
                dve.wait_ge(small_in, 64)
                span = per_node(info["span"], HEADS)
                cmax = carry[:, D + HEADS:T3]
                link(nc.vector.tensor_scalar(inv[:, :], info["span"][:, :], -1.0, -NEG, ALU.add, ALU.mult))
                link(nc.vector.tensor_tensor(theirs[:, :, :], span, heads(cmax), ALU.mult))
                link(nc.vector.tensor_tensor(theirs[:, :, :], theirs[:, :, :], per_node(inv, HEADS), ALU.add))
                link(nc.vector.tensor_tensor(mx[:, :, :], theirs[:, :, :], rows[:, :, D + HEADS:T3], ALU.max))
                link(nc.vector.tensor_tensor(dif[:, :, :], rows[:, :, D + HEADS:T3], mx[:, :, :], ALU.subtract))
                link(nc.vector.tensor_tensor(dif2[:, :, :], theirs[:, :, :], mx[:, :, :], ALU.subtract))
                nc.vector.tensor_copy(inv[:, 0:1], info["span"][:, 0:1]).then_inc(fed, 1)
                dve.wait_ge(exped, 2)
                link(nc.vector.tensor_tensor(denom[:, :, :], rows[:, :, D:D + HEADS], fac[:, :, :], ALU.mult))
                link(nc.vector.tensor_tensor(scaled[:, :, :], fac2[:, :, :], heads(carry[:, D:D + HEADS]), ALU.mult))
                link(nc.vector.tensor_tensor(denom[:, :, :], denom[:, :, :], scaled[:, :, :], ALU.add))
                link(nc.vector.tensor_scalar(denom[:, :, :], denom[:, :, :], 1e-16, None, ALU.add))
                link(nc.vector.reciprocal(rden[:, :, :], denom[:, :, :]))
                link(nc.vector.tensor_tensor(split(Y[:, :, :]), split(rows[:, :, 0:D]), spread_out(fac), ALU.mult))
                link(nc.vector.tensor_tensor(split(Z[:, :, :]), carry[:, 0:D].unsqueeze(1).to_broadcast((P, NJ, D)).rearrange("p j (a f) -> p j a f", a=HEADS),
                                             spread_out(fac2), ALU.mult))
                link(nc.vector.tensor_tensor(Y[:, :, :], Y[:, :, :], Z[:, :, :], ALU.add))
                link(nc.vector.tensor_tensor(split(Z[:, :, :]), split(Y[:, :, :]), spread_out(rden), ALU.mult))
                link(nc.vector.tensor_tensor(Y[:, :, :], Z[:, :, :], per_feature(BI), ALU.add))

                def total(t, n):
                    link(nc.vector.tensor_reduce(part[:, :], t[:, :, :].rearrange("p j f -> p f j"), AX.X, ALU.add))
                    nc.vector.tensor_copy(inv[:, 1:2], info["span"][:, 1:2]).then_inc(fed, 1)
                    dve.wait_ge(totals, n)

                link(nc.vector.tensor_tensor(Z[:, :, :], Y[:, :, :], per_node(valid), ALU.mult))
                total(Z, 1)
                link(nc.vector.tensor_scalar(mean[:, :], tot[:, 0:D], 1.0 / N, None, ALU.mult))
                link(nc.vector.tensor_tensor(Y[:, :, :], Y[:, :, :], per_feature(mean), ALU.subtract))
                link(nc.vector.tensor_tensor(Z[:, :, :], Y[:, :, :], per_node(valid), ALU.mult))
                link(nc.vector.tensor_tensor(Z[:, :, :], Z[:, :, :], Y[:, :, :], ALU.mult))
                total(Z, 2)
                link(nc.vector.tensor_scalar(var[:, :], tot[:, D:2 * D], 1.0 / N, EPS, ALU.mult, ALU.add))
                nc.vector.tensor_copy(inv[:, 2:3], info["span"][:, 2:3]).then_inc(fed, 1)
                dve.wait_ge(rooted, 1)
                link(nc.vector.reciprocal(rs[:, :], sd[:, :]))
                link(nc.vector.tensor_tensor(rs[:, :], rs[:, :], GA[:, :], ALU.mult))
                link(nc.vector.tensor_tensor(Y[:, :, :], Y[:, :, :], per_feature(rs), ALU.mult))
                link(nc.vector.tensor_tensor(Y[:, :, :], Y[:, :, :], per_feature(BE), ALU.add))
                link(nc.vector.tensor_tensor(Z[:, :, :], Y[:, :, :], X[:, :, :], ALU.add))
                nc.vector.tensor_copy(inv[:, 3:4], info["span"][:, 3:4]).then_inc(fed, 1)
                dve.wait_ge(rooted, 2)
                link(nc.vector.tensor_tensor(Z[:, :, :], Y[:, :, :], X[:, :, :], ALU.add))

            @block.tensor
            def _(pe):
                for n in range(2):
                    pe.wait_ge(fed, 2 + n)
                    nc.tensor.matmul(tot[:, n * D:(n + 1) * D], ones[:, :], part[:, :], start=True, stop=True).then_inc(totals, 1)

            @block.scalar
            def _(act):
                act.wait_ge(fed, 1)
                nc.scalar.activation(fac[:, :, :], dif[:, :, :], ACT.Exp).then_inc(exped, 1)
                nc.scalar.activation(fac2[:, :, :], dif2[:, :, :], ACT.Exp).then_inc(exped, 1)
                act.wait_ge(fed, 4)
                nc.scalar.activation(sd[:, :], var[:, :], ACT.Sqrt).then_inc(rooted, 1)
                act.wait_ge(fed, 5)
                nc.scalar.activation(Y[:, :, :], Z[:, :, :], ACT.Gelu).then_inc(rooted, 1)

        norm(nc, sb, sem, [], Z, Y, [])
        written = sem(c, "written")
        with nc.Block() as block:
            @block.sync
            def _(sp):
                for s, j, rows_out in node_rows(out):
                    sp.dma_start(rows_out, Y[s, 0:j, :]).then_inc(written, 16)
                sp.wait_ge(written, 48)


_INS = {"x": "x", "src": "src", "dst": "dst", "ea16": "edge_attr_16", "ea64": "edge_attr_64", "ew": "edge_weight1",
        "w0a": "L0_gnn_W1", "b0a": "L0_gnn_b1", "w0b": "L0_gnn_W2", "b0b": "L0_gnn_b2",
        "u1": "L1_gnn_u", "w1a": "L1_gnn_W1", "b1a": "L1_gnn_b1", "w1b": "L1_gnn_W2", "b1b": "L1_gnn_b2",
        "g1": "L1_gnn_gamma", "be1": "L1_gnn_beta",
        "w2a": "L2_gnn_W1", "b2a": "L2_gnn_b1", "w2b": "L2_gnn_W2", "b2b": "L2_gnn_b2", "w2g": "L2_gnn_Wg", "b2g": "L2_gnn_bg",
        "wl": "L3_gnn_W_l", "bl": "L3_gnn_b_l", "wr": "L3_gnn_W_r", "br": "L3_gnn_b_r", "we": "L3_gnn_W_e",
        "att": "L3_gnn_att", "bias3": "L3_gnn_bias", "g3": "L3_gnn_gamma", "be3": "L3_gnn_beta"}


def kernel(**inputs):
    import numpy as _np
    import concourse.bacc as _bacc
    from concourse import mybir as _mybir
    from concourse.bass_utils import run_bass_kernel_spmd as _run

    nc = _bacc.Bacc("TRN2", target_bir_lowering=False, num_devices=1)
    arrays, args = {}, {}
    for name, given in _INS.items():
        a = _np.ascontiguousarray(inputs[given])
        if name in ("src", "dst"):
            a = a.reshape(-1, 1)
        arrays[f"in_{name}_dram"] = a
        args[name] = nc.dram_tensor(f"in_{name}_dram", a.shape, _mybir.dt.from_np(a.dtype), kind="ExternalInput").ap()
    args["out"] = nc.dram_tensor("out_0_dram", (N, D), F32, kind="ExternalOutput").ap()
    build(nc, **args)
    r = _run(nc, [arrays], core_ids=[0])
    return r.results[0]["out_0_dram"]
```

```python
import itertools
import numpy as np
import concourse.bass as bass
from concourse import mybir
from contextlib import ExitStack

F32 = mybir.dt.float32
I32 = mybir.dt.int32
BF16 = mybir.dt.bfloat16
ALU = mybir.AluOpType
ACT = mybir.ActivationFunctionType
AX = mybir.AxisListType
ds = bass.ds

P = 128
N = 6250
E = 200000
D = 64
H = E // 2
NJ = -(-N // P)
NP = P * NJ
FULLP, LASTJ = N // NJ, N % NJ
W = 512
C = 4
NG = H // W
TAIL = H - NG * W
AHEAD = 4
LAG = 3
UNROLL = 4
FIRST = NG - (NG - LAG - AHEAD) // UNROLL * UNROLL
SR, SC = 64, E // 64
KR, KC, KT = 1600, 125, 40
NONE = 1 << 20
NEG = -2.0 ** 126
EPS = 1e-5
HEADS, HC, ED = 4, 16, 16
LOGN = 18
SF = (1 << LOGN) // P
SB = 13
KEYBASE = 1 << 29
T3 = 72


class Stage(ExitStack):

    def __init__(self, nc):
        super().__init__()
        self.nc, self.sems = nc, []

    def __exit__(self, *what):
        if self.sems and what[0] is None:
            self.nc.clear_and_free_semaphores(self.sems)
            self.nc.all_engine_barrier()
        return super().__exit__(*what)


class Group:

    def __init__(self, it, base):
        self.it, self.base = it, base
        self.n = base if it is None else it * UNROLL + base
        self.row = self.n * W
        self.w = TAIL if it is None and base == NG else W
        self.p = self.w // C
        self.zero = it is None and base == 0
        self.late = it is None and base + LAG > NG

    def slot(self, slots):
        return self.base % slots

    def turn(self, slots):
        return self.base // slots if self.it is None else self.it * (UNROLL // slots) + self.base // slots


def each_group(eng, *steps):
    behind = max(lag for lag, _ in steps)
    for t in range(FIRST):
        for lag, step in steps:
            if t >= lag:
                step(Group(None, t - lag))
    with eng.Fori(0, (NG - FIRST) // UNROLL) as i:
        it = eng.snap(i)
        for t in range(FIRST, FIRST + UNROLL):
            for lag, step in steps:
                step(Group(it, t - lag))
    for t in range(NG, NG + 1 + behind):
        for lag, step in steps:
            if t - lag <= NG:
                step(Group(None, t - lag))


def wait_from(eng, sem, value):
    if not isinstance(value, int) or value > 0:
        eng.wait_ge(sem, value)


def snapped(eng, value):
    return value if isinstance(value, int) else eng.snap(value)


def by_edge(table, h, row, width):
    half = table[h * H:(h + 1) * H, :][ds(row, width), :]
    return half.rearrange("(p c) f -> p c f", c=C)


def both_halves(table, row, width):
    rows = table.rearrange("(h r) f -> r h f", h=2)[ds(row, width), :, :]
    return rows.rearrange("(p c) h f -> p h c f", c=C)


def indices_of(table, row, width):
    return table.rearrange("(h r) o -> r (h o)", h=2)[ds(row, width), :].rearrange("(p c) h -> p h c", c=C)


def by_place(t, g):
    return t[:, 0:g.w].rearrange("q (p c) -> q p c", c=C)


def by_block(bank, g, q=P):
    return bank[0:q, :].rearrange("q (c p) -> q p c", c=C)[:, 0:g.p, :]


def turn_to_features(nc, bank, by_edges, g, ident, q=P):
    for cc in range(C):
        mm = nc.tensor.transpose(bank[0:q, cc * P:cc * P + g.p], by_edges[0:g.p, cc, :, :].rearrange("p h f -> p (h f)"), ident[0:g.p, 0:g.p])
    return mm


def turn_to_edges(nc, bank, t, g, ident):
    for cc in range(C):
        mm = nc.tensor.transpose(bank[0:g.p, cc, :], by_place(t, g)[:, :, cc], ident[:, :])
    return mm


def build(nc, x, src, dst, ea16, ea64, ew, w0a, b0a, w0b, b0b, u1, w1a, b1a, w1b, b1b, g1, be1,
          w2a, b2a, w2b, b2b, w2g, b2g, wl, bl, wr, br, we, att, bias3, g3, be3, out):
    ctx = ExitStack()
    with ctx:
        def dram(name, shape, dt):
            return nc.dram_tensor(name, shape, dt, kind="Internal").ap()

        t1 = dram("t1", [E, 2 * D], F32)
        t2 = dram("t2", [E, D], F32)
        t3 = dram("t3", [E, T3], F32)
        start2 = dram("start2", [E, D], F32)
        start3 = dram("start3", [E, D], F32)
        wsum = dram("wsum", [E, 1], F32)
        srcs = dram("srcs", [E, 1], I32)
        dsts = dram("dsts", [E, 1], I32)
        rowlast = [dram(f"rowlast{o}", [KT, KT], I32) for o in range(2)]
        marks = dram("marks", [2, 2, 2, H], BF16)
        tabg = [dram(f"tabg{i}", [NP, D], F32) for i in range(2)]
        tabs = [dram(f"tabs{i}", [NP, D], F32) for i in range(2)]

        serial = itertools.count()

        def sb(c, name, shape, dt=F32):
            return c.enter_context(nc.sbuf_tensor(f"{name}_{next(serial)}", shape, dt))

        def ps(c, name, shape, dt=F32):
            return c.enter_context(nc.psum_tensor(f"{name}_{next(serial)}", shape, dt))

        def sem(c, name):
            c.sems.append(nc.alloc_semaphore(f"{name}_{next(serial)}"))
            return c.sems[-1]

        X = sb(ctx, "X", [P, NJ, D])
        ident = sb(ctx, "ident", [P, P])
        nid = sb(ctx, "nid", [P, NJ])
        valid = sb(ctx, "valid", [P, NJ])
        sel2 = sb(ctx, "sel2", [2, P], BF16)
        order = [{k: sb(ctx, f"{k}{o}", [P, NJ], dt) for k, dt in
                  (("first", I32), ("last", I32), ("span", F32), ("cnt", F32))} for o in range(2)]

        ident_of[0] = ident
        keys = [dst, srcs]
        setup_and_sort(nc, sb, ps, sem, x, src, dst, X, ident, nid, valid, sel2, start2, start3, srcs, dsts)
        for o in range(2):
            runs_of(nc, sb, ps, sem, o, keys[o], order[o], nid, rowlast, marks, ident, ew, wsum)
        edge_sums(nc, sb, ps, sem, ea64, marks, t1, ident, sel2)
        node_layers_1_2(nc, sb, ps, sem, X, order[0], t1, wsum, ident, w0a, b0a, w0b, b0b, u1, w1a, b1a,
                        w1b, b1b, g1, be1)
        node_tables(nc, sb, ps, sem, 0, X, order[1], srcs, (w2a[D:2 * D, :], b2a), (w2a[0:D, :], None),
                    tabg[0], tabs[0], start2, ident)
        edges_3(nc, sb, ps, sem, dsts, marks, tabg[0], start2, t2, ident, sel2, w2b, b2b, w2g, b2g)
        pool_3(nc, sb, ps, sem, X, order[1], t2)
        node_tables(nc, sb, ps, sem, 1, X, order[0], dst, (wl, bl), (wr, br), tabg[1], tabs[1], start3, ident)
        edges_4(nc, sb, ps, sem, src, ea16, marks, tabg[1], start3, t3, ident, sel2, we, att)
        finish_4(nc, sb, ps, sem, X, order[0], t3, valid, bias3, g3, be3, out)


def node_rows(flat):
    cut = FULLP // 16 * 16
    for a, b in ((0, cut), (cut, FULLP)):
        yield slice(a, b), NJ, flat[a * NJ:b * NJ, :].rearrange("(p j) f -> p j f", j=NJ)
    yield slice(FULLP, FULLP + 1), LASTJ, flat[FULLP * NJ:N, :].rearrange("(p j) f -> p j f", j=LASTJ)



ROW = LOGN - 7


def network():
    for k in range(1, LOGN + 1):
        if k >= ROW:
            yield "sign", k
        if k > ROW:
            yield "turn", k
            for j in range(k - 1, ROW - 1, -1):
                yield "step", k, j - ROW
            yield "turn", k
        for j in range(min(k, ROW) - 1, -1, -1):
            yield "step", k, j


def ops_before_turns():
    n, out = 2, []
    for what in network():
        if what[0] == "turn":
            out.append(n)
        else:
            n += 1 if what[0] == "sign" else (4 if what[1] < ROW else 2)
    return out


def setup_and_sort(nc, sb, ps, sem, x, src, dst, X, ident, nid, valid, sel2, start2, start3, srcs, dsts):
    FULL, REST = E // SF, E % SF
    CUT = FULL // 16 * 16
    ZC = 4000
    TURNS = ops_before_turns()
    with Stage(nc) as c:
        zeros = sb(c, "zeros", [P, ZC])
        nodei = sb(c, "nodei", [P, NJ], I32)
        parti = sb(c, "parti", [P, 1], I32)
        bits = sb(c, "bits", [P, LOGN - ROW + 2], I32)
        sign = sb(c, "sign", [P, LOGN - ROW + 2])
        flip = sb(c, "flip", [P, LOGN - ROW + 1])
        ones2, sel2f, sel2g = (sb(c, n, [2, P]) for n in ("ones2", "sel2f", "sel2g"))
        zerop = sb(c, "zerop", [P, P])
        si, di = (sb(c, n, [P, SF], I32) for n in ("si", "di"))
        ka, kb = (sb(c, n, [P, SF]) for n in ("ka", "kb"))
        pt = ps(c, "pt", [P, SF])

        made, consts = sem(c, "made"), sem(c, "consts")
        cleared, nodes_in, zeroed, pairs_in = (sem(c, n) for n in ("cleared", "nodes_in", "zeroed", "pairs_in"))
        step, turned, back, split, sorted_out = (sem(c, n) for n in ("step", "turned", "back", "split", "sorted_out"))
        with nc.Block() as block:
            @block.sync
            def _(sp):
                sp.wait_ge(cleared, 2)
                for t, k in ((si, src), (di, dst)):
                    for a, b in ((0, CUT), (CUT, FULL)):
                        sp.dma_start(t[a:b, :], k[a * SF:b * SF, :].rearrange("(p f) o -> p (f o)", f=SF)).then_inc(pairs_in, 16)
                    sp.dma_start(t[FULL:FULL + 1, 0:REST], k[FULL * SF:E, :].rearrange("(p f) o -> p (f o)", p=1)).then_inc(pairs_in, 16)
                sp.wait_ge(cleared, 4)
                for s, j, rows in node_rows(x):
                    sp.dma_start(X[s, 0:j, :], rows).then_inc(nodes_in, 16)
                for t in (start2, start3):
                    flat = t.rearrange("r f -> (r f)").rearrange("(p n) -> p n", p=P)
                    for k in range(E * D // P // ZC):
                        sp.dma_start(flat[:, k * ZC:(k + 1) * ZC], zeros[:, :]).then_inc(zeroed, 16)
                sp.wait_ge(split, 2)
                for t, k in ((si, srcs), (di, dsts)):
                    for a, b in ((0, CUT), (CUT, FULL)):
                        sp.dma_start(k[a * SF:b * SF, :].rearrange("(p f) o -> p (f o)", f=SF), t[a:b, :]).then_inc(sorted_out, 16)
                    sp.dma_start(k[FULL * SF:E, :].rearrange("(p f) o -> p (f o)", p=1), t[FULL:FULL + 1, 0:REST]).then_inc(sorted_out, 16)
                sp.wait_ge(sorted_out, 96)
                sp.wait_ge(nodes_in, 48)
                sp.wait_ge(zeroed, 16 * 2 * (E * D // P // ZC))

            @block.gpsimd
            def _(pool):
                nc.gpsimd.memset(zerop[:, :], 0.0).then_inc(made, 1)
                nc.gpsimd.memset(ones2[:, :], 1.0).then_inc(made, 1)
                nc.gpsimd.iota(nodei[:, :], pattern=[[1, NJ]], base=0, channel_multiplier=NJ).then_inc(made, 1)
                nc.gpsimd.iota(parti[:, :], pattern=[[0, 1]], base=0, channel_multiplier=1).then_inc(made, 1)
                pool.wait_ge(made, 4)
                nc.gpsimd.affine_select(out=ident[:, :], in_=zerop[:, :], compare_op=ALU.not_equal, fill=1.0, base=0,
                                        pattern=[[-1, P]], channel_multiplier=1).then_inc(made, 1)
                nc.gpsimd.affine_select(out=sel2g[:, :], in_=ones2[:, :], compare_op=ALU.is_ge, fill=0.0, base=0,
                                        pattern=[[1, P]], channel_multiplier=-D).then_inc(made, 1)
                pool.wait_ge(made, 6)
                nc.gpsimd.affine_select(out=sel2f[:, :], in_=sel2g[:, :], compare_op=ALU.is_ge, fill=0.0, base=D - 1,
                                        pattern=[[-1, P]], channel_multiplier=D).then_inc(made, 1)

            @block.vector
            def _(dve):
                nc.vector.memset(si[:, :], (1 << SB) - 1).then_inc(cleared, 1)
                nc.vector.memset(di[:, :], (1 << SB) - 1).then_inc(cleared, 1)
                nc.vector.memset(zeros[:, :], 0.0).then_inc(cleared, 1)
                nc.vector.memset(X[:, :, :], 0.0).then_inc(cleared, 1)
                nc.vector.memset(bits[:, :], 0).then_inc(consts, 1)
                dve.wait_ge(made, 7)
                nc.vector.tensor_copy(sel2[:, :], sel2f[:, :]).then_inc(consts, 1)
                nc.vector.tensor_copy(nid[:, :], nodei[:, :]).then_inc(consts, 1)
                dve.wait_ge(consts, 3)
                nc.vector.tensor_scalar(valid[:, :], nid[:, :], float(N), None, ALU.is_lt).then_inc(consts, 1)
                for k in range(ROW, LOGN):
                    at = k - ROW + 1
                    nc.vector.tensor_scalar(bits[:, at:at + 1], parti[:, :], k - ROW, 1, ALU.logical_shift_right,
                                            ALU.bitwise_and).then_inc(consts, 1)
                dve.wait_ge(consts, 4 + LOGN - ROW)
                nc.vector.tensor_scalar(sign[:, :], bits[:, :], -2.0, 1.0, ALU.mult, ALU.add).then_inc(consts, 1)
                dve.wait_ge(consts, 5 + LOGN - ROW)
                nc.vector.tensor_tensor(flip[:, :], sign[:, 0:LOGN - ROW + 1], sign[:, 1:LOGN - ROW + 2], ALU.mult).then_inc(consts, 1)
                dve.wait_ge(consts, 6 + LOGN - ROW)
                dve.wait_ge(pairs_in, 96)
                done = 0
                nc.vector.tensor_scalar(ka[:, :].bitcast(I32), si[:, :], SB, KEYBASE, ALU.logical_shift_left,
                                        ALU.bitwise_or).then_inc(step, 1)
                dve.wait_ge(step, 1)
                nc.vector.tensor_tensor(kb[:, :].bitcast(I32), ka[:, :].bitcast(I32), di[:, :], ALU.bitwise_or).then_inc(step, 1)
                done = 2
                now, then, turns = kb, ka, 0
                for what in network():
                    if what[0] == "turn":
                        turns += 1
                        now, then = then, now
                        dve.wait_ge(back, 4 * turns)
                        continue
                    dve.wait_ge(step, done)
                    if what[0] == "sign":
                        at = what[1] - ROW
                        nc.vector.tensor_scalar(then[:, :], now[:, :], flip[:, at:at + 1], None, ALU.mult).then_inc(step, 1)
                        done += 1
                    elif what[1] < ROW:
                        k, i = what[1:]
                        a, b = (z[:, :].rearrange("p (n d s l i) -> p n d s l i", d=2, s=1 << (k - i - 1), l=2, i=1 << i) for z in (now, then))
                        for d, (low, high) in enumerate(((ALU.min, ALU.max), (ALU.max, ALU.min))):
                            for side, op in ((0, low), (1, high)):
                                nc.vector.tensor_tensor(b[:, :, d, :, side, :], a[:, :, d, :, 0, :], a[:, :, d, :, 1, :], op).then_inc(step, 1)
                        done += 4
                    else:
                        a, b = (z[:, :].rearrange("p (n l i) -> p n l i", l=2, i=1 << what[2]) for z in (now, then))
                        for side, op in ((0, ALU.min), (1, ALU.max)):
                            nc.vector.tensor_tensor(b[:, :, side, :], a[:, :, 0, :], a[:, :, 1, :], op).then_inc(step, 1)
                        done += 2
                    now, then = then, now
                dve.wait_ge(step, done)
                ki = now[:, :].bitcast(I32)
                nc.vector.tensor_scalar(si[:, :], ki, SB, (1 << SB) - 1, ALU.logical_shift_right, ALU.bitwise_and).then_inc(split, 1)
                nc.vector.tensor_scalar(di[:, :], ki, (1 << SB) - 1, None, ALU.bitwise_and).then_inc(split, 1)

            def keys_at(turn):
                ops = 0
                for what in network():
                    if what[0] == "turn":
                        if turn == 0:
                            break
                        turn -= 1
                    ops += 1
                return (kb, ka) if ops % 2 == 0 else (ka, kb)

            @block.tensor
            def _(pe):
                pe.wait_ge(made, 7)
                for t, ops in enumerate(TURNS):
                    pe.wait_ge(step, ops)
                    if t:
                        pe.wait_ge(back, 4 * t)
                    now, _ = keys_at(t)
                    for q in range(SF // P):
                        last = nc.tensor.transpose(pt[:, q * P:(q + 1) * P], now[:, q * P:(q + 1) * P], ident[:, :])
                        if q % 4 == 3:
                            last.then_inc(turned, 1)

            @block.scalar
            def _(act):
                for t in range(len(TURNS)):
                    _, then = keys_at(t)
                    for q in range(4):
                        act.wait_ge(turned, 4 * t + q + 1)
                        nc.scalar.activation(then[:, q * 512:(q + 1) * 512], pt[:, q * 512:(q + 1) * 512], ACT.Copy).then_inc(back, 1)


def runs_of(nc, sb, ps, sem, o, key, info, nid, rowlast, marks, ident, ew, wsum):
    with Stage(nc) as c:
        top = sb(c, "top", [P, KT], I32)
        low = sb(c, "low", [KT, KT], I32)
        rows1 = sb(c, "rows1", [P, NJ, KT], I32)
        rows2 = sb(c, "rows2", [P, NJ, KC], I32)
        hits = sb(c, "hits", [P, NJ, KC])
        below1, below2, below3, row, upto, before = (sb(c, n, [P, NJ]) for n in ("below1", "below2", "below3", "row", "upto", "before"))
        index1, index2 = (sb(c, n, [P, NJ], I32) for n in ("index1", "index2"))
        has, f1, f2, f3, l1, l2, l3, s1, s2 = (sb(c, n, [P, NJ]) for n in ("has", "f1", "f2", "f3", "l1", "l2", "l3", "s1", "s2"))
        edge = sb(c, "edge", [SR, SC + 1], I32)
        mark = sb(c, "mark", [SR, SC])
        mark16 = sb(c, "mark16", [SR, SC], BF16)
        reset16 = sb(c, "reset16", [SR, SC], BF16)
        wt, wrun, wprod, wall = (sb(c, n, [SR, SC]) for n in ("wt", "wrun", "wprod", "wall"))
        crow = sb(c, "crow", [1, 2 * SR])
        cscan = sb(c, "cscan", [1, SR + 1])
        ccol = sb(c, "ccol", [SR, 1])
        pe1 = ps(c, "pe1", [1, 2 * SR])
        pe2 = ps(c, "pe2", [SR, 1])
        got, lows, prefill, gat1, gat2, chain, v = (sem(c, n) for n in ("got", "lows", "prefill", "gat1", "gat2", "chain", "v"))
        edges_in, marked, marks_out, shifted, w_in, carries, cback, cturn, w_out = (
            sem(c, n) for n in ("edges_in", "marked", "marks_out", "shifted", "w_in", "carries", "cback", "cturn", "w_out"))
        flat = key.rearrange("e o -> (e o)")
        with nc.Block() as block:
            @block.sync
            def _(sp):
                block_last = flat.rearrange("(q s) -> q s", s=KT * KC)[:, KT * KC - 1:KT * KC].rearrange("q o -> o q")
                with nc.allow_non_contiguous_dma(reason="the last key of each block"):
                    sp.dma_start(top[:, :], block_last.to_broadcast((P, KT))).then_inc(got, 16)
                    sp.dma_start(low[:, :], flat.rearrange("(q r s) -> q r s", r=KT, s=KC)[:, :, KC - 1]).then_inc(lows, 16)
                sp.dma_start(edge[:, 1:SC + 1], flat.rearrange("(p f) -> p f", f=SC)).then_inc(edges_in, 16)
                with nc.allow_non_contiguous_dma(reason="one key of each row"):
                    sp.dma_start(edge[1:SR, 0:1], flat.rearrange("(p f) -> p f", f=SC)[0:SR - 1, SC - 1:SC]).then_inc(edges_in, 16)
                if not o:
                    sp.dma_start(wt[:, :], ew.rearrange("(p f) o -> p (f o)", f=SC)).then_inc(w_in, 16)
                sp.wait_ge(lows, 16)
                sp.dma_start(rowlast[o], low[:, :]).then_inc(lows, 16)
                sp.wait_ge(marked, 2)
                for h in range(2):
                    for kind, t in enumerate((mark16, reset16)):
                        sp.dma_start(marks[o, h, kind].rearrange("(p f) -> p f", f=SC), t[h * SR // 2:(h + 1) * SR // 2, :]).then_inc(marks_out, 16)
                if not o:
                    sp.wait_ge(chain, 5)
                    sp.dma_start(wsum.rearrange("(p f) o -> p (f o)", f=SC), wall[:, :]).then_inc(w_out, 16)
                    sp.wait_ge(w_out, 16)
                sp.wait_ge(v, 8)
                with nc.allow_non_contiguous_dma(reason="one count of each partition"):
                    sp.dma_start(before[1:P, 0:1], upto[0:P - 1, NJ - 1:NJ]).then_inc(shifted, 16)
                sp.wait_ge(shifted, 16)
                sp.wait_ge(marks_out, 64)

            @block.gpsimd
            def _(pool):
                nc.gpsimd.memset(rows1[:, :, :], NONE).then_inc(prefill, 1)
                nc.gpsimd.memset(rows2[:, :, :], NONE).then_inc(prefill, 1)
                pool.wait_ge(prefill, 2)
                pool.wait_ge(lows, 32)
                pool.wait_ge(v, 3)
                for j in range(NJ):
                    nc.gpsimd.indirect_dma_start(rows1[:, j, :], None, rowlast[o], bass.IndirectOffsetOnAxis(ap=index1[:, j:j + 1], axis=0),
                                                 bounds_check=KT - 1, oob_is_err=False).then_inc(gat1, 16)
                pool.wait_ge(v, 6)
                for j in range(NJ):
                    nc.gpsimd.indirect_dma_start(rows2[:, j, :], None, key.rearrange("(r s) o -> r (s o)", s=KC),
                                                 bass.IndirectOffsetOnAxis(ap=index2[:, j:j + 1], axis=0),
                                                 bounds_check=KR - 1, oob_is_err=False).then_inc(gat2, 16)

            @block.vector
            def _(dve):
                def node(width):
                    return nid[:, :].unsqueeze(2).to_broadcast((P, NJ, width))

                dve.wait_ge(got, 16)
                nc.vector.tensor_tensor(hits[:, :, 0:KT], top[:, :].unsqueeze(1).to_broadcast((P, NJ, KT)), node(KT), ALU.is_le).then_inc(v, 1)
                dve.wait_ge(v, 1)
                nc.vector.tensor_reduce(below1[:, :], hits[:, :, 0:KT], AX.X, ALU.add).then_inc(v, 1)
                dve.wait_ge(v, 2)
                nc.vector.tensor_copy(index1[:, :], below1[:, :]).then_inc(v, 1)
                nc.vector.memset(edge[0:1, 0:1], -1).then_inc(chain, 1)
                dve.wait_ge(chain, 1)
                dve.wait_ge(edges_in, 32)
                nc.vector.tensor_tensor(mark[:, :], edge[:, 1:SC + 1], edge[:, 0:SC], ALU.is_equal).then_inc(chain, 1)
                dve.wait_ge(chain, 2)
                nc.vector.tensor_copy(mark16[:, :], mark[:, :]).then_inc(marked, 1)
                nc.vector.tensor_scalar(reset16[:, :], mark[:, :], -1.0, -NEG, ALU.add, ALU.mult).then_inc(marked, 1)
                if not o:
                    dve.wait_ge(w_in, 16)
                    nc.vector.tensor_tensor_scan(wrun[:, :], mark[:, :], wt[:, :], 0.0, ALU.mult, ALU.add).then_inc(carries, 1)
                    nc.vector.tensor_tensor_scan(wprod[:, :], mark[:, :], mark[:, :], 1.0, ALU.mult, ALU.min).then_inc(carries, 1)
                    nc.vector.memset(cscan[:, 0:1], 0.0).then_inc(chain, 1)
                    dve.wait_ge(cturn, 1)
                    nc.vector.tensor_copy(crow[:, :], pe1[:, :]).then_inc(cback, 1)
                    dve.wait_ge(cback, 1)
                    dve.wait_ge(chain, 3)
                    nc.vector.tensor_tensor_scan(cscan[:, 1:SR + 1], crow[:, SR:2 * SR], crow[:, 0:SR], 0.0, ALU.mult, ALU.add).then_inc(cback, 1)
                    dve.wait_ge(cturn, 2)
                    nc.vector.tensor_copy(ccol[:, :], pe2[:, :]).then_inc(chain, 1)
                    dve.wait_ge(chain, 4)
                    nc.vector.scalar_tensor_tensor(out=wall[:, :], in0=wprod[:, :], scalar=ccol[:, 0:1], in1=wrun[:, :],
                                                   op0=ALU.mult, op1=ALU.add).then_inc(chain, 1)
                dve.wait_ge(gat1, 16 * NJ)
                nc.vector.tensor_tensor(hits[:, :, 0:KT], rows1[:, :, :], node(KT), ALU.is_le).then_inc(v, 1)
                dve.wait_ge(v, 4)
                nc.vector.tensor_reduce(below2[:, :], hits[:, :, 0:KT], AX.X, ALU.add).then_inc(v, 1)
                dve.wait_ge(v, 5)
                nc.vector.scalar_tensor_tensor(out=row[:, :], in0=below1[:, :], scalar=float(KT), in1=below2[:, :],
                                               op0=ALU.mult, op1=ALU.add).then_inc(cback, 1)
                dve.wait_ge(cback, 1 if o else 3)
                nc.vector.tensor_copy(index2[:, :], row[:, :]).then_inc(v, 1)
                dve.wait_ge(gat2, 16 * NJ)
                nc.vector.tensor_tensor(hits[:, :, :], rows2[:, :, :], node(KC), ALU.is_le).then_inc(cback, 1)
                dve.wait_ge(cback, 2 if o else 4)
                nc.vector.tensor_reduce(below3[:, :], hits[:, :, :], AX.X, ALU.add).then_inc(cback, 1)
                dve.wait_ge(cback, 3 if o else 5)
                nc.vector.scalar_tensor_tensor(out=upto[:, :], in0=row[:, :], scalar=float(KC), in1=below3[:, :],
                                               op0=ALU.mult, op1=ALU.add).then_inc(v, 1)
                dve.wait_ge(v, 7)
                nc.vector.tensor_copy(before[:, 1:NJ], upto[:, 0:NJ - 1]).then_inc(cback, 1)
                nc.vector.memset(before[0:1, 0:1], 0.0).then_inc(v, 1)
                dve.wait_ge(cback, 4 if o else 6)
                dve.wait_ge(v, 8)
                dve.wait_ge(shifted, 16)
                n = 8

                def link(ins):
                    ins.then_inc(v, 1)

                link(nc.vector.tensor_tensor(info["cnt"][:, :], upto[:, :], before[:, :], ALU.subtract))
                link(nc.vector.tensor_scalar(f1[:, :], before[:, :], -float(NONE), None, ALU.add))
                link(nc.vector.tensor_scalar(l1[:, :], upto[:, :], -float(NONE + 1), None, ALU.add))
                link(nc.vector.tensor_scalar(s1[:, :], before[:, :], float(H), None, ALU.is_lt))
                link(nc.vector.tensor_scalar(s2[:, :], upto[:, :], float(H), None, ALU.is_gt))
                dve.wait_ge(v, n + 5)
                link(nc.vector.tensor_scalar(has[:, :], info["cnt"][:, :], 0.0, None, ALU.is_gt))
                link(nc.vector.tensor_tensor(info["span"][:, :], s1[:, :], s2[:, :], ALU.mult))
                dve.wait_ge(v, n + 7)
                link(nc.vector.tensor_tensor(f2[:, :], f1[:, :], has[:, :], ALU.mult))
                link(nc.vector.tensor_tensor(l2[:, :], l1[:, :], has[:, :], ALU.mult))
                dve.wait_ge(v, n + 9)
                link(nc.vector.tensor_scalar(info["first"][:, :], f2[:, :], float(NONE), None, ALU.add))
                link(nc.vector.tensor_scalar(info["last"][:, :], l2[:, :], float(NONE), None, ALU.add))

            @block.tensor
            def _(pe):
                if not o:
                    pe.wait_ge(carries, 2)
                    nc.tensor.matmul(pe1[:, 0:SR], wrun[:, SC - 1:SC], ident[0:SR, 0:SR], start=True, stop=True)
                    nc.tensor.matmul(pe1[:, SR:2 * SR], wprod[:, SC - 1:SC], ident[0:SR, 0:SR], start=True, stop=True).then_inc(cturn, 1)
                    pe.wait_ge(cback, 2)
                    nc.tensor.matmul(pe2[:, :], cscan[:, 0:SR], ident[0:1, 0:1], start=True, stop=True).then_inc(cturn, 1)


def edge_sums(nc, sb, ps, sem, ea64, marks, t1, ident, sel2):
    with Stage(nc) as c:
        ea = [sb(c, f"ea{i}", [P, C, 2, D]) for i in range(2)]
        mk = [sb(c, f"mk{i}", [2, 2, W], BF16) for i in range(2)]
        feat = [sb(c, f"feat{i}", [P, W]) for i in range(2)]
        run = [[sb(c, f"run{k}{i}", [P, W]) for i in range(2)] for k in range(2)]
        rows = [sb(c, f"rows{i}", [P, 2, C, 2, D]) for i in range(2)]
        p_in = [ps(c, f"p_in{i}", [P, C, P]) for i in range(2)]
        p_mk = [[ps(c, f"p_mk{k}{i}", [P, W]) for i in range(2)] for k in range(2)]
        p_out = [ps(c, f"p_out{k}", [P, C, P]) for k in range(2)]
        ea_in = [sem(c, f"ea_in{i}") for i in range(2)]
        stored = [sem(c, f"stored{i}") for i in range(2)]
        turned, spread, feats, summed, maxed, rowed, drained = (
            sem(c, n) for n in ("turned", "spread", "feats", "summed", "maxed", "rowed", "drained"))
        scanned = (summed, maxed)
        with nc.Block() as block:
            @block.sync
            def _(sp):
                def load(g):
                    s, n, k, row, w = g.slot(2), g.n, g.turn(2), g.row, g.w
                    row = sp.snap(row) if not isinstance(row, int) else row
                    wait_from(sp, spread, n - 1)
                    for h in range(2):
                        sp.dma_start(ea[s][0:w // C, :, h, :], by_edge(ea64, h, row, w)).then_inc(ea_in[s], 16)
                    sp.dma_start(mk[s][:, :, 0:w], marks[0][:, :, ds(row, w)]).then_inc(ea_in[s], 16)

                each_group(sp, (0, load))

            @block.gpsimd
            def _(pool):
                def store(g):
                    s, n, k, row, w = g.slot(2), g.n, g.turn(2), g.row, g.w
                    pool.wait_ge(drained, 2 * n + 2)
                    for h in range(2):
                        pool.dma_start(by_edge(t1, h, row, w), rows[s][0:w // C, h, :, :, :].rearrange("p c k f -> p c (k f)")).then_inc(stored[s], 16)

                each_group(pool, (0, store))
                for s in range(2):
                    pool.wait_ge(stored[s], 32 * ((NG + 2 - s) // 2))

            @block.tensor
            def _(pe):
                def spread_and_turn(g):
                    s, n, k, row, w = g.slot(2), g.n, g.turn(2), g.row, g.w
                    p = w // C
                    pe.wait_ge(ea_in[s], 48 * k + 48)
                    wait_from(pe, feats, n - 1)
                    for cc in range(C):
                        last = nc.tensor.transpose(p_in[s][:, cc, 0:p], ea[s][0:p, cc, :, :].rearrange("p h f -> p (h f)"), ident[0:p, 0:p])
                    last.then_inc(turned, 1)
                    wait_from(pe, maxed, n - 1)
                    for kind in range(2):
                        last = nc.tensor.matmul(p_mk[kind][s][:, 0:w], sel2[:, :], mk[s][:, kind, 0:w], start=True, stop=True)
                    last.then_inc(spread, 1)

                def turn_back(g):
                    s, n, k, row, w = g.slot(2), g.n, g.turn(2), g.row, g.w
                    p = w // C
                    for kind in range(2):
                        pe.wait_ge(scanned[kind], n + 1)
                        wait_from(pe, drained, 2 * n + kind - 1)
                        r = run[kind][s][:, 0:w].rearrange("q (p c) -> q p c", c=C)
                        for cc in range(C):
                            last = nc.tensor.transpose(p_out[kind][0:p, cc, :], r[:, :, cc], ident[:, :])
                        last.then_inc(rowed, 1)

                each_group(pe, (0, spread_and_turn), (1, turn_back))

            @block.scalar
            def _(act):
                def to_order(g):
                    s, n, k, row, w = g.slot(2), g.n, g.turn(2), g.row, g.w
                    p = w // C
                    act.wait_ge(turned, n + 1)
                    wait_from(act, maxed, n - 1)
                    nc.scalar.activation(feat[s][:, 0:w].rearrange("q (p c) -> q p c", c=C),
                                         p_in[s][:, :, 0:p].rearrange("q c p -> q p c"), ACT.Copy).then_inc(feats, 1)

                def to_rows(g):
                    s, n, k, row, w = g.slot(2), g.n, g.turn(2), g.row, g.w
                    p = w // C
                    wait_from(act, stored[s], 32 * k)
                    for kind in range(2):
                        act.wait_ge(rowed, 2 * n + kind + 1)
                        nc.scalar.activation(rows[s][0:p, :, :, kind, :].rearrange("p h c f -> p c h f"),
                                             p_out[kind][0:p, :, :].rearrange("p c (h f) -> p c h f", h=2),
                                             ACT.Copy).then_inc(drained, 1)

                each_group(act, (0, to_order), (1, to_rows))

            @block.vector
            def _(dve):
                def scan(g):
                    s, n, k, row, w = g.slot(2), g.n, g.turn(2), g.row, g.w
                    dve.wait_ge(spread, n + 1)
                    dve.wait_ge(feats, n + 1)
                    wait_from(dve, rowed, 2 * n - 2)
                    first = g.zero
                    for kind, (op0, op1, initial) in enumerate(((ALU.mult, ALU.add, 0.0), (ALU.add, ALU.max, NEG))):
                        if not first:
                            dve.wait_ge(scanned[kind], n)
                            initial = run[kind][1 - s][:, W - 1:W]
                        nc.vector.tensor_tensor_scan(run[kind][s][:, 0:w], p_mk[kind][s][:, 0:w], feat[s][:, 0:w],
                                                     initial, op0, op1).then_inc(scanned[kind], 1)

                each_group(dve, (0, scan))


NB = 7
PARTS = ((0, 4), (4, 3))
ITERS = NJ // NB


def per_node(t, width=D):
    return t[:, :].unsqueeze(2).to_broadcast((P, NJ, width))


def per_feature(t, width=D):
    return t[:, :].unsqueeze(1).to_broadcast((P, NJ, width))


def row_of(vector, width=D):
    return vector.rearrange("(o f) -> o f", o=1).to_broadcast((P, width))


def column_of(vector):
    return vector.rearrange("(p o) -> p o", o=1)


def dense(nc, sb, ps, sem, groups, loads, hidden, last, put):
    NQ = len(groups)
    width = [sum(w for _, w in g) for g in groups]
    with Stage(nc) as c:
        w1, w2, bias1, bias2, bring, nload = loads(c)
        cat = [[sb(c, f"cat{q}{i}", [P, 4, width[q]]) for i in range(2)] for q in range(NQ)]
        feats = [[sb(c, f"feats{q}{i}", [P, 4 * P]) for i in range(2)] for q in range(NQ)]
        bank_in = [[ps(c, f"bank_in{q}{i}", [P, 4 * P]) for i in range(2)] for q in range(2)]
        bank_hid = [ps(c, f"bank_hid{i}", [P, 4 * P]) for i in range(2)]
        bank_out = [ps(c, f"bank_out{i}", [P, 4 * P]) for i in range(2)]
        chunks = hidden[1] if hidden else 0
        hid = [[sb(c, f"hid{m}{i}", [P, 4 * P]) for i in range(2)] for m in range(chunks)]
        outf = [sb(c, f"outf{i}", [last[1], 4 * P]) for i in range(2)]
        bank_of = (bank_hid, bank_in[1])
        weights_in, passed = sem(c, "weights_in"), sem(c, "passed")
        taken, turned, copied, summed, acted, mixed, biased, rowed, placed = (
            [sem(c, f"{n}{i}") for i in range(2)] for n in
            ("taken", "turned", "copied", "summed", "acted", "mixed", "biased", "rowed", "placed"))
        NCAT = sum(len(g) for g in groups)
        with nc.Block() as block:
            @block.sync
            def _(sp):
                bring(sp, weights_in)

            @block.vector
            def _(dve):
                with dve.Fori(0, ITERS) as it:
                    t = dve.snap(it)
                    for i, (a, k) in enumerate(PARTS):
                        dve.wait_ge(turned[i], t)
                        for q, g in enumerate(groups):
                            at = 0
                            for tensor, f in g:
                                nc.vector.tensor_copy(cat[q][i][:, 0:k, at:at + f], tensor[:, ds(t * NB + a, k), :]).then_inc(taken[i], 1)
                                at += f
                    for i, (a, k) in enumerate(PARTS):
                        dve.wait_ge(rowed[i], t + 1)
                        put(nc.vector, ds(t * NB + a, k), bank_in[0][i][:, 0:k * last[1]].rearrange("p (j f) -> p j f", f=last[1])).then_inc(placed[i], 1)

            @block.tensor
            def _(pe):
                pe.wait_ge(weights_in, nload)
                with pe.Fori(0, ITERS) as it:
                    t = pe.snap(it)
                    for i, (a, k) in enumerate(PARTS):
                        pe.wait_ge(taken[i], t * NCAT + NCAT)
                        pe.wait_ge(placed[i], t)
                        if chunks > 1:
                            pe.wait_ge(acted[i], t * chunks)
                        pe.sem_inc(passed, 1)
                        for q in range(NQ):
                            for j in range(k):
                                last_mm = nc.tensor.transpose(bank_in[q][i][0:width[q], j * P:(j + 1) * P], cat[q][i][:, j, :], ident_of[0][:, :])
                        last_mm.then_inc(turned[i], 1)
                    for m in range(chunks):
                        for i, (a, k) in enumerate(PARTS):
                            pe.wait_ge(copied[i], t * NQ + NQ)
                            pe.wait_ge(acted[i], t * chunks)
                            for q in range(NQ):
                                mm = nc.tensor.matmul(bank_of[m][i][:, 0:k * P], w1[q][0:width[q], m * P:(m + 1) * P], feats[q][i][0:width[q], 0:k * P],
                                                      start=q == 0, stop=q == NQ - 1)
                            mm.then_inc(summed[i], 1)
                    for i, (a, k) in enumerate(PARTS):
                        if chunks:
                            pe.wait_ge(acted[i], t * chunks + chunks)
                        else:
                            pe.wait_ge(copied[i], t * NQ + NQ)
                        pe.wait_ge(biased[i], t)
                        ins = [(w2[m], hid[m][i]) for m in range(chunks)] or [(w1[0][0:width[0], :], feats[0][i][0:width[0], :])]
                        for m, (wm, xm) in enumerate(ins):
                            mm = nc.tensor.matmul(bank_out[i][0:last[1], 0:k * P], wm, xm[:, 0:k * P], start=m == 0, stop=m == len(ins) - 1)
                        mm.then_inc(mixed[i], 1)
                    for i, (a, k) in enumerate(PARTS):
                        pe.wait_ge(biased[i], t + 1)
                        pe.sem_inc(passed, 1)
                        for j in range(k):
                            mm = nc.tensor.transpose(bank_in[0][i][:, j * last[1]:(j + 1) * last[1]], outf[i][:, j * P:(j + 1) * P], ident_of[0][0:last[1], 0:last[1]])
                        mm.then_inc(rowed[i], 1)

            @block.scalar
            def _(act):
                act.wait_ge(weights_in, nload)
                with act.Fori(0, ITERS) as it:
                    t = act.snap(it)
                    for i, (a, k) in enumerate(PARTS):
                        act.wait_ge(turned[i], t + 1)
                        act.wait_ge(mixed[i], t)
                        for q in range(NQ):
                            nc.scalar.activation(feats[q][i][0:width[q], 0:k * P], bank_in[q][i][0:width[q], 0:k * P], ACT.Copy).then_inc(copied[i], 1)
                    for m in range(chunks):
                        for i, (a, k) in enumerate(PARTS):
                            act.wait_ge(summed[i], t * chunks + m + 1)
                            nc.scalar.activation(hid[m][i][:, 0:k * P], bank_of[m][i][:, 0:k * P], hidden[0], bias=bias1[:, m:m + 1]).then_inc(acted[i], 1)
                    for i, (a, k) in enumerate(PARTS):
                        act.wait_ge(mixed[i], t + 1)
                        act.wait_ge(rowed[i], t)
                        nc.scalar.activation(outf[i][:, 0:k * P], bank_out[i][0:last[1], 0:k * P], last[0], bias=bias2[:, 0:1]).then_inc(biased[i], 1)


ident_of = [None]


def norm(nc, sb, sem, ahead, t, o, behind):
    with Stage(nc) as c:
        s_sum, s_mean, s_sq, s_var, s_sd, s_rs = (sb(c, n, [P, NJ]) for n in ("s_sum", "s_mean", "s_sq", "s_var", "s_sd", "s_rs"))
        chain, root = sem(c, "chain"), sem(c, "root")
        with nc.Block() as block:
            @block.vector
            def _(dve):
                count = [0]

                def link(ins):
                    count[0] += 1
                    ins.then_inc(chain, 1)
                    dve.wait_ge(chain, count[0])

                for f in ahead:
                    link(f(nc.vector))
                link(nc.vector.tensor_reduce(s_sum[:, :], t[:, :, :], AX.X, ALU.add))
                link(nc.vector.tensor_scalar(s_mean[:, :], s_sum[:, :], 1.0 / D, None, ALU.mult))
                link(nc.vector.tensor_tensor(o[:, :, :], t[:, :, :], per_node(s_mean), ALU.subtract))
                link(nc.vector.tensor_tensor(t[:, :, :], o[:, :, :], o[:, :, :], ALU.mult))
                link(nc.vector.tensor_reduce(s_sq[:, :], t[:, :, :], AX.X, ALU.add))
                link(nc.vector.tensor_scalar(s_var[:, :], s_sq[:, :], 1.0 / D, EPS, ALU.mult, ALU.add))
                dve.wait_ge(root, 1)
                link(nc.vector.reciprocal(s_rs[:, :], s_sd[:, :]))
                link(nc.vector.tensor_tensor(o[:, :, :], o[:, :, :], per_node(s_rs), ALU.mult))
                for f in behind:
                    link(f(nc.vector))

            @block.scalar
            def _(act):
                act.wait_ge(chain, len(ahead) + 6)
                nc.scalar.activation(s_sd[:, :], s_var[:, :], ACT.Sqrt).then_inc(root, 1)


def gather_rows(pool, nc, dest, width, table, index, counted):
    for j in range(NJ):
        nc.gpsimd.indirect_dma_start(dest[:, j, :], None, table, bass.IndirectOffsetOnAxis(ap=index[:, j:j + 1], axis=0),
                                     bounds_check=E - 1, oob_is_err=False).then_inc(counted, 16)


def node_layers_1_2(nc, sb, ps, sem, X, info, t1, wsum, ident, w0a, b0a, w0b, b0b, u1, w1a, b1a, w1b, b1b, g1, be1):
    with Stage(nc) as c:
        agg = sb(c, "agg", [P, NJ, 2 * D])
        mean = sb(c, "mean", [P, NJ, D])
        Y, Z = sb(c, "Y", [P, NJ, D]), sb(c, "Z", [P, NJ, D])
        GA, BE = sb(c, "GA", [P, D]), sb(c, "BE", [P, D])
        with Stage(nc) as cc:
            wn = sb(cc, "wn", [P, NJ, 1])
            carry = sb(cc, "carry", [P, 2 * D])
            nz, iszero, safe, inv, reset, atleast, per = (sb(cc, n, [P, NJ]) for n in ("nz", "iszero", "safe", "inv", "reset", "atleast", "per"))
            cleared, agg_in, wn_in, carry_in, chain = (sem(cc, n) for n in ("cleared", "agg_in", "wn_in", "carry_in", "chain"))
            with nc.Block() as block:
                @block.sync
                def _(sp):
                    sp.dma_start(carry[:, :], t1[H - 1:H, :].to_broadcast((P, 2 * D))).then_inc(carry_in, 16)
                    sp.dma_start(GA[:, :], row_of(g1)).then_inc(carry_in, 16)
                    sp.dma_start(BE[:, :], row_of(be1)).then_inc(carry_in, 16)

                @block.gpsimd
                def _(pool):
                    pool.wait_ge(cleared, 2)
                    gather_rows(pool, nc, wn, 1, wsum, info["last"], wn_in)
                    gather_rows(pool, nc, agg, 2 * D, t1, info["last"], agg_in)

                @block.vector
                def _(dve):
                    count = [0]

                    def link(ins):
                        count[0] += 1
                        ins.then_inc(chain, 1)
                        dve.wait_ge(chain, count[0])

                    nc.vector.memset(wn[:, :, :], 0.0).then_inc(cleared, 1)
                    nc.vector.memset(agg[:, :, :], 0.0).then_inc(cleared, 1)
                    dve.wait_ge(wn_in, 16 * NJ)
                    w = wn[:, :, 0]
                    link(nc.vector.tensor_scalar(nz[:, :], w, 0.0, None, ALU.not_equal))
                    link(nc.vector.tensor_scalar(iszero[:, :], w, 0.0, None, ALU.is_equal))
                    link(nc.vector.tensor_tensor(safe[:, :], iszero[:, :], w, ALU.add))
                    link(nc.vector.reciprocal(inv[:, :], safe[:, :]))
                    link(nc.vector.tensor_tensor(Y[:, :, :], X[:, :, :], wn[:, :, :].to_broadcast((P, NJ, D)), ALU.mult))
                    link(nc.vector.tensor_tensor(Z[:, :, :], Y[:, :, :], per_node(inv), ALU.mult))
                    link(nc.vector.tensor_tensor(Y[:, :, :], Z[:, :, :], X[:, :, :], ALU.add))
                    link(nc.vector.tensor_tensor(Z[:, :, :], Y[:, :, :], per_node(nz), ALU.mult))
                    link(nc.vector.tensor_scalar(reset[:, :], info["span"][:, :], -1.0, -NEG, ALU.add, ALU.mult))
                    link(nc.vector.tensor_scalar(atleast[:, :], info["cnt"][:, :], 1.0, None, ALU.max))
                    link(nc.vector.reciprocal(per[:, :], atleast[:, :]))
                    dve.wait_ge(agg_in, 16 * NJ)
                    dve.wait_ge(carry_in, 48)
                    link(nc.vector.tensor_tensor(mean[:, :, :], per_node(info["span"]), per_feature(carry[:, 0:D]), ALU.mult))
                    link(nc.vector.tensor_tensor(agg[:, :, 0:D], agg[:, :, 0:D], mean[:, :, :], ALU.add))
                    link(nc.vector.tensor_tensor(mean[:, :, :], per_node(info["span"]), per_feature(carry[:, D:2 * D]), ALU.mult))
                    link(nc.vector.tensor_tensor(mean[:, :, :], mean[:, :, :], per_node(reset), ALU.add))
                    has = count[0]
                    link(nc.vector.tensor_tensor(agg[:, :, D:2 * D], agg[:, :, D:2 * D], mean[:, :, :], ALU.max))
                    link(nc.vector.tensor_tensor(mean[:, :, :], agg[:, :, 0:D], per_node(per), ALU.mult))

        def loads_1(c):
            W1, W2 = sb(c, "W1", [D, 2 * P]), sb(c, "W2", [P, 2, D])
            B1, B2 = sb(c, "B1", [P, 2]), sb(c, "B2", [D, 1])

            def bring(sp, done):
                sp.dma_start(W1[:, :], w0a).then_inc(done, 16)
                sp.dma_start(W2[:, :, :], w0b.rearrange("(q p) f -> p q f", q=2)).then_inc(done, 16)
                with nc.allow_non_contiguous_dma(reason="biases by partition"):
                    sp.dma_start(B1[:, :], b0a.rearrange("(q p) -> p q", q=2)).then_inc(done, 16)
                    sp.dma_start(B2[:, :], column_of(b0b)).then_inc(done, 16)
            return [W1], [W2[:, 0, :], W2[:, 1, :]], B1, B2, bring, 64

        dense(nc, sb, ps, sem, [[(Z, D)]], loads_1, (ACT.Relu, 2), (ACT.Relu, D),
              lambda eng, cols, bank: eng.tensor_tensor(Y[:, cols, :], X[:, cols, :], bank, ALU.add))
        norm(nc, sb, sem, [], Y, X, [])

        V1a, V1b, V2 = sb(c, "V1a", [P, P]), sb(c, "V1b", [P, P]), sb(c, "V2", [P, D])
        VU, UB, C1, C1B, C2 = (sb(c, n, [P, 1]) for n in ("VU", "UB", "C1", "C1B", "C2"))
        weights2, folded = sem(c, "weights2"), sem(c, "folded")
        with nc.Block() as block:
            @block.sync
            def _(sp):
                sp.dma_start(V1a[:, :], w1a[D:3 * D, :]).then_inc(weights2, 16)
                sp.dma_start(V1b[0:D, :], w1a[0:D, :]).then_inc(weights2, 16)
                sp.dma_start(V1b[D:P, :], w1a[3 * D:4 * D, :]).then_inc(weights2, 16)
                sp.dma_start(V2[:, :], w1b).then_inc(weights2, 16)
                with nc.allow_non_contiguous_dma(reason="biases by partition"):
                    sp.dma_start(C1[:, :], column_of(b1a)).then_inc(weights2, 16)
                    sp.dma_start(C2[0:D, :], column_of(b1b)).then_inc(weights2, 16)
                    sp.dma_start(VU[:, :], w1a[4 * D:4 * D + 1, :].rearrange("o f -> f o")).then_inc(weights2, 16)
                    sp.dma_start(UB[:, :], u1[0:1, 0:1].to_broadcast((P, 1))).then_inc(weights2, 16)

            @block.vector
            def _(dve):
                dve.wait_ge(weights2, 16 * 8)
                nc.vector.scalar_tensor_tensor(out=C1B[:, :], in0=VU[:, :], scalar=UB[:, 0:1], in1=C1[:, :],
                                               op0=ALU.mult, op1=ALU.add).then_inc(folded, 1)

        dense(nc, sb, ps, sem, [[(agg, 2 * D)], [(X, D), (mean, D)]], lambda c: ([V1a, V1b], [V2[:, :]], C1B, C2[0:D, :], lambda sp, done: None, 0),
              (ACT.Gelu, 1), (ACT.Identity, D), lambda eng, cols, bank: eng.tensor_copy(Y[:, cols, :], bank))
        norm(nc, sb, sem, [], Y, Z, [
            lambda eng: eng.tensor_tensor(Y[:, :, :], Z[:, :, :], per_feature(GA), ALU.mult),
            lambda eng: eng.tensor_tensor(Z[:, :, :], Y[:, :, :], per_feature(BE), ALU.add),
            lambda eng: eng.tensor_tensor(Y[:, :, :], Z[:, :, :], X[:, :, :], ALU.add),
            lambda eng: eng.tensor_tensor(Z[:, :, :], Y[:, :, :], X[:, :, :], ALU.add)])
        norm(nc, sb, sem, [], Z, X, [])


def node_tables(nc, sb, ps, sem, which, X, info, key, gathered, spread, tabg, tabs, start, ident):
    with Stage(nc) as c:
        rows = sb(c, "rows", [P, NJ, 2 * D])
        prime_key = sb(c, "prime_key", [2, 1], I32)
        prime = sb(c, "prime", [2, D])

        def loads(cc):
            WW, BB = sb(cc, "WW", [D, 2 * D]), sb(cc, "BB", [2 * D, 1])
            biases = [b for b in (gathered[1], spread[1]) if b is not None]
            zero = sem(cc, "zero")

            def bring(sp, done):
                sp.dma_start(WW[:, 0:D], gathered[0]).then_inc(done, 16)
                sp.dma_start(WW[:, D:2 * D], spread[0]).then_inc(done, 16)
                if len(biases) < 2:
                    sp.wait_ge(zero, 1)
                for q, b in enumerate(biases):
                    with nc.allow_non_contiguous_dma(reason="biases by partition"):
                        sp.dma_start(BB[q * D:(q + 1) * D, :], column_of(b)).then_inc(done, 16)

            if len(biases) < 2:
                with nc.Block() as block:
                    @block.vector
                    def _(dve):
                        nc.vector.memset(BB[:, :], 0.0).then_inc(zero, 1)
            return [WW], None, None, BB, bring, 32 + 16 * len(biases)

        dense(nc, sb, ps, sem, [[(X, D)]], loads, None, (ACT.Identity, 2 * D),
              lambda eng, cols, bank: eng.tensor_copy(rows[:, cols, :], bank))
        stored, keyed, primed, firsts, put = (sem(c, n) for n in ("stored", "keyed", "primed", "firsts", "put"))
        with nc.Block() as block:
            @block.sync
            def _(sp):
                sp.dma_start(prime_key[:, :], key[H:H + 1, :].to_broadcast((2, 1))).then_inc(keyed, 16)
                sp.dma_start(tabs.rearrange("(p j) f -> p j f", j=NJ), rows[:, :, D:2 * D]).then_inc(stored, 16)
                sp.dma_start(tabg.rearrange("(p j) f -> p j f", j=NJ), rows[:, :, 0:D]).then_inc(stored, 16)
                sp.wait_ge(primed, 16)
                sp.wait_ge(firsts, 16 * NJ)
                sp.dma_start(start[H:H + 1, :], prime[0:1, :]).then_inc(put, 16)
                sp.wait_ge(put, 16)

            @block.gpsimd
            def _(pool):
                for j in range(NJ):
                    nc.gpsimd.indirect_dma_start(start, bass.IndirectOffsetOnAxis(ap=info["first"][:, j:j + 1], axis=0), rows[:, j, D:2 * D], None,
                                                 bounds_check=E - 1, oob_is_err=False).then_inc(firsts, 16)
                pool.wait_ge(keyed, 16)
                pool.wait_ge(stored, 32)
                nc.gpsimd.indirect_dma_start(prime[:, :], None, tabs, bass.IndirectOffsetOnAxis(ap=prime_key[:, :], axis=0)).then_inc(primed, 16)


def edges_3(nc, sb, ps, sem, other, marks, tabg, start, t2, ident, sel2, w2b, b2b, w2g, b2g):
    with Stage(nc) as c:
        W2, WG = sb(c, "W2", [P, P]), sb(c, "WG", [P, P])
        B2, BG = sb(c, "B2", [P, 1]), sb(c, "BG", [P, 1])
        first = [sb(c, f"first{i}", [P, C, 2, D]) for i in range(AHEAD)]
        mk = [sb(c, f"mk{i}", [2, W], BF16) for i in range(AHEAD)]
        ix = [sb(c, f"ix{i}", [P, 2, C], I32) for i in range(AHEAD)]
        got = [sb(c, f"got{i}", [P, C, 2, D]) for i in range(AHEAD)]
        starts, own, pre, hid, inter, gate, gated, run = (
            [sb(c, f"{n}{i}", [P, W]) for i in range(2)] for n in ("starts", "own", "pre", "hid", "inter", "gate", "gated", "run"))
        rows = [sb(c, f"rows{i}", [P, 2, C, D]) for i in range(2)]
        p_first, p_got, p_inter, p_gate, p_own, p_sum = (
            ps(c, n, [P, C * P]) for n in ("p_first", "p_got", "p_inter", "p_gate", "p_own", "p_sum"))
        p_out = [ps(c, f"p_out{i}", [P, C, P]) for i in range(2)]
        zeroed, weights_in, passed = (sem(c, n) for n in ("zeroed", "weights_in", "passed"))
        first_in, ix_in, got_in = ([sem(c, f"{n}{i}") for i in range(AHEAD)] for n in ("first_in", "ix_in", "got_in"))
        stored = [sem(c, f"stored{i}") for i in range(2)]
        (marked, turned_first, turned_got, started, owned, added, relued, mixed, biased, scored, gates, products, remarked,
         summed, rowed, drained) = (
            sem(c, n) for n in ("marked", "turned_first", "turned_got", "started", "owned", "added", "relued", "mixed", "biased",
                                "scored", "gates", "products", "remarked", "summed", "rowed", "drained"))
        with nc.Block() as block:
            @block.sync
            def _(sp):
                sp.wait_ge(zeroed, 2)
                for h in range(2):
                    at = slice(h * D, (h + 1) * D)
                    for t, w in ((W2, w2b), (WG, w2g)):
                        sp.dma_start(t[at, at], w).then_inc(weights_in, 16)
                    with nc.allow_non_contiguous_dma(reason="biases by partition"):
                        for t, b in ((B2, b2b), (BG, b2g)):
                            sp.dma_start(t[at, :], column_of(b)).then_inc(weights_in, 16)

                def load(g):
                    s, row = g.slot(AHEAD), snapped(sp, g.row)
                    wait_from(sp, remarked, g.n - AHEAD + 1)
                    sp.dma_start(ix[s][0:g.p, :, :], indices_of(other, row, g.w)).then_inc(ix_in[s], 16)
                    for h in range(2):
                        sp.dma_start(first[s][0:g.p, :, h, :], by_edge(start, h, row, g.w)).then_inc(first_in[s], 16)
                    sp.dma_start(mk[s][:, 0:g.w], marks[1][:, 0, ds(row, g.w)]).then_inc(first_in[s], 16)

                each_group(sp, (0, load))

            @block.gpsimd
            def _(pool):
                def gather(g):
                    s = g.slot(AHEAD)
                    pool.wait_ge(ix_in[s], 16 * g.turn(AHEAD) + 16)
                    wait_from(pool, turned_got, g.n - AHEAD + 1)
                    pool.sem_inc(passed, 1)
                    for cc in range(C):
                        for h in range(2):
                            nc.gpsimd.indirect_dma_start(got[s][0:g.p, cc, h, :], None, tabg,
                                                         bass.IndirectOffsetOnAxis(ap=ix[s][0:g.p, h, cc:cc + 1], axis=0)).then_inc(got_in[s], 16)

                each_group(pool, (0, gather))

            @block.tensor
            def _(pe):
                pe.wait_ge(weights_in, 128)

                def turn_back(g):
                    s = g.slot(2)
                    pe.wait_ge(summed, g.n + 1)
                    wait_from(pe, drained, g.n - 1)
                    turn_to_edges(nc, p_out[s], run[s], g, ident).then_inc(rowed, 1)

                def gate_scores(g):
                    pe.wait_ge(biased, g.n + 1)
                    wait_from(pe, gates, g.n)
                    nc.tensor.matmul(p_gate[:, 0:g.w], WG[:, :], inter[g.slot(2)][:, 0:g.w], start=True, stop=True).then_inc(scored, 1)

                def first_rows(g):
                    s = g.slot(AHEAD)
                    pe.wait_ge(first_in[s], 48 * g.turn(AHEAD) + 48)
                    wait_from(pe, started, g.n)
                    turn_to_features(nc, p_first, first[s], g, ident).then_inc(turned_first, 1)
                    wait_from(pe, owned, g.n)
                    nc.tensor.matmul(p_own[:, 0:g.w], sel2[:, :], mk[s][:, 0:g.w], start=True, stop=True).then_inc(marked, 1)

                def gathered_rows(g):
                    s = g.slot(AHEAD)
                    pe.wait_ge(got_in[s], 128 * g.turn(AHEAD) + 128)
                    wait_from(pe, added, g.n)
                    turn_to_features(nc, p_got, got[s], g, ident).then_inc(turned_got, 1)

                def marks_again(g):
                    wait_from(pe, summed, g.n)
                    nc.tensor.matmul(p_sum[:, 0:g.w], sel2[:, :], mk[g.slot(AHEAD)][:, 0:g.w], start=True, stop=True).then_inc(remarked, 1)

                def interact(g):
                    pe.wait_ge(relued, g.n + 1)
                    wait_from(pe, biased, g.n)
                    nc.tensor.matmul(p_inter[:, 0:g.w], W2[:, :], hid[g.slot(2)][:, 0:g.w], start=True, stop=True).then_inc(mixed, 1)

                each_group(pe, (3, turn_back), (2, gate_scores), (0, first_rows), (2, marks_again), (1, gathered_rows), (1, interact))

            @block.scalar
            def _(act):
                act.wait_ge(weights_in, 128)

                def start_rows(g):
                    act.wait_ge(turned_first, g.n + 1)
                    wait_from(act, owned, g.n - 1)
                    nc.scalar.activation(by_place(starts[g.slot(2)], g), by_block(p_first, g), ACT.Copy).then_inc(started, 1)

                def gates_of(g):
                    act.wait_ge(scored, g.n + 1)
                    wait_from(act, products, g.n - 1)
                    nc.scalar.activation(gate[g.slot(2)][:, 0:g.w], p_gate[:, 0:g.w], ACT.Sigmoid, bias=BG[:, 0:1]).then_inc(gates, 1)

                def relu(g):
                    act.wait_ge(added, g.n + 1)
                    wait_from(act, mixed, g.n - 1)
                    nc.scalar.activation(hid[g.slot(2)][:, 0:g.w], pre[g.slot(2)][:, 0:g.w], ACT.Relu).then_inc(relued, 1)

                def to_rows(g):
                    s = g.slot(2)
                    act.wait_ge(rowed, g.n + 1)
                    wait_from(act, stored[s], 16 * g.turn(2))
                    nc.scalar.activation(rows[s][0:g.p, :, :, :].rearrange("p h c f -> p c h f"),
                                         p_out[s][0:g.p, :, :].rearrange("p c (h f) -> p c h f", h=2), ACT.Copy).then_inc(drained, 1)
                    act.wait_ge(drained, g.n + 1)
                    act.dma_start(both_halves(t2, g.row, g.w), rows[s][0:g.p, :, :, :].rearrange("p h c f -> p h (c f)")).then_inc(stored[s], 16)

                def bias(g):
                    act.wait_ge(mixed, g.n + 1)
                    wait_from(act, products, g.n - 1)
                    nc.scalar.activation(inter[g.slot(2)][:, 0:g.w], p_inter[:, 0:g.w], ACT.Identity, bias=B2[:, 0:1]).then_inc(biased, 1)

                each_group(act, (2, gates_of), (0, start_rows), (3, to_rows), (1, relu), (1, bias))
                for s in range(2):
                    act.wait_ge(stored[s], 16 * ((NG + 2 - s) // 2))

            @block.vector
            def _(dve):
                nc.vector.memset(W2[:, :], 0.0).then_inc(zeroed, 1)
                nc.vector.memset(WG[:, :], 0.0).then_inc(zeroed, 1)

                def spread(g):
                    s = g.slot(2)
                    dve.wait_ge(marked, g.n + 1)
                    dve.wait_ge(started, g.n + 1)
                    wait_from(dve, owned, g.n)
                    wait_from(dve, added, g.n - 1)
                    nc.vector.tensor_tensor_scan(own[s][:, 0:g.w], p_own[:, 0:g.w], starts[s][:, 0:g.w],
                                                 0.0 if g.zero else own[1 - s][:, W - 1:W], ALU.mult, ALU.add).then_inc(owned, 1)

                def add(g):
                    s = g.slot(2)
                    dve.wait_ge(owned, g.n + 1)
                    dve.wait_ge(turned_got, g.n + 1)
                    wait_from(dve, relued, g.n - 1)
                    nc.vector.tensor_tensor(by_place(pre[s], g), by_place(own[s], g), by_block(p_got, g), ALU.add).then_inc(added, 1)

                def multiply(g):
                    s = g.slot(2)
                    dve.wait_ge(gates, g.n + 1)
                    wait_from(dve, summed, g.n - 1)
                    nc.vector.tensor_tensor(gated[s][:, 0:g.w], inter[s][:, 0:g.w], gate[s][:, 0:g.w], ALU.mult).then_inc(products, 1)

                def accumulate(g):
                    s = g.slot(2)
                    dve.wait_ge(products, g.n + 1)
                    dve.wait_ge(remarked, g.n + 1)
                    wait_from(dve, summed, g.n)
                    wait_from(dve, rowed, g.n - 1)
                    nc.vector.tensor_tensor_scan(run[s][:, 0:g.w], p_sum[:, 0:g.w], gated[s][:, 0:g.w],
                                                 0.0 if g.zero else run[1 - s][:, W - 1:W], ALU.mult, ALU.add).then_inc(summed, 1)

                each_group(dve, (2, multiply), (1, add), (0, spread), (2, accumulate))


def pool_3(nc, sb, ps, sem, X, info, t2):
    with Stage(nc) as c:
        pooled, Z = sb(c, "pooled", [P, NJ, D]), sb(c, "Z", [P, NJ, D])
        carry = sb(c, "carry", [P, D])
        atleast, per = sb(c, "atleast", [P, NJ]), sb(c, "per", [P, NJ])
        cleared, rows_in, carry_in, chain = (sem(c, n) for n in ("cleared", "rows_in", "carry_in", "chain"))
        with nc.Block() as block:
            @block.sync
            def _(sp):
                sp.dma_start(carry[:, :], t2[H - 1:H, :].to_broadcast((P, D))).then_inc(carry_in, 16)

            @block.gpsimd
            def _(pool):
                pool.wait_ge(cleared, 1)
                gather_rows(pool, nc, pooled, D, t2, info["last"], rows_in)

            @block.vector
            def _(dve):
                nc.vector.memset(pooled[:, :, :], 0.0).then_inc(cleared, 1)
                nc.vector.tensor_scalar(atleast[:, :], info["cnt"][:, :], 1.0, None, ALU.max).then_inc(chain, 1)
                dve.wait_ge(chain, 1)
                nc.vector.reciprocal(per[:, :], atleast[:, :]).then_inc(chain, 1)
                dve.wait_ge(carry_in, 16)
                nc.vector.tensor_tensor(Z[:, :, :], per_node(info["span"]), per_feature(carry), ALU.mult).then_inc(chain, 1)
                dve.wait_ge(chain, 3)
                dve.wait_ge(rows_in, 16 * NJ)
                nc.vector.tensor_tensor(pooled[:, :, :], pooled[:, :, :], Z[:, :, :], ALU.add).then_inc(chain, 1)
                dve.wait_ge(chain, 4)
                nc.vector.tensor_tensor(pooled[:, :, :], pooled[:, :, :], per_node(per), ALU.mult).then_inc(chain, 1)
                dve.wait_ge(chain, 5)
                nc.vector.tensor_tensor(Z[:, :, :], pooled[:, :, :], X[:, :, :], ALU.add).then_inc(chain, 1)
        norm(nc, sb, sem, [], Z, X, [])


def edges_4(nc, sb, ps, sem, other, ea16, marks, tabg, start, t3, ident, sel2, we, att):
    R = 2 * HEADS
    with Stage(nc) as c:
        WE, AT = sb(c, "WE", [2 * ED, P]), sb(c, "AT", [P, P])
        AV = sb(c, "AV", [P, 1])
        onesr, pick = sb(c, "onesr", [P, R]), sb(c, "pick", [P, R])
        blocks = [sb(c, f"blocks{i}", [P, P]) for i in range(3)]
        first, got = ([sb(c, f"{n}{i}", [P, C, 2, D]) for i in range(AHEAD)] for n in ("first", "got"))
        ea = [sb(c, f"ea{i}", [P, C, 2, ED]) for i in range(AHEAD)]
        mk = [sb(c, f"mk{i}", [2, 2, W], BF16) for i in range(AHEAD)]
        ix = [sb(c, f"ix{i}", [P, 2, C], I32) for i in range(AHEAD)]
        starts, own, theirs, both, pre, act_in, logit, left, weighted, run, den = (
            [sb(c, f"{n}{i}", [P, W]) for i in range(2)] for n in ("starts", "own", "theirs", "both", "pre", "act_in", "logit", "left",
                                                                    "weighted", "run", "den"))
        eat = [sb(c, f"eat{i}", [2 * ED, W]) for i in range(2)]
        top = [sb(c, f"top{i}", [P, 1 + W]) for i in range(2)]
        expo, grow = ([sb(c, f"{n}{i}", [P, 2, W]) for i in range(2)] for n in ("expo", "grow"))
        rows = [sb(c, f"rows{i}", [P, 2, C, T3]) for i in range(2)]
        p_first, p_got, p_mk, p_reset, p_small, p_pre, p_logit, p_out = (
            ps(c, n, [P, C * P]) for n in ("p_first", "p_got", "p_mk", "p_reset", "p_small", "p_pre", "p_logit", "p_out"))
        zeroed, made, weights_in, passed = (sem(c, n) for n in ("zeroed", "made", "weights_in", "passed"))
        first_in, ix_in, got_in = ([sem(c, f"{n}{i}") for i in range(AHEAD)] for n in ("first_in", "ix_in", "got_in"))
        stored = [sem(c, f"stored{i}") for i in range(2)]
        (marked, resets, turned_first, turned_ea, turned_got, started, featured, gotten, summed_ea, owned, twice, added, leaked, scored,
         logits, carried, maxed, lefts, expos, grown, weighted_s, summed, dens, rowed, smalls, drained, drained_small) = (
            sem(c, n) for n in ("marked", "resets", "turned_first", "turned_ea", "turned_got", "started", "featured", "gotten", "summed_ea",
                                "owned", "twice", "added", "leaked", "scored", "logits", "carried", "maxed", "lefts", "expos", "grown",
                                "weighted_s", "summed", "dens", "rowed", "smalls", "drained", "drained_small"))
        with nc.Block() as block:
            @block.sync
            def _(sp):
                sp.wait_ge(zeroed, 1)
                for h in range(2):
                    sp.dma_start(WE[h * ED:(h + 1) * ED, h * D:(h + 1) * D], we).then_inc(weights_in, 16)
                    with nc.allow_non_contiguous_dma(reason="the heads' vectors by partition"):
                        sp.dma_start(AV[h * D:(h + 1) * D, :], column_of(att.rearrange("a f -> (a f)"))).then_inc(weights_in, 16)

                def load(g):
                    s, row = g.slot(AHEAD), snapped(sp, g.row)
                    wait_from(sp, resets, g.n - AHEAD + 1)
                    sp.dma_start(ix[s][0:g.p, :, :], indices_of(other, row, g.w)).then_inc(ix_in[s], 16)
                    for h in range(2):
                        sp.dma_start(first[s][0:g.p, :, h, :], by_edge(start, h, row, g.w)).then_inc(first_in[s], 16)
                        sp.dma_start(ea[s][0:g.p, :, h, :], by_edge(ea16, h, row, g.w)).then_inc(first_in[s], 16)
                    sp.dma_start(mk[s][:, :, 0:g.w], marks[0][:, :, ds(row, g.w)]).then_inc(first_in[s], 16)

                each_group(sp, (0, load))

            @block.gpsimd
            def _(pool):
                nc.gpsimd.memset(onesr[:, :], 1.0).then_inc(made, 1)
                nc.gpsimd.memset(blocks[0][:, :], 1.0).then_inc(made, 1)
                pool.wait_ge(made, 2)
                nc.gpsimd.affine_select(out=pick[:, :], in_=onesr[:, :], compare_op=ALU.is_equal, fill=0.0, base=0,
                                        pattern=[[-HC, R]], channel_multiplier=1).then_inc(made, 1)
                nc.gpsimd.affine_select(out=blocks[1][:, :].rearrange("p (r f) -> p r f", r=R), in_=blocks[0][:, :].rearrange("p (r f) -> p r f", r=R),
                                        compare_op=ALU.is_ge, fill=0.0, base=0, pattern=[[-HC, R], [0, HC]], channel_multiplier=1).then_inc(made, 1)
                pool.wait_ge(made, 4)
                nc.gpsimd.affine_select(out=blocks[2][:, :].rearrange("p (r f) -> p r f", r=R), in_=blocks[1][:, :].rearrange("p (r f) -> p r f", r=R),
                                        compare_op=ALU.is_ge, fill=0.0, base=HC - 1, pattern=[[HC, R], [0, HC]], channel_multiplier=-1).then_inc(made, 1)

                def gather(g):
                    s = g.slot(AHEAD)
                    pool.wait_ge(ix_in[s], 16 * g.turn(AHEAD) + 16)
                    wait_from(pool, turned_got, g.n - AHEAD + 1)
                    pool.sem_inc(passed, 1)
                    for cc in range(C):
                        for h in range(2):
                            nc.gpsimd.indirect_dma_start(got[s][0:g.p, cc, h, :], None, tabg,
                                                         bass.IndirectOffsetOnAxis(ap=ix[s][0:g.p, h, cc:cc + 1], axis=0)).then_inc(got_in[s], 16)

                each_group(pool, (0, gather))

            @block.tensor
            def _(pe):
                pe.wait_ge(weights_in, 64)
                pe.wait_ge(made, 5)
                pe.wait_ge(zeroed, 2)

                def turn_back(g):
                    pe.wait_ge(summed, g.n + 1)
                    wait_from(pe, drained, g.n)
                    turn_to_edges(nc, p_out[:, :].rearrange("p (c q) -> p c q", c=C), run[g.slot(2)], g, ident).then_inc(rowed, 1)

                def edge_inputs(g):
                    s = g.slot(AHEAD)
                    pe.wait_ge(first_in[s], 80 * g.turn(AHEAD) + 80)
                    wait_from(pe, started, g.n)
                    turn_to_features(nc, p_first, first[s], g, ident).then_inc(turned_first, 1)
                    wait_from(pe, owned, g.n)
                    nc.tensor.matmul(p_mk[:, 0:g.w], sel2[:, :], mk[s][:, 0, 0:g.w], start=True, stop=True).then_inc(marked, 1)
                    wait_from(pe, featured, g.n)
                    wait_from(pe, drained_small, g.n - LAG)
                    turn_to_features(nc, p_small, ea[s], g, ident, 2 * ED).then_inc(turned_ea, 1)

                def gathered_rows(g):
                    s = g.slot(AHEAD)
                    pe.wait_ge(got_in[s], 128 * g.turn(AHEAD) + 128)
                    wait_from(pe, gotten, g.n)
                    turn_to_features(nc, p_got, got[s], g, ident).then_inc(turned_got, 1)
                    pe.wait_ge(featured, g.n + 1)
                    wait_from(pe, added, g.n)
                    nc.tensor.matmul(p_pre[:, 0:g.w], WE[:, :], eat[g.slot(2)][:, 0:g.w], start=True, stop=True).then_inc(summed_ea, 1)

                def small_back(g):
                    s = g.slot(2)
                    pe.wait_ge(dens, g.n + 1)
                    if not g.late:
                        pe.wait_ge(featured, g.n + LAG + 1)
                    else:
                        pe.wait_ge(drained_small, g.n)
                    for q, t in enumerate((den[s][:, 0:g.w], top[s][:, 1:1 + g.w])):
                        r = t.rearrange("q (p c) -> q p c", c=C)
                        for cc in range(C):
                            at = (q * C + cc) * R
                            mm = nc.tensor.matmul(p_small[0:g.p, at:at + R], r[:, :, cc], pick[:, :], start=True, stop=True)
                    mm.then_inc(smalls, 1)

                def score(g):
                    pe.wait_ge(leaked, g.n + 1)
                    wait_from(pe, logits, g.n)
                    nc.tensor.matmul(p_logit[:, 0:g.w], AT[:, :], act_in[g.slot(2)][:, 0:g.w], start=True, stop=True).then_inc(scored, 1)
                    wait_from(pe, lefts, g.n)
                    nc.tensor.matmul(p_reset[:, 0:g.w], sel2[:, :], mk[g.slot(AHEAD)][:, 1, 0:g.w], start=True, stop=True).then_inc(resets, 1)

                each_group(pe, (3, turn_back), (0, edge_inputs), (1, gathered_rows), (3, small_back), (1, score))

            @block.scalar
            def _(act):
                def start_rows(g):
                    act.wait_ge(turned_first, g.n + 1)
                    wait_from(act, owned, g.n - 1)
                    nc.scalar.activation(by_place(starts[g.slot(2)], g), by_block(p_first, g), ACT.Copy).then_inc(started, 1)
                    act.wait_ge(turned_ea, g.n + 1)
                    wait_from(act, summed_ea, g.n - 1)
                    nc.scalar.activation(by_place(eat[g.slot(2)], g), by_block(p_small, g, 2 * ED), ACT.Copy).then_inc(featured, 1)

                def their_rows(g):
                    act.wait_ge(turned_got, g.n + 1)
                    wait_from(act, weighted_s, g.n - 1)
                    nc.scalar.activation(by_place(theirs[g.slot(2)], g), by_block(p_got, g), ACT.Copy).then_inc(gotten, 1)

                def exps(g):
                    s = g.slot(2)
                    act.wait_ge(expos, 2 * g.n + 2)
                    wait_from(act, dens, g.n - 1)
                    nc.scalar.activation(grow[s][:, :, 0:g.w], expo[s][:, :, 0:g.w], ACT.Exp).then_inc(grown, 1)

                def to_rows(g):
                    s = g.slot(2)
                    wait_from(act, stored[s], 16 * g.turn(2))
                    act.wait_ge(rowed, g.n + 1)
                    nc.scalar.activation(rows[s][0:g.p, :, :, 0:D].rearrange("p h c f -> p c h f"),
                                         p_out[0:g.p, :].rearrange("p (c h f) -> p c h f", h=2, f=D), ACT.Copy).then_inc(drained, 1)
                    act.wait_ge(smalls, g.n + 1)
                    for q in range(2):
                        ins = nc.scalar.activation(rows[s][0:g.p, :, :, D + q * HEADS:D + (q + 1) * HEADS].rearrange("p h c f -> p c h f"),
                                                   p_small[0:g.p, q * C * R:(q + 1) * C * R].rearrange("p (c h f) -> p c h f", h=2, f=HEADS), ACT.Copy)
                    ins.then_inc(drained_small, 1)

                def store(g):
                    s = g.slot(2)
                    act.wait_ge(drained_small, g.n + 1)
                    act.dma_start(both_halves(t3, g.row, g.w), rows[s][0:g.p, :, :, :].rearrange("p h c f -> p h (c f)")).then_inc(stored[s], 16)

                def keep_logits(g):
                    act.wait_ge(scored, g.n + 1)
                    wait_from(act, expos, 2 * g.n - 2)
                    nc.scalar.activation(logit[g.slot(2)][:, 0:g.w], p_logit[:, 0:g.w], ACT.Copy).then_inc(logits, 1)

                each_group(act, (0, start_rows), (1, their_rows), (2, exps), (3, to_rows), (3, store), (1, keep_logits))
                for s in range(2):
                    act.wait_ge(stored[s], 16 * ((NG + 2 - s) // 2))

            @block.vector
            def _(dve):
                nc.vector.memset(WE[:, :], 0.0).then_inc(zeroed, 1)
                dve.wait_ge(weights_in, 64)
                dve.wait_ge(made, 5)
                nc.vector.tensor_scalar(AT[:, :], blocks[2][:, :], AV[:, 0:1], None, ALU.mult).then_inc(zeroed, 1)

                def exponents(g):
                    s = g.slot(2)
                    wait_from(dve, smalls, g.n - 1)
                    if g.zero:
                        nc.vector.memset(top[s][:, 0:1], NEG).then_inc(carried, 1)
                    else:
                        dve.wait_ge(maxed, g.n)
                        nc.vector.tensor_copy(top[s][:, 0:1], top[1 - s][:, W:W + 1]).then_inc(carried, 1)
                    dve.wait_ge(carried, g.n + 1)
                    dve.wait_ge(logits, g.n + 1)
                    dve.wait_ge(resets, g.n + 1)
                    nc.vector.tensor_tensor_scan(top[s][:, 1:1 + g.w], p_reset[:, 0:g.w], logit[s][:, 0:g.w], top[s][:, 0:1], ALU.add, ALU.max).then_inc(maxed, 1)
                    dve.wait_ge(maxed, g.n + 1)
                    wait_from(dve, expos, 2 * g.n - 2)
                    nc.vector.tensor_tensor(left[s][:, 0:g.w], top[s][:, 0:g.w], p_reset[:, 0:g.w], ALU.add).then_inc(lefts, 1)
                    wait_from(dve, grown, g.n - 1)
                    nc.vector.tensor_tensor(expo[s][:, 1, 0:g.w], logit[s][:, 0:g.w], top[s][:, 1:1 + g.w], ALU.subtract).then_inc(expos, 1)
                    dve.wait_ge(lefts, g.n + 1)
                    nc.vector.tensor_tensor(expo[s][:, 0, 0:g.w], left[s][:, 0:g.w], top[s][:, 1:1 + g.w], ALU.subtract).then_inc(expos, 1)

                def spread(g):
                    s = g.slot(2)
                    dve.wait_ge(marked, g.n + 1)
                    dve.wait_ge(started, g.n + 1)
                    wait_from(dve, owned, g.n)
                    wait_from(dve, twice, g.n - 1)
                    nc.vector.tensor_tensor_scan(own[s][:, 0:g.w], p_mk[:, 0:g.w], starts[s][:, 0:g.w],
                                                 0.0 if g.zero else own[1 - s][:, W - 1:W], ALU.mult, ALU.add).then_inc(owned, 1)

                def attend(g):
                    s = g.slot(2)
                    dve.wait_ge(owned, g.n + 1)
                    dve.wait_ge(gotten, g.n + 1)
                    wait_from(dve, added, g.n - 1)
                    nc.vector.tensor_tensor(both[s][:, 0:g.w], own[s][:, 0:g.w], theirs[s][:, 0:g.w], ALU.add).then_inc(twice, 1)
                    dve.wait_ge(twice, g.n + 1)
                    dve.wait_ge(summed_ea, g.n + 1)
                    wait_from(dve, leaked, g.n - 1)
                    nc.vector.tensor_tensor(pre[s][:, 0:g.w], both[s][:, 0:g.w], p_pre[:, 0:g.w], ALU.add).then_inc(added, 1)
                    dve.wait_ge(added, g.n + 1)
                    wait_from(dve, scored, g.n - 1)
                    nc.vector.scalar_tensor_tensor(out=act_in[s][:, 0:g.w], in0=pre[s][:, 0:g.w], scalar=0.2, in1=pre[s][:, 0:g.w],
                                                   op0=ALU.mult, op1=ALU.max).then_inc(leaked, 1)

                def accumulate(g):
                    s = g.slot(2)
                    dve.wait_ge(grown, g.n + 1)
                    wait_from(dve, summed, g.n - 1)
                    nc.vector.tensor_tensor(weighted[s][:, 0:g.w], theirs[s][:, 0:g.w], grow[s][:, 1, 0:g.w], ALU.mult).then_inc(weighted_s, 1)
                    wait_from(dve, dens, g.n)
                    wait_from(dve, smalls, g.n - 1)
                    nc.vector.tensor_tensor_scan(den[s][:, 0:g.w], grow[s][:, 0, 0:g.w], grow[s][:, 1, 0:g.w],
                                                 0.0 if g.zero else den[1 - s][:, W - 1:W], ALU.mult, ALU.add).then_inc(dens, 1)
                    dve.wait_ge(weighted_s, g.n + 1)
                    wait_from(dve, rowed, g.n - 1)
                    wait_from(dve, summed, g.n)
                    nc.vector.tensor_tensor_scan(run[s][:, 0:g.w], grow[s][:, 0, 0:g.w], weighted[s][:, 0:g.w],
                                                 0.0 if g.zero else run[1 - s][:, W - 1:W], ALU.mult, ALU.add).then_inc(summed, 1)

                each_group(dve, (2, exponents), (0, spread), (1, attend), (2, accumulate))


def finish_4(nc, sb, ps, sem, X, info, t3, valid, bias3, g3, be3, out):
    with Stage(nc) as c:
        rows = sb(c, "rows", [P, NJ, T3])
        carry = sb(c, "carry", [P, T3])
        Y, Z = sb(c, "Y", [P, NJ, D]), sb(c, "Z", [P, NJ, D])
        BI, GA, BE = (sb(c, n, [P, D]) for n in ("BI", "GA", "BE"))
        inv = sb(c, "inv", [P, NJ])
        theirs, mx, dif, fac, scaled, denom, rden = (sb(c, n, [P, NJ, HEADS]) for n in ("theirs", "mx", "dif", "fac", "scaled", "denom", "rden"))
        dif2, fac2 = sb(c, "dif2", [P, NJ, HEADS]), sb(c, "fac2", [P, NJ, HEADS])
        part, mean, var, sd, rs = (sb(c, n, [P, D]) for n in ("part", "mean", "var", "sd", "rs"))
        ones = sb(c, "ones", [P, P])
        tot = ps(c, "tot", [P, 2 * D])
        cleared, rows_in, small_in, chain, fed, exped, totals, rooted = (
            sem(c, n) for n in ("cleared", "rows_in", "small_in", "chain", "fed", "exped", "totals", "rooted"))
        with nc.Block() as block:
            @block.sync
            def _(sp):
                sp.dma_start(carry[:, :], t3[H - 1:H, :].to_broadcast((P, T3))).then_inc(small_in, 16)
                for t, w in ((BI, bias3), (GA, g3), (BE, be3)):
                    sp.dma_start(t[:, :], row_of(w)).then_inc(small_in, 16)

            @block.gpsimd
            def _(pool):
                pool.wait_ge(cleared, 1)
                gather_rows(pool, nc, rows, T3, t3, info["last"], rows_in)

            @block.vector
            def _(dve):
                count = [0]

                def link(ins):
                    count[0] += 1
                    ins.then_inc(chain, 1)
                    dve.wait_ge(chain, count[0])

                def heads(t):
                    return t.unsqueeze(1).to_broadcast((P, NJ, HEADS))

                def spread_out(t):
                    return t[:, :, :].unsqueeze(3).to_broadcast((P, NJ, HEADS, HC))

                def split(t):
                    return t.rearrange("p j (a f) -> p j a f", a=HEADS)

                nc.vector.memset(rows[:, :, :], 0.0).then_inc(cleared, 1)
                link(nc.vector.memset(ones[:, :], 1.0))
                dve.wait_ge(rows_in, 16 * NJ)
                dve.wait_ge(small_in, 64)
                span = per_node(info["span"], HEADS)
                cmax = carry[:, D + HEADS:T3]
                link(nc.vector.tensor_scalar(inv[:, :], info["span"][:, :], -1.0, -NEG, ALU.add, ALU.mult))
                link(nc.vector.tensor_tensor(theirs[:, :, :], span, heads(cmax), ALU.mult))
                link(nc.vector.tensor_tensor(theirs[:, :, :], theirs[:, :, :], per_node(inv, HEADS), ALU.add))
                link(nc.vector.tensor_tensor(mx[:, :, :], theirs[:, :, :], rows[:, :, D + HEADS:T3], ALU.max))
                link(nc.vector.tensor_tensor(dif[:, :, :], rows[:, :, D + HEADS:T3], mx[:, :, :], ALU.subtract))
                link(nc.vector.tensor_tensor(dif2[:, :, :], theirs[:, :, :], mx[:, :, :], ALU.subtract))
                nc.vector.tensor_copy(inv[:, 0:1], info["span"][:, 0:1]).then_inc(fed, 1)
                dve.wait_ge(exped, 2)
                link(nc.vector.tensor_tensor(denom[:, :, :], rows[:, :, D:D + HEADS], fac[:, :, :], ALU.mult))
                link(nc.vector.tensor_tensor(scaled[:, :, :], fac2[:, :, :], heads(carry[:, D:D + HEADS]), ALU.mult))
                link(nc.vector.tensor_tensor(denom[:, :, :], denom[:, :, :], scaled[:, :, :], ALU.add))
                link(nc.vector.tensor_scalar(denom[:, :, :], denom[:, :, :], 1e-16, None, ALU.add))
                link(nc.vector.reciprocal(rden[:, :, :], denom[:, :, :]))
                link(nc.vector.tensor_tensor(split(Y[:, :, :]), split(rows[:, :, 0:D]), spread_out(fac), ALU.mult))
                link(nc.vector.tensor_tensor(split(Z[:, :, :]), carry[:, 0:D].unsqueeze(1).to_broadcast((P, NJ, D)).rearrange("p j (a f) -> p j a f", a=HEADS),
                                             spread_out(fac2), ALU.mult))
                link(nc.vector.tensor_tensor(Y[:, :, :], Y[:, :, :], Z[:, :, :], ALU.add))
                link(nc.vector.tensor_tensor(split(Z[:, :, :]), split(Y[:, :, :]), spread_out(rden), ALU.mult))
                link(nc.vector.tensor_tensor(Y[:, :, :], Z[:, :, :], per_feature(BI), ALU.add))

                def total(t, n):
                    link(nc.vector.tensor_reduce(part[:, :], t[:, :, :].rearrange("p j f -> p f j"), AX.X, ALU.add))
                    nc.vector.tensor_copy(inv[:, 1:2], info["span"][:, 1:2]).then_inc(fed, 1)
                    dve.wait_ge(totals, n)

                link(nc.vector.tensor_tensor(Z[:, :, :], Y[:, :, :], per_node(valid), ALU.mult))
                total(Z, 1)
                link(nc.vector.tensor_scalar(mean[:, :], tot[:, 0:D], 1.0 / N, None, ALU.mult))
                link(nc.vector.tensor_tensor(Y[:, :, :], Y[:, :, :], per_feature(mean), ALU.subtract))
                link(nc.vector.tensor_tensor(Z[:, :, :], Y[:, :, :], per_node(valid), ALU.mult))
                link(nc.vector.tensor_tensor(Z[:, :, :], Z[:, :, :], Y[:, :, :], ALU.mult))
                total(Z, 2)
                link(nc.vector.tensor_scalar(var[:, :], tot[:, D:2 * D], 1.0 / N, EPS, ALU.mult, ALU.add))
                nc.vector.tensor_copy(inv[:, 2:3], info["span"][:, 2:3]).then_inc(fed, 1)
                dve.wait_ge(rooted, 1)
                link(nc.vector.reciprocal(rs[:, :], sd[:, :]))
                link(nc.vector.tensor_tensor(rs[:, :], rs[:, :], GA[:, :], ALU.mult))
                link(nc.vector.tensor_tensor(Y[:, :, :], Y[:, :, :], per_feature(rs), ALU.mult))
                link(nc.vector.tensor_tensor(Y[:, :, :], Y[:, :, :], per_feature(BE), ALU.add))
                link(nc.vector.tensor_tensor(Z[:, :, :], Y[:, :, :], X[:, :, :], ALU.add))
                nc.vector.tensor_copy(inv[:, 3:4], info["span"][:, 3:4]).then_inc(fed, 1)
                dve.wait_ge(rooted, 2)
                link(nc.vector.tensor_tensor(Z[:, :, :], Y[:, :, :], X[:, :, :], ALU.add))

            @block.tensor
            def _(pe):
                for n in range(2):
                    pe.wait_ge(fed, 2 + n)
                    nc.tensor.matmul(tot[:, n * D:(n + 1) * D], ones[:, :], part[:, :], start=True, stop=True).then_inc(totals, 1)

            @block.scalar
            def _(act):
                act.wait_ge(fed, 1)
                nc.scalar.activation(fac[:, :, :], dif[:, :, :], ACT.Exp).then_inc(exped, 1)
                nc.scalar.activation(fac2[:, :, :], dif2[:, :, :], ACT.Exp).then_inc(exped, 1)
                act.wait_ge(fed, 4)
                nc.scalar.activation(sd[:, :], var[:, :], ACT.Sqrt).then_inc(rooted, 1)
                act.wait_ge(fed, 5)
                nc.scalar.activation(Y[:, :, :], Z[:, :, :], ACT.Gelu).then_inc(rooted, 1)

        norm(nc, sb, sem, [], Z, Y, [])
        written = sem(c, "written")
        with nc.Block() as block:
            @block.sync
            def _(sp):
                for s, j, rows_out in node_rows(out):
                    sp.dma_start(rows_out, Y[s, 0:j, :]).then_inc(written, 16)
                sp.wait_ge(written, 48)


_INS = {"x": "x", "src": "src", "dst": "dst", "ea16": "edge_attr_16", "ea64": "edge_attr_64", "ew": "edge_weight1",
        "w0a": "L0_gnn_W1", "b0a": "L0_gnn_b1", "w0b": "L0_gnn_W2", "b0b": "L0_gnn_b2",
        "u1": "L1_gnn_u", "w1a": "L1_gnn_W1", "b1a": "L1_gnn_b1", "w1b": "L1_gnn_W2", "b1b": "L1_gnn_b2",
        "g1": "L1_gnn_gamma", "be1": "L1_gnn_beta",
        "w2a": "L2_gnn_W1", "b2a": "L2_gnn_b1", "w2b": "L2_gnn_W2", "b2b": "L2_gnn_b2", "w2g": "L2_gnn_Wg", "b2g": "L2_gnn_bg",
        "wl": "L3_gnn_W_l", "bl": "L3_gnn_b_l", "wr": "L3_gnn_W_r", "br": "L3_gnn_b_r", "we": "L3_gnn_W_e",
        "att": "L3_gnn_att", "bias3": "L3_gnn_bias", "g3": "L3_gnn_gamma", "be3": "L3_gnn_beta"}


def kernel(**inputs):
    import numpy as _np
    import concourse.bacc as _bacc
    from concourse import mybir as _mybir
    from concourse.bass_utils import run_bass_kernel_spmd as _run

    nc = _bacc.Bacc("TRN2", target_bir_lowering=False, num_devices=1)
    arrays, args = {}, {}
    for name, given in _INS.items():
        a = _np.ascontiguousarray(inputs[given])
        if name in ("src", "dst"):
            a = a.reshape(-1, 1)
        arrays[f"in_{name}_dram"] = a
        args[name] = nc.dram_tensor(f"in_{name}_dram", a.shape, _mybir.dt.from_np(a.dtype), kind="ExternalInput").ap()
    args["out"] = nc.dram_tensor("out_0_dram", (N, D), F32, kind="ExternalOutput").ap()
    build(nc, **args)
    r = _run(nc, [arrays], core_ids=[0])
    return r.results[0]["out_0_dram"]
```

```python
import itertools
import numpy as np
import concourse.bass as bass
from concourse import mybir
from contextlib import ExitStack

F32 = mybir.dt.float32
I32 = mybir.dt.int32
BF16 = mybir.dt.bfloat16
ALU = mybir.AluOpType
ACT = mybir.ActivationFunctionType
AX = mybir.AxisListType
ds = bass.ds

P = 128
N = 6250
E = 200000
D = 64
H = E // 2
NJ = -(-N // P)
NP = P * NJ
FULLP, LASTJ = N // NJ, N % NJ
W = 512
C = 4
NG = H // W
TAIL = H - NG * W
AHEAD = 4
LAG = 3
UNROLL = 4
SEARCH_ROWS, SEARCH_KEYS = 35, 65
SR, SC = 64, E // 64
KR, KC, KT = 1600, 125, 40
NONE = 1 << 20
NEG = -2.0 ** 126
EPS = 1e-5
HEADS, HC, ED = 4, 16, 16
LOGN = 18
SF = (1 << LOGN) // P
SB = 13
KEYBASE = 1 << 29
T3 = 72


class Stage(ExitStack):

    def __init__(self, nc):
        super().__init__()
        self.nc, self.sems = nc, []

    def __exit__(self, *what):
        if self.sems and what[0] is None:
            self.nc.clear_and_free_semaphores(self.sems)
            self.nc.all_engine_barrier()
        return super().__exit__(*what)


class Group:

    def __init__(self, it, base):
        self.it, self.base = it, base
        self.n = base if it is None else it * UNROLL + base
        self.row = self.n * W
        self.w = TAIL if it is None and base == NG else W
        self.p = self.w // C
        self.zero = it is None and base == 0
        self.late = it is None and base + LAG > NG

    def slot(self, slots):
        return self.base % slots

    def turn(self, slots):
        return self.base // slots if self.it is None else self.it * (UNROLL // slots) + self.base // slots


def run_ticks(eng, a, b, steps):
    def tick(t):
        for lag, step in steps:
            if 0 <= t - lag <= NG:
                step(Group(None, t - lag))

    end = min(b, NG)
    count = max(end - max(a, LAG + AHEAD), 0) // UNROLL
    if count < 2:
        count, end = 0, b
    for t in range(a, end - count * UNROLL):
        tick(t)
    if count:
        with eng.Fori(0, count) as i:
            it = eng.snap(i)
            for t in range(end - count * UNROLL, end - (count - 1) * UNROLL):
                for lag, step in steps:
                    step(Group(it, t - lag))
        for t in range(end, b):
            tick(t)


def each_group(eng, *steps):
    run_ticks(eng, 0, NG + 1 + max(lag for lag, _ in steps), steps)


def wait_from(eng, sem, value):
    if not isinstance(value, int) or value > 0:
        eng.wait_ge(sem, value)


def snapped(eng, value):
    return value if isinstance(value, int) else eng.snap(value)


def by_edge(table, h, row, width):
    half = table[h * H:(h + 1) * H, :][ds(row, width), :]
    return half.rearrange("(p c) f -> p c f", c=C)


def both_halves(table, row, width):
    rows = table.rearrange("(h r) f -> r h f", h=2)[ds(row, width), :, :]
    return rows.rearrange("(p c) h f -> p h c f", c=C)


def indices_of(table, row, width):
    return table.rearrange("(h r) o -> r (h o)", h=2)[ds(row, width), :].rearrange("(p c) h -> p h c", c=C)


def by_place(t, g):
    return t[:, 0:g.w].rearrange("q (p c) -> q p c", c=C)


def by_block(bank, g, q=P):
    return bank[0:q, :].rearrange("q (c p) -> q p c", c=C)[:, 0:g.p, :]


def turn_to_features(nc, bank, by_edges, g, ident, q=P):
    for cc in range(C):
        mm = nc.tensor.transpose(bank[0:q, cc * P:cc * P + g.p], by_edges[0:g.p, cc, :, :].rearrange("p h f -> p (h f)"), ident[0:g.p, 0:g.p])
    return mm


def turn_to_edges(nc, bank, t, g, ident):
    for cc in range(C):
        mm = nc.tensor.transpose(bank[0:g.p, cc, :], by_place(t, g)[:, :, cc], ident[:, :])
    return mm


def build(nc, x, src, dst, ea16, ea64, ew, w0a, b0a, w0b, b0b, u1, w1a, b1a, w1b, b1b, g1, be1,
          w2a, b2a, w2b, b2b, w2g, b2g, wl, bl, wr, br, we, att, bias3, g3, be3, out):
    ctx = ExitStack()
    with ctx:
        def dram(name, shape, dt):
            return nc.dram_tensor(name, shape, dt, kind="Internal").ap()

        t1 = dram("t1", [E, 2 * D], F32)
        t2 = dram("t2", [E, D], F32)
        t3 = dram("t3", [E, T3], F32)
        start2 = dram("start2", [E, D], F32)
        start3 = dram("start3", [E, D], F32)
        wsum = dram("wsum", [E, 1], F32)
        srcs = dram("srcs", [E, 1], I32)
        dsts = dram("dsts", [E, 1], I32)
        rowlast = [dram(f"rowlast{o}", [KT, KT], I32) for o in range(2)]
        marks = dram("marks", [2, 2, 2, H], BF16)
        tabg = [dram(f"tabg{i}", [NP, D], F32) for i in range(2)]
        tabs = [dram(f"tabs{i}", [NP, D], F32) for i in range(2)]

        serial = itertools.count()

        def sb(c, name, shape, dt=F32):
            return c.enter_context(nc.sbuf_tensor(f"{name}_{next(serial)}", shape, dt))

        def ps(c, name, shape, dt=F32):
            return c.enter_context(nc.psum_tensor(f"{name}_{next(serial)}", shape, dt))

        def sem(c, name):
            c.sems.append(nc.alloc_semaphore(f"{name}_{next(serial)}"))
            return c.sems[-1]

        X = sb(ctx, "X", [P, NJ, D])
        ident = sb(ctx, "ident", [P, P])
        nid = sb(ctx, "nid", [P, NJ])
        valid = sb(ctx, "valid", [P, NJ])
        sel2 = sb(ctx, "sel2", [2, P], BF16)
        wn = sb(ctx, "wn", [P, NJ, 1])
        order = [{k: sb(ctx, f"{k}{o}", [P, NJ], dt) for k, dt in
                  (("first", I32), ("last", I32), ("span", F32), ("cnt", F32))} for o in range(2)]

        with Stage(nc) as c:
            si, di = (sb(c, n, [P, SF], I32) for n in ("si", "di"))
            flip = sb(c, "flip", [P, LOGN - ROW + 1])
            ends = Ends(nc, sb, ps, sem, c, 0, dst, order[0], nid, rowlast)
            with Stage(nc) as cc:
                setup(nc, sb, ps, sem, x, src, dst, X, ident, nid, valid, sel2, si, di, flip,
                      Marks(nc, sb, ps, sem, cc, 0, dst, marks, ident, ew, wsum), ends)
            sort_and_edge_sums(nc, sb, ps, sem, si, di, flip, srcs, dsts, ends, ea64, marks, t1, wsum, wn, ident, sel2)
        with Stage(nc) as c:
            blank = Blank(nc, sb, sem, c, start2)
            node_layers_1_2(nc, sb, ps, sem, X, order, nid, srcs, marks, rowlast, blank, t1, wn, ident, w0a, b0a, w0b, b0b, u1,
                            w1a, b1a, w1b, b1b, g1, be1)
            node_tables(nc, sb, ps, sem, X, order[1], srcs, (w2a[D:2 * D, :], b2a), (w2a[0:D, :], None),
                        tabg[0], tabs[0], start2, ident, blank)
        edges_3(nc, sb, ps, sem, dsts, marks, tabg[0], start2, start3, t2, ident, sel2, w2b, b2b, w2g, b2g)
        pool_3(nc, sb, ps, sem, X, order[1], t2)
        node_tables(nc, sb, ps, sem, X, order[0], dst, (wl, bl), (wr, br), tabg[1], tabs[1], start3, ident)
        edges_4(nc, sb, ps, sem, src, ea16, marks, tabg[1], start3, t3, ident, sel2, we, att)
        finish_4(nc, sb, ps, sem, X, order[0], t3, valid, bias3, g3, be3, out)


def node_rows(flat):
    cut = FULLP // 16 * 16
    for a, b in ((0, cut), (cut, FULLP)):
        yield slice(a, b), NJ, flat[a * NJ:b * NJ, :].rearrange("(p j) f -> p j f", j=NJ)
    yield slice(FULLP, FULLP + 1), LASTJ, flat[FULLP * NJ:N, :].rearrange("(p j) f -> p j f", j=LASTJ)



ROW = LOGN - 7


def network():
    for k in range(1, LOGN + 1):
        if k >= ROW:
            yield "sign", k
        if k > ROW:
            yield "turn", k
            for j in range(k - 1, ROW - 1, -1):
                yield "step", k, j - ROW
            yield "turn", k
        for j in range(min(k, ROW) - 1, -1, -1):
            yield "step", k, j


def ops_before_turns():
    n, out = 2, []
    for what in network():
        if what[0] == "turn":
            out.append(n)
        else:
            n += 1 if what[0] == "sign" else (4 if what[1] < ROW else 2)
    return out


def setup(nc, sb, ps, sem, x, src, dst, X, ident, nid, valid, sel2, si, di, flip, marks, ends):
    with Stage(nc) as c:
        nodei = sb(c, "nodei", [P, NJ], I32)
        parti = sb(c, "parti", [P, 1], I32)
        bits = sb(c, "bits", [P, LOGN - ROW + 2], I32)
        sign = sb(c, "sign", [P, LOGN - ROW + 2])
        ones2, sel2f, sel2g = (sb(c, n, [2, P]) for n in ("ones2", "sel2f", "sel2g"))
        zerop = sb(c, "zerop", [P, P])
        made, consts, cleared, nodes_in, pairs_in = (sem(c, n) for n in ("made", "consts", "cleared", "nodes_in", "pairs_in"))
        with nc.Block() as block:
            @block.sync
            def _(sp):
                marks.load(sp)
                ends.load(sp)
                ends.store(sp)
                sp.wait_ge(cleared, 2)
                for t, k in ((si, src), (di, dst)):
                    for part, rows in sort_rows(k):
                        sp.dma_start(t[part, 0:rows.shape[1]], rows).then_inc(pairs_in, 16)
                sp.wait_ge(cleared, 3)
                for s, j, rows in node_rows(x):
                    sp.dma_start(X[s, 0:j, :], rows).then_inc(nodes_in, 16)
                marks.store(sp)
                sp.wait_ge(pairs_in, 96)
                sp.wait_ge(nodes_in, 48)

            @block.gpsimd
            def _(pool):
                nc.gpsimd.memset(zerop[:, :], 0.0).then_inc(made, 1)
                nc.gpsimd.memset(ones2[:, :], 1.0).then_inc(made, 1)
                nc.gpsimd.iota(nodei[:, :], pattern=[[1, NJ]], base=0, channel_multiplier=NJ).then_inc(made, 1)
                nc.gpsimd.iota(parti[:, :], pattern=[[0, 1]], base=0, channel_multiplier=1).then_inc(made, 1)
                pool.wait_ge(made, 4)
                nc.gpsimd.affine_select(out=ident[:, :], in_=zerop[:, :], compare_op=ALU.not_equal, fill=1.0, base=0,
                                        pattern=[[-1, P]], channel_multiplier=1).then_inc(made, 1)
                nc.gpsimd.affine_select(out=sel2g[:, :], in_=ones2[:, :], compare_op=ALU.is_ge, fill=0.0, base=0,
                                        pattern=[[1, P]], channel_multiplier=-D).then_inc(made, 1)
                pool.wait_ge(made, 6)
                nc.gpsimd.affine_select(out=sel2f[:, :], in_=sel2g[:, :], compare_op=ALU.is_ge, fill=0.0, base=D - 1,
                                        pattern=[[-1, P]], channel_multiplier=D).then_inc(made, 1)

            @block.vector
            def _(dve):
                nc.vector.memset(si[:, :], (1 << SB) - 1).then_inc(cleared, 1)
                nc.vector.memset(di[:, :], (1 << SB) - 1).then_inc(cleared, 1)
                nc.vector.memset(X[:, :, :], 0.0).then_inc(cleared, 1)
                nc.vector.memset(bits[:, :], 0).then_inc(consts, 1)
                dve.wait_ge(made, 7)
                nc.vector.tensor_copy(sel2[:, :], sel2f[:, :]).then_inc(consts, 1)
                nc.vector.tensor_copy(nid[:, :], nodei[:, :]).then_inc(consts, 1)
                dve.wait_ge(consts, 3)
                nc.vector.tensor_scalar(valid[:, :], nid[:, :], float(N), None, ALU.is_lt).then_inc(consts, 1)
                for k in range(ROW, LOGN):
                    at = k - ROW + 1
                    nc.vector.tensor_scalar(bits[:, at:at + 1], parti[:, :], k - ROW, 1, ALU.logical_shift_right,
                                            ALU.bitwise_and).then_inc(consts, 1)
                dve.wait_ge(consts, 4 + LOGN - ROW)
                nc.vector.tensor_scalar(sign[:, :], bits[:, :], -2.0, 1.0, ALU.mult, ALU.add).then_inc(consts, 1)
                dve.wait_ge(consts, 5 + LOGN - ROW)
                nc.vector.tensor_tensor(flip[:, :], sign[:, 0:LOGN - ROW + 1], sign[:, 1:LOGN - ROW + 2], ALU.mult).then_inc(consts, 1)
                marks.compare(dve)
                ends.count_blocks(dve)
                marks.weigh(dve)

            @block.tensor
            def _(pe):
                pe.wait_ge(made, 5)
                marks.turn(pe)


def sort_rows(flat):
    full, rest = E // SF, E % SF
    cut = full // 16 * 16
    for a, b in ((0, cut), (cut, full)):
        yield slice(a, b), flat[a * SF:b * SF, :].rearrange("(p f) o -> p (f o)", f=SF)
    yield slice(full, full + 1), flat[full * SF:full * SF + rest, :].rearrange("(p f) o -> p (f o)", p=1)


def sort_and_edge_sums(nc, sb, ps, sem, si, di, flip, srcs, dsts, ends, ea64, marks, t1, wsum, wn, ident, sel2):
    steps = list(network())
    turns_at = [i for i, what in enumerate(steps) if what[0] == "turn"]
    TURNS = ops_before_turns()
    with Stage(nc) as c:
        ka, kb = (sb(c, n, [P, SF]) for n in ("ka", "kb"))
        wn_cleared, wn_in = sem(c, "wn_cleared"), sem(c, "wn_in")
        ea = [sb(c, f"ea{i}", [P, C, 2, D]) for i in range(AHEAD)]
        mk = [sb(c, f"mk{i}", [2, 2, W], BF16) for i in range(AHEAD)]
        feat = [sb(c, f"feat{i}", [P, W]) for i in range(2)]
        run = [[sb(c, f"run{k}{i}", [P, W]) for i in range(2)] for k in range(2)]
        rows = [sb(c, f"rows{i}", [P, 2, C, 2, D]) for i in range(2)]
        p_keys = [ps(c, f"p_keys{i}", [P, 4 * P]) for i in range(2)]
        p_in = [ps(c, f"p_in{i}", [P, C * P]) for i in range(2)]
        p_mk = [ps(c, f"p_mk{k}", [P, W]) for k in range(2)]
        p_out = [ps(c, f"p_out{k}", [P, C, P]) for k in range(2)]
        step, turned_keys, back, split, sorted_out = (sem(c, n) for n in ("step", "turned_keys", "back", "split", "sorted_out"))
        ea_in = [sem(c, f"ea_in{i}") for i in range(AHEAD)]
        stored = [sem(c, f"stored{i}") for i in range(2)]
        turned, spread, feats, summed, maxed, rowed, drained = (
            sem(c, n) for n in ("turned", "spread", "feats", "summed", "maxed", "rowed", "drained"))
        scanned = (summed, maxed)

        def keys_at(turn):
            return (kb, ka) if turns_at[turn] % 2 == 0 else (ka, kb)

        def between_turns(eng, groups, turn):
            a = 0
            for t, at in enumerate(turns_at):
                run_ticks(eng, a, at + 1, groups)
                turn(t)
                a = at + 1
            run_ticks(eng, a, NG + 1 + max(lag for lag, _ in groups), groups)

        with nc.Block() as block:
            @block.sync
            def _(sp):
                def load(g):
                    s, row = g.slot(AHEAD), snapped(sp, g.row)
                    wait_from(sp, spread, g.n - AHEAD + 1)
                    for h in range(2):
                        sp.dma_start(ea[s][0:g.p, :, h, :], by_edge(ea64, h, row, g.w)).then_inc(ea_in[s], 16)
                    sp.dma_start(mk[s][:, :, 0:g.w], marks[0][:, :, ds(row, g.w)]).then_inc(ea_in[s], 16)

                each_group(sp, (0, load))
                sp.wait_ge(split, 2)
                for t, k in ((si, srcs), (di, dsts)):
                    for part, out in sort_rows(k):
                        sp.dma_start(out, t[part, 0:out.shape[1]]).then_inc(sorted_out, 16)
                sp.wait_ge(sorted_out, 96)

            @block.gpsimd
            def _(pool):
                ends.clear()
                ends.fetch_rows(pool)
                ends.fetch_keys(pool)
                nc.gpsimd.memset(wn[:, :, :], 0.0).then_inc(wn_cleared, 1)
                pool.wait_ge(wn_cleared, 1)
                pool.wait_ge(ends.v, 23)
                gather_rows(pool, nc, wn, 1, wsum, ends.info["last"], wn_in)
                pool.wait_ge(wn_in, 16 * NJ)

            @block.vector
            def _(dve):
                def scan(g):
                    s = g.slot(2)
                    dve.wait_ge(spread, g.n + 1)
                    dve.wait_ge(feats, g.n + 1)
                    wait_from(dve, rowed, 2 * g.n - 2)
                    for kind, (op0, op1, initial) in enumerate(((ALU.mult, ALU.add, 0.0), (ALU.add, ALU.max, NEG))):
                        if not g.zero:
                            dve.wait_ge(scanned[kind], g.n)
                            initial = run[kind][1 - s][:, W - 1:W]
                        nc.vector.tensor_tensor_scan(run[kind][s][:, 0:g.w], p_mk[kind][:, 0:g.w], feat[s][:, 0:g.w],
                                                     initial, op0, op1).then_inc(scanned[kind], 1)

                nc.vector.tensor_scalar(ka[:, :].bitcast(I32), si[:, :], SB, KEYBASE, ALU.logical_shift_left,
                                        ALU.bitwise_or).then_inc(step, 1)
                dve.wait_ge(step, 1)
                nc.vector.tensor_tensor(kb[:, :].bitcast(I32), ka[:, :].bitcast(I32), di[:, :], ALU.bitwise_or).then_inc(step, 1)
                done = 2
                now, then, turns = kb, ka, 0
                for i, what in enumerate(steps):
                    if what[0] == "turn":
                        turns += 1
                        scan(Group(None, i))
                        dve.wait_ge(back, 4 * turns)
                    else:
                        dve.wait_ge(step, done)
                        if what[0] == "sign":
                            at = what[1] - ROW
                            nc.vector.tensor_scalar(then[:, :], now[:, :], flip[:, at:at + 1], None, ALU.mult).then_inc(step, 1)
                            done += 1
                        elif what[1] < ROW:
                            k, i2 = what[1:]
                            a, b = (z[:, :].rearrange("p (n d s l i) -> p n d s l i", d=2, s=1 << (k - i2 - 1), l=2, i=1 << i2) for z in (now, then))
                            for d, (low, high) in enumerate(((ALU.min, ALU.max), (ALU.max, ALU.min))):
                                for side, op in ((0, low), (1, high)):
                                    nc.vector.tensor_tensor(b[:, :, d, :, side, :], a[:, :, d, :, 0, :], a[:, :, d, :, 1, :], op).then_inc(step, 1)
                            done += 4
                        else:
                            a, b = (z[:, :].rearrange("p (n l i) -> p n l i", l=2, i=1 << what[2]) for z in (now, then))
                            for side, op in ((0, ALU.min), (1, ALU.max)):
                                nc.vector.tensor_tensor(b[:, :, side, :], a[:, :, 0, :], a[:, :, 1, :], op).then_inc(step, 1)
                            done += 2
                        scan(Group(None, i))
                    now, then = then, now
                    if i == SEARCH_ROWS:
                        ends.count_rows(dve)
                    if i == SEARCH_KEYS:
                        ends.count_keys(dve)
                    if i == SEARCH_KEYS + 3:
                        ends.finish(dve)
                dve.wait_ge(step, done)
                ki = now[:, :].bitcast(I32)
                nc.vector.tensor_scalar(si[:, :], ki, SB, (1 << SB) - 1, ALU.logical_shift_right, ALU.bitwise_and).then_inc(split, 1)
                nc.vector.tensor_scalar(di[:, :], ki, (1 << SB) - 1, None, ALU.bitwise_and).then_inc(split, 1)
                for n in range(len(steps), NG + 1):
                    scan(Group(None, n))

            @block.tensor
            def _(pe):
                def spread_and_turn(g):
                    s, t = g.slot(AHEAD), g.slot(2)
                    pe.wait_ge(ea_in[s], 48 * g.turn(AHEAD) + 48)
                    wait_from(pe, feats, g.n - 1)
                    turn_to_features(nc, p_in[t], ea[s], g, ident).then_inc(turned, 1)
                    wait_from(pe, maxed, g.n)
                    for kind in range(2):
                        mm = nc.tensor.matmul(p_mk[kind][:, 0:g.w], sel2[:, :], mk[s][:, kind, 0:g.w], start=True, stop=True)
                    mm.then_inc(spread, 1)

                def turn_back(g):
                    for kind in range(2):
                        pe.wait_ge(scanned[kind], g.n + 1)
                        wait_from(pe, drained, 2 * g.n + kind - 1)
                        turn_to_edges(nc, p_out[kind], run[kind][g.slot(2)], g, ident).then_inc(rowed, 1)

                def turn_keys(t):
                    pe.wait_ge(step, TURNS[t])
                    now, _ = keys_at(t)
                    for q in range(4):
                        wait_from(pe, back, 4 * t + q - 1)
                        for j in range(4 * q, 4 * q + 4):
                            mm = nc.tensor.transpose(p_keys[q % 2][:, j % 4 * P:(j % 4 + 1) * P], now[:, j * P:(j + 1) * P], ident[:, :])
                        mm.then_inc(turned_keys, 1)

                between_turns(pe, [(0, spread_and_turn), (1, turn_back)], turn_keys)

            @block.scalar
            def _(act):
                def to_order(g):
                    act.wait_ge(turned, g.n + 1)
                    wait_from(act, maxed, g.n - 1)
                    nc.scalar.activation(by_place(feat[g.slot(2)], g), by_block(p_in[g.slot(2)], g), ACT.Copy).then_inc(feats, 1)

                def to_rows(g):
                    s = g.slot(2)
                    wait_from(act, stored[s], 16 * g.turn(2))
                    for kind in range(2):
                        act.wait_ge(rowed, 2 * g.n + kind + 1)
                        nc.scalar.activation(rows[s][0:g.p, :, :, kind, :].rearrange("p h c f -> p c h f"),
                                             p_out[kind][0:g.p, :, :].rearrange("p c (h f) -> p c h f", h=2), ACT.Copy).then_inc(drained, 1)
                    act.wait_ge(drained, 2 * g.n + 2)
                    act.dma_start(both_halves(t1, g.row, g.w), rows[s][0:g.p, :, :, :, :].rearrange("p h c k f -> p h (c k f)")).then_inc(stored[s], 16)

                def keys_back(t):
                    _, then = keys_at(t)
                    for q in range(4):
                        act.wait_ge(turned_keys, 4 * t + q + 1)
                        nc.scalar.activation(then[:, q * 512:(q + 1) * 512], p_keys[q % 2][:, :], ACT.Copy).then_inc(back, 1)

                between_turns(act, [(0, to_order), (1, to_rows)], keys_back)
                for s in range(2):
                    act.wait_ge(stored[s], 16 * ((NG + 2 - s) // 2))


class Marks:

    def __init__(self, nc, sb, ps, sem, c, o, key, marks, ident, ew=None, wsum=None):
        self.nc, self.o, self.flat, self.marks, self.ident, self.ew, self.wsum = nc, o, key.rearrange("e o -> (e o)"), marks, ident, ew, wsum
        self.edge = sb(c, "edge", [SR, SC + 1], I32)
        self.mark = sb(c, "mark", [SR, SC])
        self.mark16, self.reset16 = (sb(c, n, [SR, SC], BF16) for n in ("mark16", "reset16"))
        self.edges_in, self.marked, self.marks_out, self.compared = (sem(c, n) for n in ("edges_in", "marked", "marks_out", "compared"))
        if ew is not None:
            self.wt, self.wrun, self.wprod, self.wall = (sb(c, n, [SR, SC]) for n in ("wt", "wrun", "wprod", "wall"))
            self.crow = sb(c, "crow", [1, 2 * SR])
            self.cscan = sb(c, "cscan", [1, SR + 1])
            self.ccol = sb(c, "ccol", [SR, 1])
            self.pe1 = ps(c, "pe1", [1, 2 * SR])
            self.pe2 = ps(c, "pe2", [SR, 1])
            self.w_in, self.carries, self.cback, self.cturn, self.walls, self.w_out = (
                sem(c, n) for n in ("w_in", "carries", "cback", "cturn", "walls", "w_out"))

    def load(self, sp):
        rows = self.flat.rearrange("(p f) -> p f", f=SC)
        sp.dma_start(self.edge[:, 1:SC + 1], rows).then_inc(self.edges_in, 16)
        with self.nc.allow_non_contiguous_dma(reason="one key of each row"):
            sp.dma_start(self.edge[1:SR, 0:1], rows[0:SR - 1, SC - 1:SC]).then_inc(self.edges_in, 16)
        if self.ew is not None:
            sp.dma_start(self.wt[:, :], self.ew.rearrange("(p f) o -> p (f o)", f=SC)).then_inc(self.w_in, 16)

    def store(self, sp):
        sp.wait_ge(self.marked, 2)
        for h in range(2):
            for kind, t in enumerate((self.mark16, self.reset16)):
                sp.dma_start(self.marks[self.o, h, kind].rearrange("(p f) -> p f", f=SC), t[h * SR // 2:(h + 1) * SR // 2, :]).then_inc(self.marks_out, 16)
        if self.ew is not None:
            sp.wait_ge(self.walls, 3)
            sp.dma_start(self.wsum.rearrange("(p f) o -> p (f o)", f=SC), self.wall[:, :]).then_inc(self.w_out, 16)
            sp.wait_ge(self.w_out, 16)
        sp.wait_ge(self.marks_out, 64)

    def compare(self, dve):
        nc = self.nc
        nc.vector.memset(self.edge[0:1, 0:1], -1).then_inc(self.compared, 1)
        dve.wait_ge(self.compared, 1)
        dve.wait_ge(self.edges_in, 32)
        nc.vector.tensor_tensor(self.mark[:, :], self.edge[:, 1:SC + 1], self.edge[:, 0:SC], ALU.is_equal).then_inc(self.compared, 1)
        dve.wait_ge(self.compared, 2)
        nc.vector.tensor_copy(self.mark16[:, :], self.mark[:, :]).then_inc(self.marked, 1)
        nc.vector.tensor_scalar(self.reset16[:, :], self.mark[:, :], -1.0, -NEG, ALU.add, ALU.mult).then_inc(self.marked, 1)

    def weigh(self, dve):
        nc = self.nc
        dve.wait_ge(self.w_in, 16)
        nc.vector.tensor_tensor_scan(self.wrun[:, :], self.mark[:, :], self.wt[:, :], 0.0, ALU.mult, ALU.add).then_inc(self.carries, 1)
        nc.vector.tensor_tensor_scan(self.wprod[:, :], self.mark[:, :], self.mark[:, :], 1.0, ALU.mult, ALU.min).then_inc(self.carries, 1)
        nc.vector.memset(self.cscan[:, 0:1], 0.0).then_inc(self.walls, 1)
        dve.wait_ge(self.cturn, 1)
        nc.vector.tensor_copy(self.crow[:, :], self.pe1[:, :]).then_inc(self.cback, 1)
        dve.wait_ge(self.cback, 1)
        dve.wait_ge(self.walls, 1)
        nc.vector.tensor_tensor_scan(self.cscan[:, 1:SR + 1], self.crow[:, SR:2 * SR], self.crow[:, 0:SR], 0.0, ALU.mult, ALU.add).then_inc(self.cback, 1)
        dve.wait_ge(self.cturn, 2)
        nc.vector.tensor_copy(self.ccol[:, :], self.pe2[:, :]).then_inc(self.walls, 1)
        dve.wait_ge(self.walls, 2)
        nc.vector.scalar_tensor_tensor(out=self.wall[:, :], in0=self.wprod[:, :], scalar=self.ccol[:, 0:1], in1=self.wrun[:, :],
                                       op0=ALU.mult, op1=ALU.add).then_inc(self.walls, 1)

    def turn(self, pe):
        nc = self.nc
        pe.wait_ge(self.carries, 2)
        nc.tensor.matmul(self.pe1[:, 0:SR], self.wrun[:, SC - 1:SC], self.ident[0:SR, 0:SR], start=True, stop=True)
        nc.tensor.matmul(self.pe1[:, SR:2 * SR], self.wprod[:, SC - 1:SC], self.ident[0:SR, 0:SR], start=True, stop=True).then_inc(self.cturn, 1)
        pe.wait_ge(self.cback, 2)
        nc.tensor.matmul(self.pe2[:, :], self.cscan[:, 0:SR], self.ident[0:1, 0:1], start=True, stop=True).then_inc(self.cturn, 1)


class Ends:

    def __init__(self, nc, sb, ps, sem, c, o, key, info, nid, rowlast):
        self.nc, self.key, self.info, self.nid, self.rowlast = nc, key, info, nid, rowlast[o]
        self.top = sb(c, "top", [P, KT], I32)
        self.low = sb(c, "low", [KT, KT], I32)
        self.rows1 = sb(c, "rows1", [P, NJ, KT], I32)
        self.rows2 = sb(c, "rows2", [P, NJ, KC], I32)
        self.hits = sb(c, "hits", [P, NJ, KC])
        self.below1, self.below2, self.below3, self.row, self.upto, self.before = (
            sb(c, n, [P, NJ]) for n in ("below1", "below2", "below3", "row", "upto", "before"))
        self.index1, self.index2 = (sb(c, n, [P, NJ], I32) for n in ("index1", "index2"))
        self.has, self.f1, self.f2, self.l1, self.l2, self.s1, self.s2 = (
            sb(c, n, [P, NJ]) for n in ("has", "f1", "f2", "l1", "l2", "s1", "s2"))
        self.tops_in, self.lows, self.prefill, self.rows_in, self.keys_in, self.v, self.shifted = (
            sem(c, n) for n in ("tops_in", "lows", "prefill", "rows_in", "keys_in", "v", "shifted"))

    def load(self, sp):
        flat = self.key.rearrange("e o -> (e o)")
        block_last = flat.rearrange("(q s) -> q s", s=KT * KC)[:, KT * KC - 1:KT * KC].rearrange("q o -> o q")
        with self.nc.allow_non_contiguous_dma(reason="the last key of each block"):
            sp.dma_start(self.top[:, :], block_last.to_broadcast((P, KT))).then_inc(self.tops_in, 16)
            sp.dma_start(self.low[:, :], flat.rearrange("(q r s) -> q r s", r=KT, s=KC)[:, :, KC - 1]).then_inc(self.lows, 16)

    def store(self, sp):
        sp.wait_ge(self.lows, 16)
        sp.dma_start(self.rowlast, self.low[:, :]).then_inc(self.lows, 16)
        sp.wait_ge(self.lows, 32)

    def clear(self):
        self.nc.gpsimd.memset(self.rows1[:, :, :], NONE).then_inc(self.prefill, 1)
        self.nc.gpsimd.memset(self.rows2[:, :, :], NONE).then_inc(self.prefill, 1)

    def fetch_rows(self, pool):
        nc = self.nc
        pool.wait_ge(self.prefill, 2)
        pool.wait_ge(self.lows, 32)
        pool.wait_ge(self.v, 3)
        for j in range(NJ):
            nc.gpsimd.indirect_dma_start(self.rows1[:, j, :], None, self.rowlast, bass.IndirectOffsetOnAxis(ap=self.index1[:, j:j + 1], axis=0),
                                         bounds_check=KT - 1, oob_is_err=False).then_inc(self.rows_in, 16)

    def fetch_keys(self, pool):
        nc = self.nc
        pool.wait_ge(self.v, 7)
        for j in range(NJ):
            nc.gpsimd.indirect_dma_start(self.rows2[:, j, :], None, self.key.rearrange("(r s) o -> r (s o)", s=KC),
                                         bass.IndirectOffsetOnAxis(ap=self.index2[:, j:j + 1], axis=0),
                                         bounds_check=KR - 1, oob_is_err=False).then_inc(self.keys_in, 16)
        pool.wait_ge(self.v, 12)
        with nc.allow_non_contiguous_dma(reason="one count of each partition"):
            pool.dma_start(self.before[1:P, 0:1], self.upto[0:P - 1, NJ - 1:NJ]).then_inc(self.shifted, 16)

    def node(self, width):
        return self.nid[:, :].unsqueeze(2).to_broadcast((P, NJ, width))

    def link(self, dve, n, ins):
        ins.then_inc(self.v, 1)
        dve.wait_ge(self.v, n)

    def count_blocks(self, dve):
        nc = self.nc
        dve.wait_ge(self.tops_in, 16)
        self.link(dve, 1, nc.vector.tensor_tensor(self.hits[:, :, 0:KT], self.top[:, :].unsqueeze(1).to_broadcast((P, NJ, KT)), self.node(KT), ALU.is_le))
        self.link(dve, 2, nc.vector.tensor_reduce(self.below1[:, :], self.hits[:, :, 0:KT], AX.X, ALU.add))
        self.link(dve, 3, nc.vector.tensor_copy(self.index1[:, :], self.below1[:, :]))

    def count_rows(self, dve):
        nc = self.nc
        dve.wait_ge(self.rows_in, 16 * NJ)
        self.link(dve, 4, nc.vector.tensor_tensor(self.hits[:, :, 0:KT], self.rows1[:, :, :], self.node(KT), ALU.is_le))
        self.link(dve, 5, nc.vector.tensor_reduce(self.below2[:, :], self.hits[:, :, 0:KT], AX.X, ALU.add))
        self.link(dve, 6, nc.vector.scalar_tensor_tensor(out=self.row[:, :], in0=self.below1[:, :], scalar=float(KT), in1=self.below2[:, :],
                                                         op0=ALU.mult, op1=ALU.add))
        self.link(dve, 7, nc.vector.tensor_copy(self.index2[:, :], self.row[:, :]))

    def count_keys(self, dve):
        nc = self.nc
        dve.wait_ge(self.keys_in, 16 * NJ)
        self.link(dve, 8, nc.vector.tensor_tensor(self.hits[:, :, :], self.rows2[:, :, :], self.node(KC), ALU.is_le))
        self.link(dve, 9, nc.vector.tensor_reduce(self.below3[:, :], self.hits[:, :, :], AX.X, ALU.add))
        self.link(dve, 10, nc.vector.scalar_tensor_tensor(out=self.upto[:, :], in0=self.row[:, :], scalar=float(KC), in1=self.below3[:, :],
                                                          op0=ALU.mult, op1=ALU.add))
        self.link(dve, 11, nc.vector.tensor_copy(self.before[:, 1:NJ], self.upto[:, 0:NJ - 1]))
        self.link(dve, 12, nc.vector.memset(self.before[0:1, 0:1], 0.0))

    def finish(self, dve):
        nc, info = self.nc, self.info
        dve.wait_ge(self.shifted, 16)
        nc.vector.tensor_tensor(info["cnt"][:, :], self.upto[:, :], self.before[:, :], ALU.subtract).then_inc(self.v, 1)
        nc.vector.tensor_scalar(self.f1[:, :], self.before[:, :], -float(NONE), None, ALU.add).then_inc(self.v, 1)
        nc.vector.tensor_scalar(self.l1[:, :], self.upto[:, :], -float(NONE + 1), None, ALU.add).then_inc(self.v, 1)
        nc.vector.tensor_scalar(self.s1[:, :], self.before[:, :], float(H), None, ALU.is_lt).then_inc(self.v, 1)
        nc.vector.tensor_scalar(self.s2[:, :], self.upto[:, :], float(H), None, ALU.is_gt).then_inc(self.v, 1)
        dve.wait_ge(self.v, 17)
        nc.vector.tensor_scalar(self.has[:, :], info["cnt"][:, :], 0.0, None, ALU.is_gt).then_inc(self.v, 1)
        nc.vector.tensor_tensor(info["span"][:, :], self.s1[:, :], self.s2[:, :], ALU.mult).then_inc(self.v, 1)
        dve.wait_ge(self.v, 19)
        nc.vector.tensor_tensor(self.f2[:, :], self.f1[:, :], self.has[:, :], ALU.mult).then_inc(self.v, 1)
        nc.vector.tensor_tensor(self.l2[:, :], self.l1[:, :], self.has[:, :], ALU.mult).then_inc(self.v, 1)
        dve.wait_ge(self.v, 21)
        nc.vector.tensor_scalar(info["first"][:, :], self.f2[:, :], float(NONE), None, ALU.add).then_inc(self.v, 1)
        nc.vector.tensor_scalar(info["last"][:, :], self.l2[:, :], float(NONE), None, ALU.add).then_inc(self.v, 1)


NB = 7
PARTS = ((0, 4), (4, 3))
ITERS = NJ // NB


def per_node(t, width=D):
    return t[:, :].unsqueeze(2).to_broadcast((P, NJ, width))


def per_feature(t, width=D):
    return t[:, :].unsqueeze(1).to_broadcast((P, NJ, width))


def row_of(vector, width=D):
    return vector.rearrange("(o f) -> o f", o=1).to_broadcast((P, width))


def column_of(vector):
    return vector.rearrange("(p o) -> p o", o=1)


def dense(nc, sb, ps, sem, ident, groups, loads, hidden, last, put, beside):
    NQ = len(groups)
    width = [sum(w for _, w in g) for g in groups]
    with Stage(nc) as c:
        w1, w2, bias1, bias2, bring, nload = loads(c)
        cat = [[sb(c, f"cat{q}{i}", [P, 4, width[q]]) for i in range(2)] for q in range(NQ)]
        feats = [[sb(c, f"feats{q}{i}", [P, 4 * P]) for i in range(2)] for q in range(NQ)]
        bank_in = [[ps(c, f"bank_in{q}{i}", [P, 4 * P]) for i in range(2)] for q in range(2)]
        bank_hid = [ps(c, f"bank_hid{i}", [P, 4 * P]) for i in range(2)]
        bank_out = [ps(c, f"bank_out{i}", [P, 4 * P]) for i in range(2)]
        chunks = hidden[1] if hidden else 0
        hid = [[sb(c, f"hid{m}{i}", [P, 4 * P]) for i in range(2)] for m in range(chunks)]
        outf = [sb(c, f"outf{i}", [last[1], 4 * P]) for i in range(2)]
        bank_of = (bank_hid, bank_in[1])
        weights_in, passed = sem(c, "weights_in"), sem(c, "passed")
        taken, turned, copied, summed, acted, mixed, biased, rowed, placed = (
            [sem(c, f"{n}{i}") for i in range(2)] for n in
            ("taken", "turned", "copied", "summed", "acted", "mixed", "biased", "rowed", "placed"))
        NCAT = sum(len(g) for g in groups)
        with nc.Block() as block:
            @block.sync
            def _(sp):
                bring(sp, weights_in)
                if "sp" in beside:
                    beside["sp"](sp)
                if "sp placed" in beside:
                    beside["sp placed"](sp, placed)

            @block.gpsimd
            def _(pool):
                if "pool" in beside:
                    beside["pool"](pool)
                if "pool placed" in beside:
                    beside["pool placed"](pool, placed)

            @block.vector
            def _(dve):
                with dve.Fori(0, ITERS) as it:
                    t = dve.snap(it)
                    for i, (a, k) in enumerate(PARTS):
                        dve.wait_ge(turned[i], t)
                        for q, g in enumerate(groups):
                            at = 0
                            for tensor, f in g:
                                nc.vector.tensor_copy(cat[q][i][:, 0:k, at:at + f], tensor[:, ds(t * NB + a, k), :]).then_inc(taken[i], 1)
                                at += f
                    for i, (a, k) in enumerate(PARTS):
                        dve.wait_ge(rowed[i], t + 1)
                        put(nc.vector, ds(t * NB + a, k), bank_in[0][i][:, 0:k * last[1]].rearrange("p (j f) -> p j f", f=last[1])).then_inc(placed[i], 1)
                if "dve behind" in beside:
                    beside["dve behind"](dve)

            @block.tensor
            def _(pe):
                pe.wait_ge(weights_in, nload)
                with pe.Fori(0, ITERS) as it:
                    t = pe.snap(it)
                    for i, (a, k) in enumerate(PARTS):
                        pe.wait_ge(taken[i], t * NCAT + NCAT)
                        pe.wait_ge(placed[i], t)
                        if chunks > 1:
                            pe.wait_ge(acted[i], t * chunks)
                        pe.sem_inc(passed, 1)
                        for q in range(NQ):
                            for j in range(k):
                                last_mm = nc.tensor.transpose(bank_in[q][i][0:width[q], j * P:(j + 1) * P], cat[q][i][:, j, :], ident[:, :])
                        last_mm.then_inc(turned[i], 1)
                    for m in range(chunks):
                        for i, (a, k) in enumerate(PARTS):
                            pe.wait_ge(copied[i], t * NQ + NQ)
                            pe.wait_ge(acted[i], t * chunks)
                            for q in range(NQ):
                                mm = nc.tensor.matmul(bank_of[m][i][:, 0:k * P], w1[q][0:width[q], m * P:(m + 1) * P], feats[q][i][0:width[q], 0:k * P],
                                                      start=q == 0, stop=q == NQ - 1)
                            mm.then_inc(summed[i], 1)
                    for i, (a, k) in enumerate(PARTS):
                        if chunks:
                            pe.wait_ge(acted[i], t * chunks + chunks)
                        else:
                            pe.wait_ge(copied[i], t * NQ + NQ)
                        pe.wait_ge(biased[i], t)
                        ins = [(w2[m], hid[m][i]) for m in range(chunks)] or [(w1[0][0:width[0], :], feats[0][i][0:width[0], :])]
                        for m, (wm, xm) in enumerate(ins):
                            mm = nc.tensor.matmul(bank_out[i][0:last[1], 0:k * P], wm, xm[:, 0:k * P], start=m == 0, stop=m == len(ins) - 1)
                        mm.then_inc(mixed[i], 1)
                    for i, (a, k) in enumerate(PARTS):
                        pe.wait_ge(biased[i], t + 1)
                        pe.sem_inc(passed, 1)
                        for j in range(k):
                            mm = nc.tensor.transpose(bank_in[0][i][:, j * last[1]:(j + 1) * last[1]], outf[i][:, j * P:(j + 1) * P], ident[0:last[1], 0:last[1]])
                        mm.then_inc(rowed[i], 1)

            @block.scalar
            def _(act):
                act.wait_ge(weights_in, nload)
                with act.Fori(0, ITERS) as it:
                    t = act.snap(it)
                    for i, (a, k) in enumerate(PARTS):
                        act.wait_ge(turned[i], t + 1)
                        act.wait_ge(mixed[i], t)
                        for q in range(NQ):
                            nc.scalar.activation(feats[q][i][0:width[q], 0:k * P], bank_in[q][i][0:width[q], 0:k * P], ACT.Copy).then_inc(copied[i], 1)
                    for m in range(chunks):
                        for i, (a, k) in enumerate(PARTS):
                            act.wait_ge(summed[i], t * chunks + m + 1)
                            nc.scalar.activation(hid[m][i][:, 0:k * P], bank_of[m][i][:, 0:k * P], hidden[0], bias=bias1[:, m:m + 1]).then_inc(acted[i], 1)
                    for i, (a, k) in enumerate(PARTS):
                        act.wait_ge(mixed[i], t + 1)
                        act.wait_ge(rowed[i], t)
                        nc.scalar.activation(outf[i][:, 0:k * P], bank_out[i][0:last[1], 0:k * P], last[0], bias=bias2[:, 0:1]).then_inc(biased[i], 1)


def norm(nc, sb, sem, ahead, t, o, behind):
    with Stage(nc) as c:
        s_sum, s_mean, s_sq, s_var, s_sd, s_rs = (sb(c, n, [P, NJ]) for n in ("s_sum", "s_mean", "s_sq", "s_var", "s_sd", "s_rs"))
        chain, root = sem(c, "chain"), sem(c, "root")
        with nc.Block() as block:
            @block.vector
            def _(dve):
                count = [0]

                def link(ins):
                    count[0] += 1
                    ins.then_inc(chain, 1)
                    dve.wait_ge(chain, count[0])

                for f in ahead:
                    link(f(nc.vector))
                link(nc.vector.tensor_reduce(s_sum[:, :], t[:, :, :], AX.X, ALU.add))
                link(nc.vector.tensor_scalar(s_mean[:, :], s_sum[:, :], 1.0 / D, None, ALU.mult))
                link(nc.vector.tensor_tensor(o[:, :, :], t[:, :, :], per_node(s_mean), ALU.subtract))
                link(nc.vector.tensor_tensor(t[:, :, :], o[:, :, :], o[:, :, :], ALU.mult))
                link(nc.vector.tensor_reduce(s_sq[:, :], t[:, :, :], AX.X, ALU.add))
                link(nc.vector.tensor_scalar(s_var[:, :], s_sq[:, :], 1.0 / D, EPS, ALU.mult, ALU.add))
                dve.wait_ge(root, 1)
                link(nc.vector.reciprocal(s_rs[:, :], s_sd[:, :]))
                link(nc.vector.tensor_tensor(o[:, :, :], o[:, :, :], per_node(s_rs), ALU.mult))
                for f in behind:
                    link(f(nc.vector))

            @block.scalar
            def _(act):
                act.wait_ge(chain, len(ahead) + 6)
                nc.scalar.activation(s_sd[:, :], s_var[:, :], ACT.Sqrt).then_inc(root, 1)


class Blank:

    def __init__(self, nc, sb, sem, c, table):
        self.width = E * D // P // 100
        self.nc, self.zeros = nc, sb(c, "zeros", [P, self.width])
        self.flat = table.rearrange("r f -> (r f)").rearrange("(p n) -> p n", p=P)
        self.cleared, self.filled = sem(c, "cleared"), sem(c, "filled")

    def clear(self):
        self.nc.vector.memset(self.zeros[:, :], 0.0).then_inc(self.cleared, 1)

    def fill(self, sp, a, b):
        sp.wait_ge(self.cleared, 1)
        for k in range(a, b):
            sp.dma_start(self.flat[:, k * self.width:(k + 1) * self.width], self.zeros[:, :]).then_inc(self.filled, 16)

    def wait(self, eng):
        eng.wait_ge(self.filled, 16 * 100)


def gather_rows(pool, nc, dest, width, table, index, counted):
    for j in range(NJ):
        nc.gpsimd.indirect_dma_start(dest[:, j, :], None, table, bass.IndirectOffsetOnAxis(ap=index[:, j:j + 1], axis=0),
                                     bounds_check=E - 1, oob_is_err=False).then_inc(counted, 16)


def node_layers_1_2(nc, sb, ps, sem, X, order, nid, srcs, marks, rowlast, blank, t1, wn, ident, w0a, b0a, w0b, b0b, u1, w1a, b1a, w1b, b1b, g1, be1):
    info = order[0]
    CUTS = 30, 70
    with Stage(nc) as c:
        agg = sb(c, "agg", [P, NJ, 2 * D])
        mean = sb(c, "mean", [P, NJ, D])
        Y, Z = sb(c, "Y", [P, NJ, D]), sb(c, "Z", [P, NJ, D])
        GA, BE = sb(c, "GA", [P, D]), sb(c, "BE", [P, D])
        ends = Ends(nc, sb, ps, sem, c, 1, srcs, order[1], nid, rowlast)
        with Stage(nc) as cc:
            carry = sb(cc, "carry", [P, 2 * D])
            nz, iszero, safe, inv, reset, atleast, per = (sb(cc, n, [P, NJ]) for n in ("nz", "iszero", "safe", "inv", "reset", "atleast", "per"))
            cleared, agg_in, carry_in, chain = (sem(cc, n) for n in ("cleared", "agg_in", "carry_in", "chain"))
            marks_1 = Marks(nc, sb, ps, sem, cc, 1, srcs, marks, ident)
            with nc.Block() as block:
                @block.sync
                def _(sp):
                    sp.dma_start(carry[:, :], t1[H - 1:H, :].to_broadcast((P, 2 * D))).then_inc(carry_in, 16)
                    sp.dma_start(GA[:, :], row_of(g1)).then_inc(carry_in, 16)
                    sp.dma_start(BE[:, :], row_of(be1)).then_inc(carry_in, 16)
                    ends.load(sp)
                    ends.store(sp)
                    marks_1.load(sp)
                    blank.fill(sp, 0, CUTS[0])
                    marks_1.store(sp)

                @block.gpsimd
                def _(pool):
                    pool.wait_ge(cleared, 1)
                    gather_rows(pool, nc, agg, 2 * D, t1, info["last"], agg_in)
                    ends.clear()

                @block.vector
                def _(dve):
                    count = [0]

                    def link(ins):
                        count[0] += 1
                        ins.then_inc(chain, 1)
                        dve.wait_ge(chain, count[0])

                    nc.vector.memset(agg[:, :, :], 0.0).then_inc(cleared, 1)
                    blank.clear()
                    marks_1.compare(dve)
                    ends.count_blocks(dve)
                    w = wn[:, :, 0]
                    link(nc.vector.tensor_scalar(nz[:, :], w, 0.0, None, ALU.not_equal))
                    link(nc.vector.tensor_scalar(iszero[:, :], w, 0.0, None, ALU.is_equal))
                    link(nc.vector.tensor_tensor(safe[:, :], iszero[:, :], w, ALU.add))
                    link(nc.vector.reciprocal(inv[:, :], safe[:, :]))
                    link(nc.vector.tensor_tensor(Y[:, :, :], X[:, :, :], wn[:, :, :].to_broadcast((P, NJ, D)), ALU.mult))
                    link(nc.vector.tensor_tensor(Z[:, :, :], Y[:, :, :], per_node(inv), ALU.mult))
                    link(nc.vector.tensor_tensor(Y[:, :, :], Z[:, :, :], X[:, :, :], ALU.add))
                    link(nc.vector.tensor_tensor(Z[:, :, :], Y[:, :, :], per_node(nz), ALU.mult))
                    link(nc.vector.tensor_scalar(reset[:, :], info["span"][:, :], -1.0, -NEG, ALU.add, ALU.mult))
                    link(nc.vector.tensor_scalar(atleast[:, :], info["cnt"][:, :], 1.0, None, ALU.max))
                    link(nc.vector.reciprocal(per[:, :], atleast[:, :]))
                    dve.wait_ge(agg_in, 16 * NJ)
                    dve.wait_ge(carry_in, 48)
                    link(nc.vector.tensor_tensor(mean[:, :, :], per_node(info["span"]), per_feature(carry[:, 0:D]), ALU.mult))
                    link(nc.vector.tensor_tensor(agg[:, :, 0:D], agg[:, :, 0:D], mean[:, :, :], ALU.add))
                    link(nc.vector.tensor_tensor(mean[:, :, :], per_node(info["span"]), per_feature(carry[:, D:2 * D]), ALU.mult))
                    link(nc.vector.tensor_tensor(mean[:, :, :], mean[:, :, :], per_node(reset), ALU.add))
                    link(nc.vector.tensor_tensor(agg[:, :, D:2 * D], agg[:, :, D:2 * D], mean[:, :, :], ALU.max))
                    link(nc.vector.tensor_tensor(mean[:, :, :], agg[:, :, 0:D], per_node(per), ALU.mult))

        def loads_1(c):
            W1, W2 = sb(c, "W1", [D, 2 * P]), sb(c, "W2", [P, 2, D])
            B1, B2 = sb(c, "B1", [P, 2]), sb(c, "B2", [D, 1])

            def bring(sp, done):
                sp.dma_start(W1[:, :], w0a).then_inc(done, 16)
                sp.dma_start(W2[:, :, :], w0b.rearrange("(q p) f -> p q f", q=2)).then_inc(done, 16)
                with nc.allow_non_contiguous_dma(reason="biases by partition"):
                    sp.dma_start(B1[:, :], b0a.rearrange("(q p) -> p q", q=2)).then_inc(done, 16)
                    sp.dma_start(B2[:, :], column_of(b0b)).then_inc(done, 16)
            return [W1], [W2[:, 0, :], W2[:, 1, :]], B1, B2, bring, 64

        def fill_more(sp):
            sp.wait_ge(ends.rows_in, 16 * NJ)
            blank.fill(sp, *CUTS)

        dense(nc, sb, ps, sem, ident, [[(Z, D)]], loads_1, (ACT.Relu, 2), (ACT.Relu, D),
              lambda eng, cols, bank: eng.tensor_tensor(Y[:, cols, :], X[:, cols, :], bank, ALU.add),
              {"sp": fill_more, "pool": ends.fetch_rows, "dve behind": ends.count_rows})
        norm(nc, sb, sem, [], Y, X, [])

        V1a, V1b, V2 = sb(c, "V1a", [P, P]), sb(c, "V1b", [P, P]), sb(c, "V2", [P, D])
        VU, UB, C1, C1B, C2 = (sb(c, n, [P, 1]) for n in ("VU", "UB", "C1", "C1B", "C2"))
        weights2, folded = sem(c, "weights2"), sem(c, "folded")
        with nc.Block() as block:
            @block.sync
            def _(sp):
                sp.dma_start(V1a[:, :], w1a[D:3 * D, :]).then_inc(weights2, 16)
                sp.dma_start(V1b[0:D, :], w1a[0:D, :]).then_inc(weights2, 16)
                sp.dma_start(V1b[D:P, :], w1a[3 * D:4 * D, :]).then_inc(weights2, 16)
                sp.dma_start(V2[:, :], w1b).then_inc(weights2, 16)
                with nc.allow_non_contiguous_dma(reason="biases by partition"):
                    sp.dma_start(C1[:, :], column_of(b1a)).then_inc(weights2, 16)
                    sp.dma_start(C2[0:D, :], column_of(b1b)).then_inc(weights2, 16)
                    sp.dma_start(VU[:, :], w1a[4 * D:4 * D + 1, :].rearrange("o f -> f o")).then_inc(weights2, 16)
                    sp.dma_start(UB[:, :], u1[0:1, 0:1].to_broadcast((P, 1))).then_inc(weights2, 16)

            @block.vector
            def _(dve):
                dve.wait_ge(weights2, 16 * 8)
                nc.vector.scalar_tensor_tensor(out=C1B[:, :], in0=VU[:, :], scalar=UB[:, 0:1], in1=C1[:, :],
                                               op0=ALU.mult, op1=ALU.add).then_inc(folded, 1)

        def fill_behind(sp):
            sp.wait_ge(ends.shifted, 16)
            blank.fill(sp, CUTS[1], 100)

        def search_ends(dve):
            ends.count_keys(dve)
            ends.finish(dve)

        dense(nc, sb, ps, sem, ident, [[(agg, 2 * D)], [(X, D), (mean, D)]], lambda c: ([V1a, V1b], [V2[:, :]], C1B, C2[0:D, :], lambda sp, done: None, 0),
              (ACT.Gelu, 1), (ACT.Identity, D), lambda eng, cols, bank: eng.tensor_copy(Y[:, cols, :], bank),
              {"sp": fill_behind, "pool": ends.fetch_keys, "dve behind": search_ends})
        norm(nc, sb, sem, [], Y, Z, [
            lambda eng: eng.tensor_tensor(Y[:, :, :], Z[:, :, :], per_feature(GA), ALU.mult),
            lambda eng: eng.tensor_tensor(Z[:, :, :], Y[:, :, :], per_feature(BE), ALU.add),
            lambda eng: eng.tensor_tensor(Y[:, :, :], Z[:, :, :], X[:, :, :], ALU.add),
            lambda eng: eng.tensor_tensor(Z[:, :, :], Y[:, :, :], X[:, :, :], ALU.add)])
        norm(nc, sb, sem, [], Z, X, [])


def node_tables(nc, sb, ps, sem, X, info, key, gathered, spread, tabg, tabs, start, ident, blank=None):
    with Stage(nc) as c:
        rows = sb(c, "rows", [P, NJ, 2 * D])
        prime_key = sb(c, "prime_key", [2, 1], I32)
        prime = sb(c, "prime", [2, D])

        stored, keyed, primed, firsts, put = (sem(c, n) for n in ("stored", "keyed", "primed", "firsts", "put"))

        def scatter(pool, placed):
            if blank:
                blank.wait(pool)
            for t in range(ITERS):
                for i, (a, k) in enumerate(PARTS):
                    pool.wait_ge(placed[i], t + 1)
                    for j in range(t * NB + a, t * NB + a + k):
                        nc.gpsimd.indirect_dma_start(start, bass.IndirectOffsetOnAxis(ap=info["first"][:, j:j + 1], axis=0), rows[:, j, D:2 * D], None,
                                                     bounds_check=E - 1, oob_is_err=False).then_inc(firsts, 16)

        def store(sp, placed):
            sp.dma_start(prime_key[:, :], key[H:H + 1, :].to_broadcast((2, 1))).then_inc(keyed, 16)
            for t in range(ITERS):
                for i in range(2):
                    sp.wait_ge(placed[i], t + 1)
                for table, part in ((tabs, slice(D, 2 * D)), (tabg, slice(0, D))):
                    sp.dma_start(table.rearrange("(p j) f -> p j f", j=NJ)[:, t * NB:(t + 1) * NB, :], rows[:, t * NB:(t + 1) * NB, part]).then_inc(stored, 16)

        def loads(cc):
            WW, BB = sb(cc, "WW", [D, 2 * D]), sb(cc, "BB", [2 * D, 1])
            biases = [b for b in (gathered[1], spread[1]) if b is not None]
            zero = sem(cc, "zero")

            def bring(sp, done):
                sp.dma_start(WW[:, 0:D], gathered[0]).then_inc(done, 16)
                sp.dma_start(WW[:, D:2 * D], spread[0]).then_inc(done, 16)
                if len(biases) < 2:
                    sp.wait_ge(zero, 1)
                for q, b in enumerate(biases):
                    with nc.allow_non_contiguous_dma(reason="biases by partition"):
                        sp.dma_start(BB[q * D:(q + 1) * D, :], column_of(b)).then_inc(done, 16)

            if len(biases) < 2:
                with nc.Block() as block:
                    @block.vector
                    def _(dve):
                        nc.vector.memset(BB[:, :], 0.0).then_inc(zero, 1)
            return [WW], None, None, BB, bring, 32 + 16 * len(biases)

        dense(nc, sb, ps, sem, ident, [[(X, D)]], loads, None, (ACT.Identity, 2 * D),
              lambda eng, cols, bank: eng.tensor_copy(rows[:, cols, :], bank), {"pool placed": scatter, "sp placed": store})
        with nc.Block() as block:
            @block.sync
            def _(sp):
                sp.wait_ge(primed, 16)
                sp.wait_ge(firsts, 16 * NJ)
                sp.dma_start(start[H:H + 1, :], prime[0:1, :]).then_inc(put, 16)
                sp.wait_ge(put, 16)

            @block.gpsimd
            def _(pool):
                pool.wait_ge(keyed, 16)
                pool.wait_ge(stored, 16 * 2 * ITERS)
                nc.gpsimd.indirect_dma_start(prime[:, :], None, tabs, bass.IndirectOffsetOnAxis(ap=prime_key[:, :], axis=0)).then_inc(primed, 16)


def edges_3(nc, sb, ps, sem, other, marks, tabg, start, next_start, t2, ident, sel2, w2b, b2b, w2g, b2g):
    with Stage(nc) as c:
        zeros = sb(c, "zeros", [P, 2, C * D])
        blank, blanked = sem(c, "blank"), sem(c, "blanked")
        W2, WG = sb(c, "W2", [P, P]), sb(c, "WG", [P, P])
        B2, BG = sb(c, "B2", [P, 1]), sb(c, "BG", [P, 1])
        first = [sb(c, f"first{i}", [P, C, 2, D]) for i in range(AHEAD)]
        mk = [sb(c, f"mk{i}", [2, W], BF16) for i in range(AHEAD)]
        ix = [sb(c, f"ix{i}", [P, 2, C], I32) for i in range(AHEAD)]
        got = [sb(c, f"got{i}", [P, C, 2, D]) for i in range(AHEAD)]
        starts, own, pre, hid, inter, gate, gated, run = (
            [sb(c, f"{n}{i}", [P, W]) for i in range(2)] for n in ("starts", "own", "pre", "hid", "inter", "gate", "gated", "run"))
        rows = [sb(c, f"rows{i}", [P, 2, C, D]) for i in range(2)]
        p_first, p_got, p_inter, p_gate, p_own, p_sum = (
            ps(c, n, [P, C * P]) for n in ("p_first", "p_got", "p_inter", "p_gate", "p_own", "p_sum"))
        p_out = [ps(c, f"p_out{i}", [P, C, P]) for i in range(2)]
        zeroed, weights_in, passed = (sem(c, n) for n in ("zeroed", "weights_in", "passed"))
        first_in, ix_in, got_in = ([sem(c, f"{n}{i}") for i in range(AHEAD)] for n in ("first_in", "ix_in", "got_in"))
        stored = [sem(c, f"stored{i}") for i in range(2)]
        (marked, turned_first, turned_got, started, owned, added, relued, mixed, biased, scored, gates, products, remarked,
         summed, rowed, drained) = (
            sem(c, n) for n in ("marked", "turned_first", "turned_got", "started", "owned", "added", "relued", "mixed", "biased",
                                "scored", "gates", "products", "remarked", "summed", "rowed", "drained"))
        with nc.Block() as block:
            @block.sync
            def _(sp):
                sp.wait_ge(zeroed, 2)
                for h in range(2):
                    at = slice(h * D, (h + 1) * D)
                    for t, w in ((W2, w2b), (WG, w2g)):
                        sp.dma_start(t[at, at], w).then_inc(weights_in, 16)
                    with nc.allow_non_contiguous_dma(reason="biases by partition"):
                        for t, b in ((B2, b2b), (BG, b2g)):
                            sp.dma_start(t[at, :], column_of(b)).then_inc(weights_in, 16)

                def load(g):
                    s, row = g.slot(AHEAD), snapped(sp, g.row)
                    wait_from(sp, remarked, g.n - AHEAD + 1)
                    sp.dma_start(ix[s][0:g.p, :, :], indices_of(other, row, g.w)).then_inc(ix_in[s], 16)
                    for h in range(2):
                        sp.dma_start(first[s][0:g.p, :, h, :], by_edge(start, h, row, g.w)).then_inc(first_in[s], 16)
                    sp.dma_start(mk[s][:, 0:g.w], marks[1][:, 0, ds(row, g.w)]).then_inc(first_in[s], 16)
                    sp.dma_start(both_halves(next_start, row, g.w), zeros[0:g.p, :, :]).then_inc(blanked, 16)

                sp.wait_ge(blank, 1)
                each_group(sp, (0, load))
                sp.wait_ge(blanked, 16 * (NG + 1))

            @block.gpsimd
            def _(pool):
                def gather(g):
                    s = g.slot(AHEAD)
                    pool.wait_ge(ix_in[s], 16 * g.turn(AHEAD) + 16)
                    wait_from(pool, turned_got, g.n - AHEAD + 1)
                    pool.sem_inc(passed, 1)
                    for cc in range(C):
                        for h in range(2):
                            nc.gpsimd.indirect_dma_start(got[s][0:g.p, cc, h, :], None, tabg,
                                                         bass.IndirectOffsetOnAxis(ap=ix[s][0:g.p, h, cc:cc + 1], axis=0)).then_inc(got_in[s], 16)

                each_group(pool, (0, gather))

            @block.tensor
            def _(pe):
                pe.wait_ge(weights_in, 128)

                def turn_back(g):
                    s = g.slot(2)
                    pe.wait_ge(summed, g.n + 1)
                    wait_from(pe, drained, g.n - 1)
                    turn_to_edges(nc, p_out[s], run[s], g, ident).then_inc(rowed, 1)

                def gate_scores(g):
                    pe.wait_ge(biased, g.n + 1)
                    wait_from(pe, gates, g.n)
                    nc.tensor.matmul(p_gate[:, 0:g.w], WG[:, :], inter[g.slot(2)][:, 0:g.w], start=True, stop=True).then_inc(scored, 1)

                def first_rows(g):
                    s = g.slot(AHEAD)
                    pe.wait_ge(first_in[s], 48 * g.turn(AHEAD) + 48)
                    wait_from(pe, started, g.n)
                    turn_to_features(nc, p_first, first[s], g, ident).then_inc(turned_first, 1)
                    wait_from(pe, owned, g.n)
                    nc.tensor.matmul(p_own[:, 0:g.w], sel2[:, :], mk[s][:, 0:g.w], start=True, stop=True).then_inc(marked, 1)

                def gathered_rows(g):
                    s = g.slot(AHEAD)
                    pe.wait_ge(got_in[s], 128 * g.turn(AHEAD) + 128)
                    wait_from(pe, added, g.n)
                    turn_to_features(nc, p_got, got[s], g, ident).then_inc(turned_got, 1)

                def marks_again(g):
                    wait_from(pe, summed, g.n)
                    nc.tensor.matmul(p_sum[:, 0:g.w], sel2[:, :], mk[g.slot(AHEAD)][:, 0:g.w], start=True, stop=True).then_inc(remarked, 1)

                def interact(g):
                    pe.wait_ge(relued, g.n + 1)
                    wait_from(pe, biased, g.n)
                    nc.tensor.matmul(p_inter[:, 0:g.w], W2[:, :], hid[g.slot(2)][:, 0:g.w], start=True, stop=True).then_inc(mixed, 1)

                each_group(pe, (3, turn_back), (2, gate_scores), (0, first_rows), (2, marks_again), (1, gathered_rows), (1, interact))

            @block.scalar
            def _(act):
                act.wait_ge(weights_in, 128)

                def start_rows(g):
                    act.wait_ge(turned_first, g.n + 1)
                    wait_from(act, owned, g.n - 1)
                    nc.scalar.activation(by_place(starts[g.slot(2)], g), by_block(p_first, g), ACT.Copy).then_inc(started, 1)

                def gates_of(g):
                    act.wait_ge(scored, g.n + 1)
                    wait_from(act, products, g.n - 1)
                    nc.scalar.activation(gate[g.slot(2)][:, 0:g.w], p_gate[:, 0:g.w], ACT.Sigmoid, bias=BG[:, 0:1]).then_inc(gates, 1)

                def relu(g):
                    act.wait_ge(added, g.n + 1)
                    wait_from(act, mixed, g.n - 1)
                    nc.scalar.activation(hid[g.slot(2)][:, 0:g.w], pre[g.slot(2)][:, 0:g.w], ACT.Relu).then_inc(relued, 1)

                def to_rows(g):
                    s = g.slot(2)
                    act.wait_ge(rowed, g.n + 1)
                    wait_from(act, stored[s], 16 * g.turn(2))
                    nc.scalar.activation(rows[s][0:g.p, :, :, :].rearrange("p h c f -> p c h f"),
                                         p_out[s][0:g.p, :, :].rearrange("p c (h f) -> p c h f", h=2), ACT.Copy).then_inc(drained, 1)
                    act.wait_ge(drained, g.n + 1)
                    act.dma_start(both_halves(t2, g.row, g.w), rows[s][0:g.p, :, :, :].rearrange("p h c f -> p h (c f)")).then_inc(stored[s], 16)

                def bias(g):
                    act.wait_ge(mixed, g.n + 1)
                    wait_from(act, products, g.n - 1)
                    nc.scalar.activation(inter[g.slot(2)][:, 0:g.w], p_inter[:, 0:g.w], ACT.Identity, bias=B2[:, 0:1]).then_inc(biased, 1)

                each_group(act, (2, gates_of), (0, start_rows), (3, to_rows), (1, relu), (1, bias))
                for s in range(2):
                    act.wait_ge(stored[s], 16 * ((NG + 2 - s) // 2))

            @block.vector
            def _(dve):
                nc.vector.memset(W2[:, :], 0.0).then_inc(zeroed, 1)
                nc.vector.memset(WG[:, :], 0.0).then_inc(zeroed, 1)
                nc.vector.memset(zeros[:, :, :], 0.0).then_inc(blank, 1)

                def spread(g):
                    s = g.slot(2)
                    dve.wait_ge(marked, g.n + 1)
                    dve.wait_ge(started, g.n + 1)
                    wait_from(dve, owned, g.n)
                    wait_from(dve, added, g.n - 1)
                    nc.vector.tensor_tensor_scan(own[s][:, 0:g.w], p_own[:, 0:g.w], starts[s][:, 0:g.w],
                                                 0.0 if g.zero else own[1 - s][:, W - 1:W], ALU.mult, ALU.add).then_inc(owned, 1)

                def add(g):
                    s = g.slot(2)
                    dve.wait_ge(owned, g.n + 1)
                    dve.wait_ge(turned_got, g.n + 1)
                    wait_from(dve, relued, g.n - 1)
                    nc.vector.tensor_tensor(by_place(pre[s], g), by_place(own[s], g), by_block(p_got, g), ALU.add).then_inc(added, 1)

                def multiply(g):
                    s = g.slot(2)
                    dve.wait_ge(gates, g.n + 1)
                    wait_from(dve, summed, g.n - 1)
                    nc.vector.tensor_tensor(gated[s][:, 0:g.w], inter[s][:, 0:g.w], gate[s][:, 0:g.w], ALU.mult).then_inc(products, 1)

                def accumulate(g):
                    s = g.slot(2)
                    dve.wait_ge(products, g.n + 1)
                    dve.wait_ge(remarked, g.n + 1)
                    wait_from(dve, summed, g.n)
                    wait_from(dve, rowed, g.n - 1)
                    nc.vector.tensor_tensor_scan(run[s][:, 0:g.w], p_sum[:, 0:g.w], gated[s][:, 0:g.w],
                                                 0.0 if g.zero else run[1 - s][:, W - 1:W], ALU.mult, ALU.add).then_inc(summed, 1)

                each_group(dve, (2, multiply), (1, add), (0, spread), (2, accumulate))


def pool_3(nc, sb, ps, sem, X, info, t2):
    with Stage(nc) as c:
        pooled, Z = sb(c, "pooled", [P, NJ, D]), sb(c, "Z", [P, NJ, D])
        carry = sb(c, "carry", [P, D])
        atleast, per = sb(c, "atleast", [P, NJ]), sb(c, "per", [P, NJ])
        cleared, rows_in, carry_in, chain = (sem(c, n) for n in ("cleared", "rows_in", "carry_in", "chain"))
        with nc.Block() as block:
            @block.sync
            def _(sp):
                sp.dma_start(carry[:, :], t2[H - 1:H, :].to_broadcast((P, D))).then_inc(carry_in, 16)

            @block.gpsimd
            def _(pool):
                pool.wait_ge(cleared, 1)
                gather_rows(pool, nc, pooled, D, t2, info["last"], rows_in)

            @block.vector
            def _(dve):
                nc.vector.memset(pooled[:, :, :], 0.0).then_inc(cleared, 1)
                nc.vector.tensor_scalar(atleast[:, :], info["cnt"][:, :], 1.0, None, ALU.max).then_inc(chain, 1)
                dve.wait_ge(chain, 1)
                nc.vector.reciprocal(per[:, :], atleast[:, :]).then_inc(chain, 1)
                dve.wait_ge(carry_in, 16)
                nc.vector.tensor_tensor(Z[:, :, :], per_node(info["span"]), per_feature(carry), ALU.mult).then_inc(chain, 1)
                dve.wait_ge(chain, 3)
                dve.wait_ge(rows_in, 16 * NJ)
                nc.vector.tensor_tensor(pooled[:, :, :], pooled[:, :, :], Z[:, :, :], ALU.add).then_inc(chain, 1)
                dve.wait_ge(chain, 4)
                nc.vector.tensor_tensor(pooled[:, :, :], pooled[:, :, :], per_node(per), ALU.mult).then_inc(chain, 1)
                dve.wait_ge(chain, 5)
                nc.vector.tensor_tensor(Z[:, :, :], pooled[:, :, :], X[:, :, :], ALU.add).then_inc(chain, 1)
        norm(nc, sb, sem, [], Z, X, [])


def edges_4(nc, sb, ps, sem, other, ea16, marks, tabg, start, t3, ident, sel2, we, att):
    R = 2 * HEADS
    with Stage(nc) as c:
        WE, AT = sb(c, "WE", [2 * ED, P]), sb(c, "AT", [P, P])
        AV = sb(c, "AV", [P, 1])
        onesr, second = sb(c, "onesr", [P, R]), sb(c, "second", [P, R])
        for_top, for_den = sb(c, "for_top", [P, 1]), sb(c, "for_den", [P, 1])
        blocks = [sb(c, f"blocks{i}", [P, P]) for i in range(3)]
        first, got = ([sb(c, f"{n}{i}", [P, C, 2, D]) for i in range(AHEAD)] for n in ("first", "got"))
        ea = [sb(c, f"ea{i}", [P, C, 2, ED]) for i in range(AHEAD)]
        mk = [sb(c, f"mk{i}", [2, 2, W], BF16) for i in range(AHEAD)]
        ix = [sb(c, f"ix{i}", [P, 2, C], I32) for i in range(AHEAD)]
        starts, own, theirs, pre, act_in, logit, left, weighted, run, den, tops, mixed = (
            [sb(c, f"{n}{i}", [P, W]) for i in range(2)] for n in ("starts", "own", "theirs", "pre", "act_in", "logit", "left",
                                                                    "weighted", "run", "den", "tops", "mixed"))
        eat = [sb(c, f"eat{i}", [2 * ED, W]) for i in range(2)]
        top = [sb(c, f"top{i}", [P, 1 + W]) for i in range(2)]
        expo, grow = ([sb(c, f"{n}{i}", [P, 2, W]) for i in range(2)] for n in ("expo", "grow"))
        rows = [sb(c, f"rows{i}", [P, 2, C, T3]) for i in range(2)]
        p_first, p_got, p_mk, p_reset, p_small, p_pre, p_logit, p_out = (
            ps(c, n, [P, C * P]) for n in ("p_first", "p_got", "p_mk", "p_reset", "p_small", "p_pre", "p_logit", "p_out"))
        zeroed, made, weights_in, passed = (sem(c, n) for n in ("zeroed", "made", "weights_in", "passed"))
        first_in, ix_in, got_in = ([sem(c, f"{n}{i}") for i in range(AHEAD)] for n in ("first_in", "ix_in", "got_in"))
        stored = [sem(c, f"stored{i}") for i in range(2)]
        (marked, resets, turned_first, turned_ea, turned_got, started, featured, gotten, summed_ea, owned, added, leaked, scored,
         logits, carried, maxed, lefts, expos, grown, topped, weighted_s, summed, dens, mixes, rowed, smalls, drained, drained_small) = (
            sem(c, n) for n in ("marked", "resets", "turned_first", "turned_ea", "turned_got", "started", "featured", "gotten", "summed_ea",
                                "owned", "added", "leaked", "scored", "logits", "carried", "maxed", "lefts", "expos", "grown",
                                "topped", "weighted_s", "summed", "dens", "mixes", "rowed", "smalls", "drained", "drained_small"))
        with nc.Block() as block:
            @block.sync
            def _(sp):
                sp.wait_ge(zeroed, 1)
                for h in range(2):
                    sp.dma_start(WE[h * ED:(h + 1) * ED, h * D:(h + 1) * D], we).then_inc(weights_in, 16)
                    with nc.allow_non_contiguous_dma(reason="the heads' vectors by partition"):
                        sp.dma_start(AV[h * D:(h + 1) * D, :], column_of(att.rearrange("a f -> (a f)"))).then_inc(weights_in, 16)

                def load(g):
                    s, row = g.slot(AHEAD), snapped(sp, g.row)
                    wait_from(sp, resets, g.n - AHEAD + 1)
                    sp.dma_start(ix[s][0:g.p, :, :], indices_of(other, row, g.w)).then_inc(ix_in[s], 16)
                    for h in range(2):
                        sp.dma_start(first[s][0:g.p, :, h, :], by_edge(start, h, row, g.w)).then_inc(first_in[s], 16)
                        sp.dma_start(ea[s][0:g.p, :, h, :], by_edge(ea16, h, row, g.w)).then_inc(first_in[s], 16)
                    sp.dma_start(mk[s][:, :, 0:g.w], marks[0][:, :, ds(row, g.w)]).then_inc(first_in[s], 16)

                each_group(sp, (0, load))

            @block.gpsimd
            def _(pool):
                nc.gpsimd.memset(onesr[:, :], 1.0).then_inc(made, 1)
                nc.gpsimd.memset(blocks[0][:, :], 1.0).then_inc(made, 1)
                pool.wait_ge(made, 2)
                nc.gpsimd.affine_select(out=second[:, :], in_=onesr[:, :], compare_op=ALU.is_equal, fill=0.0, base=-1,
                                        pattern=[[-HC, R]], channel_multiplier=1).then_inc(made, 1)
                nc.gpsimd.affine_select(out=blocks[1][:, :].rearrange("p (r f) -> p r f", r=R), in_=blocks[0][:, :].rearrange("p (r f) -> p r f", r=R),
                                        compare_op=ALU.is_ge, fill=0.0, base=0, pattern=[[-HC, R], [0, HC]], channel_multiplier=1).then_inc(made, 1)
                pool.wait_ge(made, 4)
                nc.gpsimd.affine_select(out=blocks[2][:, :].rearrange("p (r f) -> p r f", r=R), in_=blocks[1][:, :].rearrange("p (r f) -> p r f", r=R),
                                        compare_op=ALU.is_ge, fill=0.0, base=HC - 1, pattern=[[HC, R], [0, HC]], channel_multiplier=-1).then_inc(made, 1)

                def gather(g):
                    s = g.slot(AHEAD)
                    pool.wait_ge(ix_in[s], 16 * g.turn(AHEAD) + 16)
                    wait_from(pool, turned_got, g.n - AHEAD + 1)
                    pool.sem_inc(passed, 1)
                    for cc in range(C):
                        for h in range(2):
                            nc.gpsimd.indirect_dma_start(got[s][0:g.p, cc, h, :], None, tabg,
                                                         bass.IndirectOffsetOnAxis(ap=ix[s][0:g.p, h, cc:cc + 1], axis=0)).then_inc(got_in[s], 16)

                each_group(pool, (0, gather))

            @block.tensor
            def _(pe):
                pe.wait_ge(weights_in, 64)
                pe.wait_ge(zeroed, 2)

                def turn_back(g):
                    pe.wait_ge(summed, g.n + 1)
                    wait_from(pe, drained, g.n)
                    turn_to_edges(nc, p_out[:, :].rearrange("p (c q) -> p c q", c=C), run[g.slot(2)], g, ident).then_inc(rowed, 1)

                def edge_inputs(g):
                    s = g.slot(AHEAD)
                    pe.wait_ge(first_in[s], 80 * g.turn(AHEAD) + 80)
                    wait_from(pe, started, g.n)
                    turn_to_features(nc, p_first, first[s], g, ident).then_inc(turned_first, 1)
                    wait_from(pe, owned, g.n)
                    nc.tensor.matmul(p_mk[:, 0:g.w], sel2[:, :], mk[s][:, 0, 0:g.w], start=True, stop=True).then_inc(marked, 1)
                    wait_from(pe, featured, g.n)
                    wait_from(pe, drained_small, g.n - LAG)
                    turn_to_features(nc, p_small, ea[s], g, ident, 2 * ED).then_inc(turned_ea, 1)

                def gathered_rows(g):
                    s = g.slot(AHEAD)
                    pe.wait_ge(got_in[s], 128 * g.turn(AHEAD) + 128)
                    wait_from(pe, gotten, g.n)
                    turn_to_features(nc, p_got, got[s], g, ident).then_inc(turned_got, 1)

                def add_edge_terms(g):
                    s = g.slot(2)
                    pe.wait_ge(featured, g.n + 1)
                    wait_from(pe, added, g.n)
                    nc.tensor.matmul(p_pre[:, 0:g.w], WE[:, :], eat[s][:, 0:g.w], start=True, stop=False)
                    pe.wait_ge(gotten, g.n + 1)
                    nc.tensor.matmul(p_pre[:, 0:g.w], ident[:, :], theirs[s][:, 0:g.w], start=False, stop=True).then_inc(summed_ea, 1)

                def small_back(g):
                    pe.wait_ge(mixes, g.n + 1)
                    if not g.late:
                        pe.wait_ge(featured, g.n + LAG + 1)
                    else:
                        pe.wait_ge(drained_small, g.n)
                    turn_to_edges(nc, p_small[:, :].rearrange("p (c q) -> p c q", c=C), mixed[g.slot(2)], g, ident).then_inc(smalls, 1)

                def score(g):
                    pe.wait_ge(leaked, g.n + 1)
                    wait_from(pe, logits, g.n)
                    nc.tensor.matmul(p_logit[:, 0:g.w], AT[:, :], act_in[g.slot(2)][:, 0:g.w], start=True, stop=True).then_inc(scored, 1)
                    wait_from(pe, lefts, g.n)
                    nc.tensor.matmul(p_reset[:, 0:g.w], sel2[:, :], mk[g.slot(AHEAD)][:, 1, 0:g.w], start=True, stop=True).then_inc(resets, 1)

                each_group(pe, (1, gathered_rows), (0, edge_inputs), (1, add_edge_terms), (3, turn_back), (3, small_back), (1, score))

            @block.scalar
            def _(act):
                act.wait_ge(zeroed, 3)

                def start_rows(g):
                    act.wait_ge(turned_first, g.n + 1)
                    wait_from(act, owned, g.n - 1)
                    nc.scalar.activation(by_place(starts[g.slot(2)], g), by_block(p_first, g), ACT.Copy).then_inc(started, 1)
                    act.wait_ge(turned_ea, g.n + 1)
                    wait_from(act, summed_ea, g.n - 1)
                    nc.scalar.activation(by_place(eat[g.slot(2)], g), by_block(p_small, g, 2 * ED), ACT.Copy).then_inc(featured, 1)

                def their_rows(g):
                    act.wait_ge(turned_got, g.n + 1)
                    wait_from(act, weighted_s, g.n - 1)
                    nc.scalar.activation(by_place(theirs[g.slot(2)], g), by_block(p_got, g), ACT.Copy).then_inc(gotten, 1)

                def exps(g):
                    s = g.slot(2)
                    act.wait_ge(expos, 2 * g.n + 2)
                    wait_from(act, summed, g.n - 1)
                    nc.scalar.activation(grow[s][:, :, 0:g.w], expo[s][:, :, 0:g.w], ACT.Exp).then_inc(grown, 1)
                    wait_from(act, mixes, g.n - 1)
                    nc.scalar.activation(tops[s][:, 0:g.w], top[s][:, 1:1 + g.w], ACT.Identity, scale=for_top[:, 0:1]).then_inc(topped, 1)

                def to_rows(g):
                    s = g.slot(2)
                    wait_from(act, stored[s], 16 * g.turn(2))
                    act.wait_ge(rowed, g.n + 1)
                    nc.scalar.activation(rows[s][0:g.p, :, :, 0:D].rearrange("p h c f -> p c h f"),
                                         p_out[0:g.p, :].rearrange("p (c h f) -> p c h f", h=2, f=D), ACT.Copy).then_inc(drained, 1)
                    act.wait_ge(smalls, g.n + 1)
                    small = p_small[0:g.p, :].rearrange("p (c h a f) -> p c h a f", h=2, a=HEADS, f=HC)
                    for q in range(2):
                        ins = nc.scalar.activation(rows[s][0:g.p, :, :, D + q * HEADS:D + (q + 1) * HEADS].rearrange("p h c f -> p c h f"),
                                                   small[:, :, :, :, q], ACT.Copy)
                    ins.then_inc(drained_small, 1)

                def store(g):
                    s = g.slot(2)
                    act.wait_ge(drained_small, g.n + 1)
                    act.dma_start(both_halves(t3, g.row, g.w), rows[s][0:g.p, :, :, :].rearrange("p h c f -> p h (c f)")).then_inc(stored[s], 16)

                def keep_logits(g):
                    act.wait_ge(scored, g.n + 1)
                    wait_from(act, expos, 2 * g.n - 2)
                    nc.scalar.activation(logit[g.slot(2)][:, 0:g.w], p_logit[:, 0:g.w], ACT.Copy).then_inc(logits, 1)

                each_group(act, (1, their_rows), (0, start_rows), (2, exps), (3, to_rows), (3, store), (1, keep_logits))
                for s in range(2):
                    act.wait_ge(stored[s], 16 * ((NG + 2 - s) // 2))

            @block.vector
            def _(dve):
                nc.vector.memset(WE[:, :], 0.0).then_inc(zeroed, 1)
                dve.wait_ge(weights_in, 64)
                dve.wait_ge(made, 5)
                nc.vector.tensor_scalar(AT[:, :], blocks[2][:, :], AV[:, 0:1], None, ALU.mult).then_inc(zeroed, 1)
                nc.vector.tensor_reduce(for_top[:, :], second[:, :], AX.X, ALU.add).then_inc(zeroed, 1)
                dve.wait_ge(zeroed, 3)
                nc.vector.tensor_scalar(for_den[:, :], for_top[:, :], -1.0, 1.0, ALU.mult, ALU.add).then_inc(zeroed, 1)
                dve.wait_ge(zeroed, 4)

                def maximum(g):
                    s = g.slot(2)
                    wait_from(dve, topped, g.n - 1)
                    if g.zero:
                        nc.vector.memset(top[s][:, 0:1], NEG).then_inc(carried, 1)
                    else:
                        dve.wait_ge(maxed, g.n)
                        nc.vector.tensor_copy(top[s][:, 0:1], top[1 - s][:, W:W + 1]).then_inc(carried, 1)
                    dve.wait_ge(carried, g.n + 1)
                    dve.wait_ge(logits, g.n + 1)
                    dve.wait_ge(resets, g.n + 1)
                    nc.vector.tensor_tensor_scan(top[s][:, 1:1 + g.w], p_reset[:, 0:g.w], logit[s][:, 0:g.w], top[s][:, 0:1], ALU.add, ALU.max).then_inc(maxed, 1)

                def exponents(g):
                    s = g.slot(2)
                    dve.wait_ge(maxed, g.n + 1)
                    wait_from(dve, expos, 2 * g.n - 2)
                    nc.vector.tensor_tensor(left[s][:, 0:g.w], top[s][:, 0:g.w], p_reset[:, 0:g.w], ALU.add).then_inc(lefts, 1)
                    wait_from(dve, grown, g.n - 1)
                    nc.vector.tensor_tensor(expo[s][:, 1, 0:g.w], logit[s][:, 0:g.w], top[s][:, 1:1 + g.w], ALU.subtract).then_inc(expos, 1)
                    dve.wait_ge(lefts, g.n + 1)
                    nc.vector.tensor_tensor(expo[s][:, 0, 0:g.w], left[s][:, 0:g.w], top[s][:, 1:1 + g.w], ALU.subtract).then_inc(expos, 1)

                def spread(g):
                    s = g.slot(2)
                    dve.wait_ge(marked, g.n + 1)
                    dve.wait_ge(started, g.n + 1)
                    wait_from(dve, owned, g.n)
                    wait_from(dve, added, g.n - 1)
                    nc.vector.tensor_tensor_scan(own[s][:, 0:g.w], p_mk[:, 0:g.w], starts[s][:, 0:g.w],
                                                 0.0 if g.zero else own[1 - s][:, W - 1:W], ALU.mult, ALU.add).then_inc(owned, 1)

                def attend(g):
                    s = g.slot(2)
                    dve.wait_ge(owned, g.n + 1)
                    dve.wait_ge(summed_ea, g.n + 1)
                    wait_from(dve, leaked, g.n - 1)
                    nc.vector.tensor_tensor(pre[s][:, 0:g.w], own[s][:, 0:g.w], p_pre[:, 0:g.w], ALU.add).then_inc(added, 1)
                    dve.wait_ge(added, g.n + 1)
                    wait_from(dve, scored, g.n - 1)
                    nc.vector.scalar_tensor_tensor(out=act_in[s][:, 0:g.w], in0=pre[s][:, 0:g.w], scalar=0.2, in1=pre[s][:, 0:g.w],
                                                   op0=ALU.mult, op1=ALU.max).then_inc(leaked, 1)

                def accumulate(g):
                    s = g.slot(2)
                    dve.wait_ge(grown, g.n + 1)
                    wait_from(dve, summed, g.n - 1)
                    nc.vector.tensor_tensor(weighted[s][:, 0:g.w], theirs[s][:, 0:g.w], grow[s][:, 1, 0:g.w], ALU.mult).then_inc(weighted_s, 1)
                    wait_from(dve, dens, g.n)
                    wait_from(dve, mixes, g.n - 1)
                    nc.vector.tensor_tensor_scan(den[s][:, 0:g.w], grow[s][:, 0, 0:g.w], grow[s][:, 1, 0:g.w],
                                                 0.0 if g.zero else den[1 - s][:, W - 1:W], ALU.mult, ALU.add).then_inc(dens, 1)
                    dve.wait_ge(weighted_s, g.n + 1)
                    wait_from(dve, rowed, g.n - 1)
                    wait_from(dve, summed, g.n)
                    nc.vector.tensor_tensor_scan(run[s][:, 0:g.w], grow[s][:, 0, 0:g.w], weighted[s][:, 0:g.w],
                                                 0.0 if g.zero else run[1 - s][:, W - 1:W], ALU.mult, ALU.add).then_inc(summed, 1)
                    dve.wait_ge(dens, g.n + 1)
                    dve.wait_ge(topped, g.n + 1)
                    wait_from(dve, smalls, g.n - 1)
                    nc.vector.scalar_tensor_tensor(out=mixed[s][:, 0:g.w], in0=den[s][:, 0:g.w], scalar=for_den[:, 0:1], in1=tops[s][:, 0:g.w],
                                                   op0=ALU.mult, op1=ALU.add).then_inc(mixes, 1)

                each_group(dve, (2, maximum), (2, exponents), (0, spread), (1, attend), (2, accumulate))


def finish_4(nc, sb, ps, sem, X, info, t3, valid, bias3, g3, be3, out):
    with Stage(nc) as c:
        rows = sb(c, "rows", [P, NJ, T3])
        carry = sb(c, "carry", [P, T3])
        Y, Z = sb(c, "Y", [P, NJ, D]), sb(c, "Z", [P, NJ, D])
        BI, GA, BE = (sb(c, n, [P, D]) for n in ("BI", "GA", "BE"))
        inv = sb(c, "inv", [P, NJ])
        theirs, mx, dif, fac, scaled, denom, rden = (sb(c, n, [P, NJ, HEADS]) for n in ("theirs", "mx", "dif", "fac", "scaled", "denom", "rden"))
        dif2, fac2 = sb(c, "dif2", [P, NJ, HEADS]), sb(c, "fac2", [P, NJ, HEADS])
        part, mean, var, sd, rs = (sb(c, n, [P, D]) for n in ("part", "mean", "var", "sd", "rs"))
        ones = sb(c, "ones", [P, P])
        tot = ps(c, "tot", [P, 2 * D])
        cleared, rows_in, small_in, chain, fed, exped, totals, rooted = (
            sem(c, n) for n in ("cleared", "rows_in", "small_in", "chain", "fed", "exped", "totals", "rooted"))
        with nc.Block() as block:
            @block.sync
            def _(sp):
                sp.dma_start(carry[:, :], t3[H - 1:H, :].to_broadcast((P, T3))).then_inc(small_in, 16)
                for t, w in ((BI, bias3), (GA, g3), (BE, be3)):
                    sp.dma_start(t[:, :], row_of(w)).then_inc(small_in, 16)

            @block.gpsimd
            def _(pool):
                pool.wait_ge(cleared, 1)
                gather_rows(pool, nc, rows, T3, t3, info["last"], rows_in)

            @block.vector
            def _(dve):
                count = [0]

                def link(ins):
                    count[0] += 1
                    ins.then_inc(chain, 1)
                    dve.wait_ge(chain, count[0])

                def heads(t):
                    return t.unsqueeze(1).to_broadcast((P, NJ, HEADS))

                def spread_out(t):
                    return t[:, :, :].unsqueeze(3).to_broadcast((P, NJ, HEADS, HC))

                def split(t):
                    return t.rearrange("p j (a f) -> p j a f", a=HEADS)

                nc.vector.memset(rows[:, :, :], 0.0).then_inc(cleared, 1)
                link(nc.vector.memset(ones[:, :], 1.0))
                dve.wait_ge(rows_in, 16 * NJ)
                dve.wait_ge(small_in, 64)
                span = per_node(info["span"], HEADS)
                cmax = carry[:, D + HEADS:T3]
                link(nc.vector.tensor_scalar(inv[:, :], info["span"][:, :], -1.0, -NEG, ALU.add, ALU.mult))
                link(nc.vector.tensor_tensor(theirs[:, :, :], span, heads(cmax), ALU.mult))
                link(nc.vector.tensor_tensor(theirs[:, :, :], theirs[:, :, :], per_node(inv, HEADS), ALU.add))
                link(nc.vector.tensor_tensor(mx[:, :, :], theirs[:, :, :], rows[:, :, D + HEADS:T3], ALU.max))
                link(nc.vector.tensor_tensor(dif[:, :, :], rows[:, :, D + HEADS:T3], mx[:, :, :], ALU.subtract))
                link(nc.vector.tensor_tensor(dif2[:, :, :], theirs[:, :, :], mx[:, :, :], ALU.subtract))
                nc.vector.tensor_copy(inv[:, 0:1], info["span"][:, 0:1]).then_inc(fed, 1)
                dve.wait_ge(exped, 2)
                link(nc.vector.tensor_tensor(denom[:, :, :], rows[:, :, D:D + HEADS], fac[:, :, :], ALU.mult))
                link(nc.vector.tensor_tensor(scaled[:, :, :], fac2[:, :, :], heads(carry[:, D:D + HEADS]), ALU.mult))
                link(nc.vector.tensor_tensor(denom[:, :, :], denom[:, :, :], scaled[:, :, :], ALU.add))
                link(nc.vector.tensor_scalar(denom[:, :, :], denom[:, :, :], 1e-16, None, ALU.add))
                link(nc.vector.reciprocal(rden[:, :, :], denom[:, :, :]))
                link(nc.vector.tensor_tensor(split(Y[:, :, :]), split(rows[:, :, 0:D]), spread_out(fac), ALU.mult))
                link(nc.vector.tensor_tensor(split(Z[:, :, :]), carry[:, 0:D].unsqueeze(1).to_broadcast((P, NJ, D)).rearrange("p j (a f) -> p j a f", a=HEADS),
                                             spread_out(fac2), ALU.mult))
                link(nc.vector.tensor_tensor(Y[:, :, :], Y[:, :, :], Z[:, :, :], ALU.add))
                link(nc.vector.tensor_tensor(split(Z[:, :, :]), split(Y[:, :, :]), spread_out(rden), ALU.mult))
                link(nc.vector.tensor_tensor(Y[:, :, :], Z[:, :, :], per_feature(BI), ALU.add))

                def total(t, n):
                    link(nc.vector.tensor_reduce(part[:, :], t[:, :, :].rearrange("p j f -> p f j"), AX.X, ALU.add))
                    nc.vector.tensor_copy(inv[:, 1:2], info["span"][:, 1:2]).then_inc(fed, 1)
                    dve.wait_ge(totals, n)

                link(nc.vector.tensor_tensor(Z[:, :, :], Y[:, :, :], per_node(valid), ALU.mult))
                total(Z, 1)
                link(nc.vector.tensor_scalar(mean[:, :], tot[:, 0:D], 1.0 / N, None, ALU.mult))
                link(nc.vector.tensor_tensor(Y[:, :, :], Y[:, :, :], per_feature(mean), ALU.subtract))
                link(nc.vector.tensor_tensor(Z[:, :, :], Y[:, :, :], per_node(valid), ALU.mult))
                link(nc.vector.tensor_tensor(Z[:, :, :], Z[:, :, :], Y[:, :, :], ALU.mult))
                total(Z, 2)
                link(nc.vector.tensor_scalar(var[:, :], tot[:, D:2 * D], 1.0 / N, EPS, ALU.mult, ALU.add))
                nc.vector.tensor_copy(inv[:, 2:3], info["span"][:, 2:3]).then_inc(fed, 1)
                dve.wait_ge(rooted, 1)
                link(nc.vector.reciprocal(rs[:, :], sd[:, :]))
                link(nc.vector.tensor_tensor(rs[:, :], rs[:, :], GA[:, :], ALU.mult))
                link(nc.vector.tensor_tensor(Y[:, :, :], Y[:, :, :], per_feature(rs), ALU.mult))
                link(nc.vector.tensor_tensor(Y[:, :, :], Y[:, :, :], per_feature(BE), ALU.add))
                link(nc.vector.tensor_tensor(Z[:, :, :], Y[:, :, :], X[:, :, :], ALU.add))
                nc.vector.tensor_copy(inv[:, 3:4], info["span"][:, 3:4]).then_inc(fed, 1)
                dve.wait_ge(rooted, 2)
                link(nc.vector.tensor_tensor(Z[:, :, :], Y[:, :, :], X[:, :, :], ALU.add))

            @block.tensor
            def _(pe):
                for n in range(2):
                    pe.wait_ge(fed, 2 + n)
                    nc.tensor.matmul(tot[:, n * D:(n + 1) * D], ones[:, :], part[:, :], start=True, stop=True).then_inc(totals, 1)

            @block.scalar
            def _(act):
                act.wait_ge(fed, 1)
                nc.scalar.activation(fac[:, :, :], dif[:, :, :], ACT.Exp).then_inc(exped, 1)
                nc.scalar.activation(fac2[:, :, :], dif2[:, :, :], ACT.Exp).then_inc(exped, 1)
                act.wait_ge(fed, 4)
                nc.scalar.activation(sd[:, :], var[:, :], ACT.Sqrt).then_inc(rooted, 1)
                act.wait_ge(fed, 5)
                nc.scalar.activation(Y[:, :, :], Z[:, :, :], ACT.Gelu).then_inc(rooted, 1)

        norm(nc, sb, sem, [], Z, Y, [])
        written = sem(c, "written")
        with nc.Block() as block:
            @block.sync
            def _(sp):
                for s, j, rows_out in node_rows(out):
                    sp.dma_start(rows_out, Y[s, 0:j, :]).then_inc(written, 16)
                sp.wait_ge(written, 48)


_INS = {"x": "x", "src": "src", "dst": "dst", "ea16": "edge_attr_16", "ea64": "edge_attr_64", "ew": "edge_weight1",
        "w0a": "L0_gnn_W1", "b0a": "L0_gnn_b1", "w0b": "L0_gnn_W2", "b0b": "L0_gnn_b2",
        "u1": "L1_gnn_u", "w1a": "L1_gnn_W1", "b1a": "L1_gnn_b1", "w1b": "L1_gnn_W2", "b1b": "L1_gnn_b2",
        "g1": "L1_gnn_gamma", "be1": "L1_gnn_beta",
        "w2a": "L2_gnn_W1", "b2a": "L2_gnn_b1", "w2b": "L2_gnn_W2", "b2b": "L2_gnn_b2", "w2g": "L2_gnn_Wg", "b2g": "L2_gnn_bg",
        "wl": "L3_gnn_W_l", "bl": "L3_gnn_b_l", "wr": "L3_gnn_W_r", "br": "L3_gnn_b_r", "we": "L3_gnn_W_e",
        "att": "L3_gnn_att", "bias3": "L3_gnn_bias", "g3": "L3_gnn_gamma", "be3": "L3_gnn_beta"}


def kernel(**inputs):
    import numpy as _np
    import concourse.bacc as _bacc
    from concourse import mybir as _mybir
    from concourse.bass_utils import run_bass_kernel_spmd as _run

    nc = _bacc.Bacc("TRN2", target_bir_lowering=False, num_devices=1)
    arrays, args = {}, {}
    for name, given in _INS.items():
        a = _np.ascontiguousarray(inputs[given])
        if name in ("src", "dst"):
            a = a.reshape(-1, 1)
        arrays[f"in_{name}_dram"] = a
        args[name] = nc.dram_tensor(f"in_{name}_dram", a.shape, _mybir.dt.from_np(a.dtype), kind="ExternalInput").ap()
    args["out"] = nc.dram_tensor("out_0_dram", (N, D), F32, kind="ExternalOutput").ap()
    build(nc, **args)
    r = _run(nc, [arrays], core_ids=[0])
    return r.results[0]["out_0_dram"]
```
